# Optimizing a Trainium2 kernel written in Bass

```python
import numpy as np
import jax
import jax.numpy as jnp

def _softmax(x, axis=-1):
    return jax.nn.softmax(x, axis=axis)

def _gelu(x):
    return jax.nn.gelu(x, approximate=True)

def _silu(x):
    return jax.nn.silu(x)

def _sigmoid(x):
    return jax.nn.sigmoid(x)

def _layernorm(x, axis=-1, eps=1e-05):
    m = jnp.mean(x, axis=axis, keepdims=True)
    v = jnp.var(x, axis=axis, keepdims=True)
    return (x - m) / jnp.sqrt(v + eps)

def _scatter_add(tgt, idx, src, axis=0):
    return tgt.at[idx].add(src)

def _segment_sum(src, seg, n):
    return jax.ops.segment_sum(src, seg, n)
kernel_name = 'mk_gnn_ffn_d1_gnn_r16_0cce89'

def setup_inputs(seed: int=0):
    np.random.seed(seed)
    _w = jnp.asarray

    def _rec_inputs():
        import jax
        import jax.numpy as jnp
        _gk = jax.random.key(seed)
        x = -0.0003713 + 1 * jax.random.normal(jax.random.fold_in(_gk, 1), (3125, 256), jnp.float32)
        _s = jax.random.randint(jax.random.fold_in(_gk, 2), (50000,), 0, 3125, jnp.int32)
        _d = jax.random.randint(jax.random.fold_in(_gk, 3), (50000,), 0, 3125, jnp.int32)
        _loop = jnp.arange(3125, dtype=jnp.int32)
        src = jnp.concatenate([_s, _d, _loop])
        dst = jnp.concatenate([_d, _s, _loop])
        _o = jnp.argsort(dst, stable=True)
        src = src[_o]
        dst = dst[_o]
        edge_weight1 = jax.random.uniform(jax.random.fold_in(_gk, 12), (103125, 1), jnp.float32, 0.0, 0.999998)
        return (x, src, dst, edge_weight1)
    x, src, dst, edge_weight1 = _rec_inputs()

    def _L0_gnn_setup():
        import jax, jax.numpy as jnp
        import numpy as np
        N_NODES = 3125
        DIM_H = 256
        N_EDGES = 50000
        LN_EPS = 1e-05

        def _layer_norm(x, g, b):
            mu = jnp.mean(x, axis=-1, keepdims=True)
            var = jnp.mean(jnp.square(x - mu), axis=-1, keepdims=True)
            return (x - mu) * jax.lax.rsqrt(var + LN_EPS) * g + b
        key = jax.random.key(seed)
        ks = jax.random.split(key, 12)
        d = DIM_H

        def lin(k, fan_in, fan_out):
            lim = 1.0 / np.sqrt(fan_in)
            kw, kb = jax.random.split(k)
            W = jax.random.uniform(kw, (fan_in, fan_out), jnp.float32, -lim, lim)
            b = jax.random.uniform(kb, (fan_out,), jnp.float32, -lim, lim)
            return (W, b)
        h = jax.random.normal(ks[0], (N_NODES, d), jnp.float32)
        e = jax.random.randint(ks[1], (2, N_EDGES), 0, N_NODES, jnp.int64)
        d2 = jax.random.uniform(ks[2], (N_EDGES, 1), jnp.float32)
        mW1, mb1 = lin(ks[3], 2 * d + 1, d)
        mW2, mb2 = lin(ks[4], d, d)
        ln_g = jnp.ones((d,), jnp.float32)
        ln_b = jnp.zeros((d,), jnp.float32)
        uW1, ub1 = lin(ks[5], 2 * d, d)
        uW2, ub2 = lin(ks[6], d, d)
        return {'h': h, 'e': e, 'd2': d2, 'mW1': mW1, 'mb1': mb1, 'ln_g': ln_g, 'ln_b': ln_b, 'mW2': mW2, 'mb2': mb2, 'uW1': uW1, 'ub1': ub1, 'uW2': uW2, 'ub2': ub2}
    _L0_gnn_all = _L0_gnn_setup()
    _L0_gnn_in = {k: v for k, v in _L0_gnn_all.items() if k in ('mW1', 'mb1', 'ln_g', 'ln_b', 'mW2', 'mb2', 'uW1', 'ub1', 'uW2', 'ub2')}
    del _L0_gnn_all

    def _L0_ffn_setup():
        import jax, jax.numpy as jnp
        import numpy as np
        B, S, D = (8, 256, 256)
        H = 4 * D
        CAPACITY = 0.5
        key = jax.random.key(seed)
        ks = jax.random.split(key, 6)
        x = jax.random.normal(ks[0], (B, S, D), dtype=jnp.float32)
        attention_mask = jnp.zeros((B, 1, 1, S), dtype=jnp.float32)
        wr = jax.random.normal(ks[1], (D, 1), dtype=jnp.float32) * 0.02
        br = jnp.zeros((1,), dtype=jnp.float32)
        w1 = jax.random.normal(ks[2], (D, H), dtype=jnp.float32) * 0.02
        b1 = jnp.zeros((H,), dtype=jnp.float32)
        w2 = jax.random.normal(ks[3], (H, D), dtype=jnp.float32) * 0.02
        b2 = jnp.zeros((D,), dtype=jnp.float32)
        return {'x': x, 'attention_mask': attention_mask, 'wr': wr, 'br': br, 'w1': w1, 'b1': b1, 'w2': w2, 'b2': b2}
    _L0_ffn_all = _L0_ffn_setup()
    _L0_ffn_in = {k: v for k, v in _L0_ffn_all.items() if k in ('attention_mask', 'wr', 'br', 'w1', 'b1', 'w2', 'b2')}
    del _L0_ffn_all
    return {'x': x, 'src': src, 'dst': dst, 'edge_weight1': edge_weight1, 'L0_gnn_mW1': _L0_gnn_in['mW1'], 'L0_gnn_mb1': _L0_gnn_in['mb1'], 'L0_gnn_ln_g': _L0_gnn_in['ln_g'], 'L0_gnn_ln_b': _L0_gnn_in['ln_b'], 'L0_gnn_mW2': _L0_gnn_in['mW2'], 'L0_gnn_mb2': _L0_gnn_in['mb2'], 'L0_gnn_uW1': _L0_gnn_in['uW1'], 'L0_gnn_ub1': _L0_gnn_in['ub1'], 'L0_gnn_uW2': _L0_gnn_in['uW2'], 'L0_gnn_ub2': _L0_gnn_in['ub2'], 'L0_ffn_attention_mask': _L0_ffn_in['attention_mask'], 'L0_ffn_wr': _L0_ffn_in['wr'], 'L0_ffn_br': _L0_ffn_in['br'], 'L0_ffn_w1': _L0_ffn_in['w1'], 'L0_ffn_b1': _L0_ffn_in['b1'], 'L0_ffn_w2': _L0_ffn_in['w2'], 'L0_ffn_b2': _L0_ffn_in['b2']}

def reference(x, src, dst, edge_weight1, L0_gnn_mW1, L0_gnn_mb1, L0_gnn_ln_g, L0_gnn_ln_b, L0_gnn_mW2, L0_gnn_mb2, L0_gnn_uW1, L0_gnn_ub1, L0_gnn_uW2, L0_gnn_ub2, L0_ffn_attention_mask, L0_ffn_wr, L0_ffn_br, L0_ffn_w1, L0_ffn_b1, L0_ffn_w2, L0_ffn_b2):
    import jax
    import jax.numpy as jnp

    def _L0_gnn_ref(h, e, d2, mW1, mb1, ln_g, ln_b, mW2, mb2, uW1, ub1, uW2, ub2):
        import jax, jax.numpy as jnp
        import numpy as np
        N_NODES = 3125
        DIM_H = 256
        N_EDGES = 50000
        LN_EPS = 1e-05

        def _layer_norm(x, g, b):
            mu = jnp.mean(x, axis=-1, keepdims=True)
            var = jnp.mean(jnp.square(x - mu), axis=-1, keepdims=True)
            return (x - mu) * jax.lax.rsqrt(var + LN_EPS) * g + b
        ei, ej = (e[0], e[1])
        hi = h[ei]
        hj = h[ej]
        x = jnp.concatenate((hi, hj, d2), axis=-1)
        msg = jax.nn.silu(x @ mW1 + mb1)
        msg = _layer_norm(msg, ln_g, ln_b)
        msg = jax.nn.silu(msg @ mW2 + mb2)
        agg = jax.ops.segment_sum(msg, ei, num_segments=h.shape[0])
        y = jnp.concatenate((h, agg), axis=-1)
        y = jax.nn.silu(y @ uW1 + ub1) @ uW2 + ub2
        return h + y

    def _L0_ffn_ref(x, attention_mask, wr, br, w1, b1, w2, b2):
        import jax, jax.numpy as jnp
        import numpy as np
        B, S, D = (8, 256, 256)
        H = 4 * D
        CAPACITY = 0.5
        b, s, d = x.shape
        weights = (jnp.einsum('bsd,do->bso', x, wr) + br)[..., 0]
        k = max(1, int(CAPACITY * s))
        kk = k - 1 if k > 1 else 1
        _, idx = jax.lax.top_k(weights, k)
        sel_idx = idx[:, :kk]
        sel = jnp.take_along_axis(x, sel_idx[:, :, None], axis=1)
        h = jax.nn.gelu(jnp.einsum('bkd,dh->bkh', sel, w1) + b1)
        y = jnp.einsum('bkh,hd->bkd', h, w2) + b2
        w_sel = jnp.take_along_axis(weights, sel_idx, axis=1)
        y = y * w_sel[..., None]
        batch_idx = jnp.arange(b)[:, None]
        processed = jnp.zeros_like(x).at[batch_idx, sel_idx].set(y)
        return processed + x
    edge_index = jnp.stack([src, dst])
    x = x + _L0_gnn_ref(_layernorm(x, axis=-1), edge_index, edge_weight1, L0_gnn_mW1, L0_gnn_mb1, L0_gnn_ln_g, L0_gnn_ln_b, L0_gnn_mW2, L0_gnn_mb2, L0_gnn_uW1, L0_gnn_ub1, L0_gnn_uW2, L0_gnn_ub2)
    x = x + _L0_ffn_ref(_layernorm(x, axis=-1)[None], L0_ffn_attention_mask, L0_ffn_wr, L0_ffn_br, L0_ffn_w1, L0_ffn_b1, L0_ffn_w2, L0_ffn_b2)[0]
    return x

_drawn_inputs = setup_inputs


def setup_inputs(seed=0):
    import zlib

    import numpy as np

    out = dict(_drawn_inputs(seed))
    spreads = {'L0_gnn_ln_g': (1.0, 0.2),
     'L0_gnn_ln_b': (0.0, 0.1),
     'L0_ffn_b1': (0.0, 0.8),
     'L0_ffn_b2': (0.0, 0.757)}
    factors = {'edge_weight1': 8.0,
     'L0_gnn_ub1': 8.0,
     'L0_gnn_ub2': 3.758,
     'L0_ffn_wr': 4.953,
     'L0_ffn_w1': 4.786,
     'L0_ffn_w2': 4.378}
    for name, (base, spread) in spreads.items():
        noise = np.random.default_rng([zlib.crc32(name.encode()), seed]).standard_normal(out[name].shape)
        drawn = base * np.exp(spread * noise) if base else spread * noise
        out[name] = jnp.asarray(drawn.astype(out[name].dtype))
    for name, factor in factors.items():
        out[name] = (out[name] * factor).astype(out[name].dtype)
    return out
```

```python
from contextlib import ExitStack

import concourse.bass as bass
from concourse import mybir

F32 = mybir.dt.float32
BF16 = mybir.dt.bfloat16
I32 = mybir.dt.int32
ALU = mybir.AluOpType
ACT = mybir.ActivationFunctionType
AX_X = mybir.AxisListType.X

P = 128
NODES, D = 3125, 256
EDGES = 103125
NB = 125
BLOCKS = NODES // NB
EP = 125
EC = EDGES // EP
CHUNKS = 5
CC = EC // CHUNKS
GROUP = 6
RI = -(-CC // GROUP)
CP = RI * GROUP
GI = 31
TC = GI * GROUP
TILES = CHUNKS * TC
PAIRS = TILES // 2
GROUPS = CHUNKS * GI
PG = GROUP // 2
NPART = 6
DRAIN = 4
H = 1024
HC = H // P
TOPK = int(0.5 * NODES) - 1
LN_EPS = 1e-5
MAGIC = 12582912.0
assert NODES == NB * BLOCKS and EDGES == EP * EC and EC == CHUNKS * CC
assert TC >= (EP * CC + BLOCKS * (P - 1)) // P and TC % 2 == 0


def build(nc, io):
    x, src, dst, ew = io["x"], io["src"], io["dst"], io["edge_weight1"]
    mW1, mb1, ln_g, ln_b = io["L0_gnn_mW1"], io["L0_gnn_mb1"], io["L0_gnn_ln_g"], io["L0_gnn_ln_b"]
    mW2, mb2 = io["L0_gnn_mW2"], io["L0_gnn_mb2"]
    uW1, ub1, uW2, ub2 = io["L0_gnn_uW1"], io["L0_gnn_ub1"], io["L0_gnn_uW2"], io["L0_gnn_ub2"]
    wr, br, w1, b1 = io["L0_ffn_wr"], io["L0_ffn_br"], io["L0_ffn_w1"], io["L0_ffn_b1"]
    w2, b2, out = io["L0_ffn_w2"], io["L0_ffn_b2"], io["out"]

    b_table = nc.dram_tensor("b_table", (NODES, D), F32, kind="Internal").ap()
    tile_block_d = nc.dram_tensor("tile_block_d", (CHUNKS, TC), I32, kind="Internal").ap()
    w_row_d = nc.dram_tensor("w_row_d", (1, 3 * D), BF16, kind="Internal").ap()
    c_row_d = nc.dram_tensor("c_row_d", (1, 3 * D), BF16, kind="Internal").ap()
    score_d = nc.dram_tensor("score_d", (BLOCKS, NB), F32, kind="Internal").ap()

    x_v = x.rearrange("(b p) d -> p b d", p=NB)
    out_v = out.rearrange("(b p) d -> p b d", p=NB)

    with ExitStack() as whole:
        def alloc(stack, name, shape, dt):
            return stack.enter_context(nc.sbuf_tensor(name, shape, dt))

        def semaphore(stack, name):
            return stack.enter_context(nc.semaphore(name))

        h_sb = alloc(whole, "h_sb", [NB, BLOCKS, D], F32)
        identf = alloc(whole, "identf", [P, P], F32)
        exph = alloc(whole, "exph", [P, BLOCKS], F32)

        agg = alloc(whole, "agg", [NB, BLOCKS, D], F32)
        s_late = semaphore(whole, "s_late")

        edge_mem = ExitStack()
        a_sb = alloc(edge_mem, "a_sb", [P, BLOCKS, 3, D], BF16)
        w2g = alloc(edge_mem, "w2g", [P, 2, D], F32)
        c_rows = alloc(edge_mem, "c_rows", [3, D], BF16)
        ones3 = alloc(edge_mem, "ones3", [3, P], BF16)
        identb = alloc(edge_mem, "identb", [P, P], BF16)
        iota_n = alloc(edge_mem, "iota_n", [P, P], BF16)
        iota_q = alloc(edge_mem, "iota_q", [P, TC], BF16)
        iota_f = alloc(edge_mem, "iota_f", [P, P], F32)
        q_col = alloc(edge_mem, "q_col", [P, CHUNKS, CP], F32)
        r_col = alloc(edge_mem, "r_col", [P, CHUNKS, CP], F32)
        vals = alloc(edge_mem, "vals", [P, NPART, CHUNKS, CP], F32)
        tile_block = alloc(edge_mem, "tile_block", [1, TILES], I32)

        with ExitStack() as ctx:
            def sb(name, shape, dt):
                return alloc(ctx, name, shape, dt)

            def sem(name):
                return semaphore(ctx, name)

            src_i = sb("src_i", [EP, EC], I32)
            dst_i = sb("dst_i", [EP, EC], I32)
            part_i = sb("part_i", [EP, EC], I32)
            ew_f = sb("ew_f", [EP, EC], F32)
            f1 = sb("f1", [EP, EC], F32)
            f2 = sb("f2", [EP, EC], F32)
            blk = sb("blk", [EP, EC], BF16)
            partb = sb("partb", [EP, EC], BF16)
            eq = sb("eq", [EP, BLOCKS, CC], BF16)
            cum = sb("cum", [EP, BLOCKS, CC], F32)
            pos = sb("pos", [EP, CC], F32)
            zero = sb("zero", [P, 1], F32)
            cnt = sb("cnt", [EP, BLOCKS], BF16)
            sm = sb("sm", [P, 12, BLOCKS], F32)
            tb_f = sb("tb_f", [P, 2], F32)
            tb_i = sb("tb_i", [P, 2 * CHUNKS], I32)
            tid = sb("tid", [P, 2], F32)
            tri = sb("tri", [P, P], BF16)
            onesb = sb("onesb", [P, P], BF16)
            stats = sb("stats", [NB, BLOCKS, 6], F32)
            mv = sb("mv", [NB, BLOCKS, 2], F32)
            rstd = sb("rstd", [NB, BLOCKS], F32)
            hT = sb("hT", [P, 2, 2, P], F32)
            wij = sb("wij", [P, 2, 2 * D], F32)
            mb1_b = sb("mb1_b", [P, D], F32)
            res = sb("res", [NB, 3, D], F32)
            b_out = sb("b_out", [NB, 2, D], F32)
            w2raw = sb("w2raw", [P, 2, D], F32)
            gcol = sb("gcol", [P, 2], F32)
            bcol = sb("bcol", [P, 2], F32)
            rowf = sb("rowf", [1, 4, D], F32)
            rowb = sb("rowb", [1, 2, 3, D], BF16)
            psX = ctx.enter_context(nc.psum_tensor("psX", [P, 2, 512], F32))
            psAB = ctx.enter_context(nc.psum_tensor("psAB", [P, 2, 512], F32))
            psC = ctx.enter_context(nc.psum_tensor("psC", [P, 512], F32))
            psK = ctx.enter_context(nc.psum_tensor("psK", [P, 512], F32))

            s_x = sem("s_x")
            s_edges = sem("s_edges")
            s_weights = sem("s_weights")
            s_pool = sem("s_pool")
            s_dve = sem("s_dve")
            s_mv1 = sem("s_mv1")
            s_rstd1 = sem("s_rstd1")
            s_h = sem("s_h")
            s_hx = sem("s_hx")
            s_hT = sem("s_hT")
            s_ab = sem("s_ab")
            s_abf = sem("s_abf")
            s_bst = [sem("s_bst0"), sem("s_bst1")]
            s_bo = sem("s_bo")
            s_w2g = sem("s_w2g")
            s_c = sem("s_c")
            s_row = sem("s_row")
            s_mv_rows = sem("s_mv_rows")
            s_rows_in = sem("s_rows_in")
            s_cnt = sem("s_cnt")
            s_cntm = sem("s_cntm")
            s_cntu = sem("s_cntu")
            s_tb = sem("s_tb")
            s_tbd = sem("s_tbd")
            s_tbl = sem("s_tbl")

            block = ctx.enter_context(nc.Block())

            @block.sync
            def _(sp):
                sp.dma_start(src_i[:, :], src.rearrange("(p t) -> p t", p=EP)).then_inc(s_edges, 16)
                sp.dma_start(h_sb[:, :, :], x_v).then_inc(s_x, 16)
                sp.dma_start(wij[:, :, 0:D], mW1[0:D, :].rearrange("(k p) n -> p k n", p=P)).then_inc(s_weights, 16)
                sp.dma_start(wij[:, :, D:2 * D], mW1[D:2 * D, :].rearrange("(k p) n -> p k n", p=P)).then_inc(s_weights, 16)
                sp.dma_start(mb1_b[:, :], mb1.rearrange("(a n) -> a n", a=1).broadcast_to([P, D])).then_inc(s_weights, 16)
                sp.dma_start(w2raw[:, :, :], mW2.rearrange("(k p) n -> p k n", p=P)).then_inc(s_weights, 16)
                sp.dma_start(gcol[:, :], ln_g.rearrange("(k p) -> p k", p=P), allow_slow_non_contiguous=True).then_inc(s_weights, 16)
                sp.dma_start(bcol[:, :], ln_b.rearrange("(k p) -> p k", p=P), allow_slow_non_contiguous=True).then_inc(s_weights, 16)
                sp.dma_start(rowf[0:1, 0, :], mW1[2 * D:2 * D + 1, :]).then_inc(s_weights, 16)
                sp.dma_start(rowf[0:1, 1, :], mb2.rearrange("(a n) -> a n", a=1)).then_inc(s_weights, 16)
                for b in range(BLOCKS):
                    sp.wait_ge(s_bo, b + 1)
                    sp.dma_start(b_table[b * NB:(b + 1) * NB, :], b_out[:, b % 2, :]).then_inc(s_bst[b % 2], 16)
                sp.wait_ge(s_bst[0], 16 * 13)
                sp.wait_ge(s_bst[1], 16 * 12)

            @block.scalar
            def _(act):
                act.dma_start(dst_i[:, :], dst.rearrange("(p t) -> p t", p=EP)).then_inc(s_edges, 16)
                act.dma_start(ew_f[:, :], ew.rearrange("(p t) a -> p (t a)", p=EP)).then_inc(s_edges, 16)
                for b in range(BLOCKS):
                    act.wait_ge(s_hx, b + 1)
                    if b >= 2:
                        act.wait_ge(s_ab, b - 1)
                    nc.scalar.activation(hT[:, b % 2, :, 0:NB], psX[:, b % 2, 0:2 * P].rearrange(
                        "p (k n) -> p k n", k=2)[:, :, 0:NB], ACT.Copy).then_inc(s_hT, 1)
                act.wait_ge(s_row, 2)
                act.dma_start(w_row_d, rowb[0:1, 0, :, :].rearrange("a k n -> a (k n)")).then_inc(s_mv_rows, 16)
                act.dma_start(c_row_d, rowb[0:1, 1, :, :].rearrange("a k n -> a (k n)")).then_inc(s_mv_rows, 16)
                act.wait_ge(s_mv_rows, 32)
                for k in range(3):
                    act.dma_start(a_sb[NB + k:NB + k + 1, :, :, :].rearrange("p b k n -> p b (k n)"),
                                  w_row_d.unsqueeze(1).broadcast_to([1, BLOCKS, 3 * D])).then_inc(s_rows_in, 16)
                act.dma_start(c_rows[:, :], c_row_d.rearrange("a (k n) -> (a k) n", k=3)).then_inc(s_rows_in, 16)
                act.wait_ge(s_tb, CHUNKS)
                for c in range(CHUNKS):
                    act.dma_start(tile_block_d[c, 0:P].rearrange("(p a) -> p a", a=1),
                                  tb_i[:, 2 * c:2 * c + 1]).then_inc(s_tbd, 16)
                    act.dma_start(tile_block_d[c, P:TC].rearrange("(p a) -> p a", a=1),
                                  tb_i[0:TC - P, 2 * c + 1:2 * c + 2]).then_inc(s_tbd, 16)
                act.wait_ge(s_tbd, 32 * CHUNKS)
                act.dma_start(tile_block[:, :], tile_block_d.rearrange("(a c) t -> a (c t)", a=1)).then_inc(s_tbl, 16)
                act.wait_ge(s_tbl, 16)
                act.wait_ge(s_rows_in, 64)

            @block.gpsimd
            def _(pool):
                pool.memset(exph[:, :], -0.5).then_inc(s_pool, 1)
                pool.memset(identf[:, :], 0.0).then_inc(s_pool, 1)
                pool.wait_ge(s_pool, 2)
                pool.affine_select(out=identf[:, :], in_=identf[:, :], compare_op=ALU.not_equal, fill=1.0, base=0,
                                   pattern=[[-1, P]], channel_multiplier=1).then_inc(s_pool, 1)
                pool.iota(iota_f[:, :], pattern=[[1, P]], base=0, channel_multiplier=0,
                          allow_small_or_imprecise_dtypes=True).then_inc(s_pool, 1)
                pool.iota(iota_n[:, :], pattern=[[1, P]], base=0, channel_multiplier=0,
                          allow_small_or_imprecise_dtypes=True).then_inc(s_pool, 1)
                pool.iota(iota_q[:, :], pattern=[[1, TC]], base=0, channel_multiplier=0,
                          allow_small_or_imprecise_dtypes=True).then_inc(s_pool, 1)
                pool.iota(tid[:, :], pattern=[[P, 2]], base=0, channel_multiplier=1,
                          allow_small_or_imprecise_dtypes=True).then_inc(s_pool, 1)
                pool.memset(onesb[:, :], 1.0).then_inc(s_pool, 1)
                pool.wait_ge(s_pool, 8)
                pool.affine_select(out=tri[:, :], in_=onesb[:, :], compare_op=ALU.is_gt, fill=0.0, base=0,
                                   pattern=[[1, P]], channel_multiplier=-1).then_inc(s_pool, 1)
                pool.tensor_copy(identb[:, :], identf[:, :]).then_inc(s_pool, 1)
                pool.memset(ones3[:, :], 1.0).then_inc(s_pool, 1)
                pool.memset(zero[:, :], 0.0).then_inc(s_pool, 1)
                pool.wait_ge(s_mv1, 1)
                pool.tensor_scalar(rstd[:, :], mv[:, :, 1], LN_EPS, None, ALU.add).then_inc(s_pool, 1)
                pool.wait_ge(s_pool, 13)
                pool.tensor_tensor(rstd[:, :], rstd[:, :], exph[0:NB, :], ALU.pow).then_inc(s_rstd1, 1)
                pool.memset(q_col[:, :, :], 0.0).then_inc(s_pool, 1)
                pool.memset(r_col[:, :, :], 0.0).then_inc(s_pool, 1)
                pool.memset(vals[:, :, :, :], 0.0).then_inc(s_pool, 1)

            @block.tensor
            def _(pe):
                pe.wait_ge(s_pool, 3)
                pe.wait_ge(s_weights, 16 * 8)
                for b in range(BLOCKS + 1):
                    if b < BLOCKS:
                        pe.wait_ge(s_h, b + 1)
                        if b >= 2:
                            pe.wait_ge(s_hT, b - 1)
                        for k in range(2):
                            mm = pe.transpose(psX[:, b % 2, k * P:k * P + NB], h_sb[:, b, k * P:(k + 1) * P],
                                              identf[0:NB, 0:NB])
                        mm.then_inc(s_hx, 1)
                    if b >= 1:
                        a = b - 1
                        pe.wait_ge(s_hT, a + 1)
                        if a >= 2:
                            pe.wait_ge(s_abf, a - 1)
                        for k in range(2):
                            mm = pe.matmul(psAB[0:NB, a % 2, :], hT[:, a % 2, k, 0:NB], wij[:, k, :],
                                           start=(k == 0), stop=(k == 1))
                        mm.then_inc(s_ab, 1)
                for k in range(2):
                    mm = pe.matmul(psC[0:1, 0:D], bcol[:, k:k + 1], w2raw[:, k, :], start=(k == 0), stop=(k == 1))
                mm.then_inc(s_c, 1)
                pe.wait_ge(s_pool, 9)
                for c in range(CHUNKS):
                    pe.wait_ge(s_cnt, c + 1)
                    if c:
                        pe.wait_ge(s_cntu, c)
                    pe.matmul(psK[0:EP, 0:BLOCKS], tri[0:EP, 0:EP], cnt[:, :], start=True, stop=True)
                    pe.matmul(psK[:, 64:64 + BLOCKS], onesb[0:EP, :], cnt[:, :], start=True, stop=True).then_inc(s_cntm, 1)

            @block.vector
            def _(dve):
                links = [0]

                def link(ins):
                    links[0] += 1
                    ins.then_inc(s_dve, 1)
                    dve.wait_ge(s_dve, links[0])

                V = nc.vector
                dve.wait_ge(s_x, 16)
                for b in range(BLOCKS):
                    ins = V.bn_stats(stats[:, b, :], h_sb[:, b, :])
                link(ins)
                for b in range(BLOCKS):
                    ins = V.bn_aggr(mv[:, b, :], stats[:, b, :])
                ins.then_inc(s_mv1, 1)

                def split_row(n, source):
                    link(V.tensor_copy(rowb[0:1, n, 0, :], source))
                    link(V.tensor_tensor(rowf[0:1, 2, :], source, rowb[0:1, n, 0, :], ALU.subtract))
                    link(V.tensor_copy(rowb[0:1, n, 1, :], rowf[0:1, 2, :]))
                    link(V.tensor_tensor(rowf[0:1, 3, :], rowf[0:1, 2, :], rowb[0:1, n, 1, :], ALU.subtract))
                    V.tensor_copy(rowb[0:1, n, 2, :], rowf[0:1, 3, :]).then_inc(s_row, 1)

                dve.wait_ge(s_weights, 16 * 8)
                split_row(0, rowf[0:1, 0, :])
                for k in range(2):
                    V.tensor_scalar(w2g[:, k, :], w2raw[:, k, :], gcol[:, k:k + 1], None, ALU.mult).then_inc(s_w2g, 1)
                dve.wait_ge(s_rstd1, 1)
                for b in range(BLOCKS):
                    V.tensor_scalar(h_sb[:, b, :], h_sb[:, b, :], mv[:, b, 0:1], rstd[:, b:b + 1],
                                    ALU.subtract, ALU.mult).then_inc(s_h, 1)

                def tables(b):
                    dve.wait_ge(s_ab, b + 1)
                    if b >= 2:
                        dve.wait_ge(s_bst[b % 2], 16 * (b // 2))
                    V.tensor_copy(b_out[:, b % 2, :], psAB[0:NB, b % 2, D:2 * D]).then_inc(s_bo, 1)
                    link(V.tensor_tensor(res[:, 0, :], psAB[0:NB, b % 2, 0:D], mb1_b[0:NB, :], ALU.add))
                    link(V.tensor_copy(a_sb[0:NB, b, 0, :], res[:, 0, :]))
                    link(V.tensor_tensor(res[:, 1, :], res[:, 0, :], a_sb[0:NB, b, 0, :], ALU.subtract))
                    link(V.tensor_copy(a_sb[0:NB, b, 1, :], res[:, 1, :]))
                    link(V.tensor_tensor(res[:, 2, :], res[:, 1, :], a_sb[0:NB, b, 1, :], ALU.subtract))
                    ins = V.tensor_copy(a_sb[0:NB, b, 2, :], res[:, 2, :])
                    ins.then_inc(s_abf, 1)
                    dve.wait_ge(s_abf, b + 1)

                for b in range(BLOCKS):
                    tables(b)

                dve.wait_ge(s_c, 1)
                link(V.tensor_tensor(rowf[0:1, 1, :], psC[0:1, 0:D], rowf[0:1, 1, :], ALU.add))
                dve.wait_ge(s_row, 1)
                split_row(1, rowf[0:1, 1, :])

                def chunked(ap):
                    return ap.rearrange("p (c t) -> p c t", c=CHUNKS)

                def put(n, source):
                    V.tensor_copy(vals[0:EP, n, :, 0:CC], chunked(source))

                dve.wait_ge(s_edges, 48)
                dve.wait_ge(s_pool, 16)
                link(V.tensor_copy(f1[:, :], src_i[:, :]))
                link(V.tensor_scalar(f2[:, :], f1[:, :], 1.0 / NB, -(NB // 2) / NB, ALU.mult, ALU.add))
                link(V.tensor_scalar(f2[:, :], f2[:, :], MAGIC, None, ALU.add))
                link(V.tensor_scalar(f2[:, :], f2[:, :], -MAGIC, None, ALU.add))
                link(V.tensor_copy(blk[:, :], f2[:, :]))
                link(V.scalar_tensor_tensor(out=f1[:, :], in0=f2[:, :], scalar=-float(NB), in1=f1[:, :],
                                            op0=ALU.mult, op1=ALU.add))
                link(V.tensor_scalar(vals[0:EP, 0, :, 0:CC], chunked(f1[:, :]), 1.0, None, ALU.add))
                link(V.tensor_single_scalar(part_i[:, :], dst_i[:, :], 5, ALU.logical_shift_right))
                link(V.tensor_copy(vals[0:EP, 1, :, 0:CC], chunked(part_i[:, :])))
                link(V.tensor_single_scalar(part_i[:, :], dst_i[:, :], 31, ALU.bitwise_and))
                link(V.tensor_copy(vals[0:EP, 2, :, 0:CC], chunked(part_i[:, :])))
                rest = ew_f[:, :]
                for n, room in ((3, f1), (4, f2), (5, None)):
                    link(V.tensor_copy(partb[:, :], rest))
                    link(V.tensor_copy(vals[0:EP, n, :, 0:CC], chunked(partb[:, :])))
                    if room is not None:
                        link(V.tensor_tensor(room[:, :], rest, partb[:, :], ALU.subtract))
                        rest = room[:, :]

                for c in range(CHUNKS):
                    cols = slice(c * CC, (c + 1) * CC)
                    for b in range(BLOCKS):
                        ins = V.tensor_scalar(eq[:, b, :], blk[:, cols], float(b), None, ALU.is_equal)
                    link(ins)
                    flat = eq[:, :, :].rearrange("p b t -> p (b t)")
                    link(V.tensor_tensor_scan(cum[:, :, :].rearrange("p b t -> p (b t)"), flat, flat, 0.0,
                                              ALU.add, ALU.bypass))
                    link(V.memset(sm[0:EP, 0, 0:1], 0.0))
                    link(V.tensor_copy(sm[0:EP, 0, 1:BLOCKS], cum[:, 0:BLOCKS - 1, CC - 1]))
                    link(V.tensor_tensor(sm[0:EP, 1, :], cum[:, :, CC - 1], sm[0:EP, 0, :], ALU.subtract))
                    ins = V.tensor_copy(cnt[:, :], sm[0:EP, 1, :])
                    ins.then_inc(s_cnt, 1)
                    dve.wait_ge(s_cntm, c + 1)
                    link(V.tensor_scalar(sm[:, 2, :], psK[:, 64:64 + BLOCKS], 1.0 / P, (P - 1.0) / P - 0.498,
                                         ALU.mult, ALU.add))
                    link(V.tensor_scalar(sm[:, 2, :], sm[:, 2, :], MAGIC, None, ALU.add))
                    link(V.tensor_scalar(sm[:, 2, :], sm[:, 2, :], -MAGIC, None, ALU.add))
                    link(V.tensor_tensor_scan(sm[:, 3, :], sm[:, 2, :], sm[:, 2, :], 0.0, ALU.add, ALU.bypass))
                    link(V.tensor_tensor(sm[:, 4, :], sm[:, 3, :], sm[:, 2, :], ALU.subtract))
                    link(V.scalar_tensor_tensor(out=sm[0:EP, 5, :], in0=sm[0:EP, 4, :], scalar=float(P),
                                                in1=psK[0:EP, 0:BLOCKS], op0=ALU.mult, op1=ALU.add))
                    ins = V.scalar_tensor_tensor(out=sm[0:EP, 6, :], in0=sm[0:EP, 5, :], scalar=-1.0,
                                                 in1=sm[0:EP, 0, :], op0=ALU.add, op1=ALU.subtract)
                    ins.then_inc(s_cntu, 1)
                    dve.wait_ge(s_cntu, c + 1)
                    for b in range(BLOCKS):
                        ins = V.scalar_tensor_tensor(out=cum[:, b, :], in0=cum[:, b, :], scalar=sm[0:EP, 6, b:b + 1],
                                                     in1=eq[:, b, :], op0=ALU.add, op1=ALU.mult)
                    link(ins)
                    link(V.tensor_reduce(pos[:, :], cum[:, :, :].rearrange("p b t -> p t b"), AX_X, ALU.add))
                    q = q_col[0:EP, c, 0:CC]
                    link(V.tensor_scalar(q, pos[:, :], 1.0 / P, -0.498, ALU.mult, ALU.add))
                    link(V.tensor_scalar(q, q, MAGIC, None, ALU.add))
                    link(V.tensor_scalar(q, q, -MAGIC, None, ALU.add))
                    link(V.scalar_tensor_tensor(out=r_col[0:EP, c, 0:CC], in0=q, scalar=-float(P), in1=pos[:, :],
                                                op0=ALU.mult, op1=ALU.add))
                    for n in range(2):
                        link(V.tensor_scalar(sm[:, 7, :], sm[:, 3, :], tid[:, n:n + 1], None, ALU.is_le))
                        link(V.tensor_reduce(tb_f[:, n:n + 1], sm[:, 7, :], AX_X, ALU.add))
                    V.tensor_scalar(tb_i[:, 2 * c:2 * c + 2], tb_f[:, :], BLOCKS - 1.0, None, ALU.min).then_inc(s_tb, 1)
                    dve.wait_ge(s_tb, c + 1)

        with ExitStack() as ctx:
            def sb(name, shape, dt):
                return alloc(ctx, name, shape, dt)

            def sem(name):
                return semaphore(ctx, name)

            loc = sb("loc", [P, TILES], F32)
            idx = sb("idx", [P, TILES], I32)
            idx_pair = sb("idx_pair", [P, PG, 2], I32)
            loc_pair = sb("loc_pair", [P, PG, 2], F32)
            ewp = sb("ewp", [P, TILES, 3], BF16)
            or_ = sb("or_", [P, 3, P], BF16)
            oq = sb("oq", [P, 3, NPART, TC], BF16)
            zerob = sb("zerob", [P, P], BF16)
            half = sb("half", [P, 2, TC], F32)
            ohb = sb("ohb", [P, PG, 2, P], BF16)
            ohT = sb("ohT", [P, PG, 2, P], BF16)
            ohf = sb("ohf", [P, PG, 2, NB], F32)
            g_rows = sb("g_rows", [P, PG, 2, D], F32)
            hid = sb("hid", [P, PG, 2, D], F32)
            act1 = sb("act1", [P, PG, 2, D], F32)
            normed = sb("normed", [P, PG, 2, D], F32)
            nT = sb("nT", [P, PG, 2, 2, P], F32)
            msg = sb("msg", [P, PG, 2, D], F32)
            stat6 = sb("stat6", [P, PG, 2, 6], F32)
            meanvar = sb("meanvar", [P, PG, 2, 2], F32)
            vare = sb("vare", [P, PG, 2], F32)
            rstd_e = sb("rstd_e", [P, PG, 2], F32)
            psR = ctx.enter_context(nc.psum_tensor("psR", [P, 3, 512], F32))
            psT = ctx.enter_context(nc.psum_tensor("psT", [P, 1024], BF16))
            psH = ctx.enter_context(nc.psum_tensor("psH", [P, 2, D], F32))
            psM = ctx.enter_context(nc.psum_tensor("psM", [P, 2, 2, P], F32))
            ps2 = ctx.enter_context(nc.psum_tensor("ps2", [P, 2, D], F32))
            psG = ctx.enter_context(nc.psum_tensor("psG", [P, 2, D], F32))

            s_clear = sem("s_clear")
            s_rready = sem("s_rready")
            s_rused = sem("s_rused")
            s_rdone = sem("s_rdone")
            s_fin = sem("s_fin")
            s_sorted = sem("s_sorted")
            s_oh = sem("s_oh")
            s_turned = sem("s_turned")
            s_ohT = sem("s_ohT")
            s_gather = [[sem(f"s_gather{j}{n}") for n in range(2)] for j in range(PG)]
            s_idx = sem("s_idx")
            s_loc = sem("s_loc")
            s_first = sem("s_first")
            s_hid = sem("s_hid")
            s_act1 = sem("s_act1")
            s_bn = sem("s_bn")
            s_mv = sem("s_mv")
            s_eps = sem("s_eps")
            s_rstd = sem("s_rstd")
            s_norm = sem("s_norm")
            s_nx = sem("s_nx")
            s_nT = sem("s_nT")
            s_second = sem("s_second")
            s_msg = sem("s_msg")
            s_ohf = sem("s_ohf")
            s_sum = sem("s_sum")
            s_agg = sem("s_agg")

            block = ctx.enter_context(nc.Block())

            s_apart = {nc.gpsimd.engine: sem("s_apart_pool"), nc.vector.engine: sem("s_apart_dve")}

            def need(eng, sm_, value):
                if not isinstance(value, int) or value > 0:
                    eng.wait_ge(sm_, value)

            def need_apart(eng, *waits):
                for sm_, v in waits:
                    need(eng, sm_, v)
                eng.sem_inc(s_apart[eng.engine], 1)

            def run_slots(eng, prepare, slot, route, route_begin, route_end):
                route_begin(0)
                for j in range(GROUP):
                    route(j, j)
                with eng.Fori(1, RI) as i:
                    for j in range(GROUP):
                        route(i * GROUP + j, j)
                route_end(0)

                def group(g, routed=None):
                    prepare(g)
                    for jp in range(PG):
                        slot(g * PG + jp, g, jp, None if routed is None else routed)

                group(0)
                group(1)
                with eng.Fori(0, CHUNKS - 1) as c:
                    route_begin(c + 1)
                    with eng.Fori(2, 2 + RI) as i:
                        group(c * GI + i, (c + 1) * CP + (i - 2) * GROUP)
                    route_end(c + 1)
                    with eng.Fori(2 + RI, 2 + GI) as i:
                        group(c * GI + i)
                with eng.Fori(2, GI) as i:
                    group((CHUNKS - 1) * GI + i)
                prepare(GROUPS)
                for jp in range(PG):
                    slot(PAIRS + jp, GROUPS, jp, None)
                prepare(GROUPS + 1)
                for jp in range(DRAIN - PG):
                    slot(PAIRS + PG + jp, GROUPS + 1, jp, None)

            def has(s, lag):
                return not isinstance(s, int) or 0 <= s - lag < PAIRS

            @block.gpsimd
            def _(pool):
                pool.memset(zerob[:, :], 0.0).then_inc(s_clear, 1)
                pool.memset(agg[:, :, :], 0.0).then_inc(s_clear, 1)

                def route_end(c):
                    need_apart(pool, (s_sorted, c + 1))

                def slot(s, g, jp, routed):
                    if has(s, 0):
                        need(pool, s_hid, s - 2)
                        pool.tensor_copy(idx_pair[:, jp, :], idx[:, bass.ds(g * GROUP + 2 * jp, 2)]).then_inc(s_idx, 1)
                        need_apart(pool, (s_idx, s + 1))
                        for n in range(2):
                            pool.indirect_dma_start(
                                g_rows[:, jp, n, :], None, b_table[:, :],
                                bass.IndirectOffsetOnAxis(ap=idx_pair[:, jp, n:n + 1], axis=0)).then_inc(s_gather[jp][n], 16)
                    if has(s, 1):
                        k = (jp - 1) % PG
                        need_apart(pool, (s_mv, s), (s_norm, s - 3))
                        pool.tensor_scalar(vare[:, k, :], meanvar[:, k, :, 1], LN_EPS, None, ALU.add).then_inc(s_eps, 1)
                        pool.wait_ge(s_eps, s)
                        pool.tensor_tensor(rstd_e[:, k, :], vare[:, k, :], exph[:, 0:2], ALU.pow).then_inc(s_rstd, 1)
                    if has(s, 3):
                        k = jp
                        need(pool, s_sum, s - 5)
                        pool.tensor_copy(loc_pair[:, k, :], loc[:, bass.ds(g * GROUP + 2 * jp - 6, 2)]).then_inc(s_loc, 1)
                        need_apart(pool, (s_loc, s - 2))
                        for n in range(2):
                            ins = pool.tensor_scalar(ohf[:, k, n, :], iota_f[:, 0:NB], loc_pair[:, k, n:n + 1], None,
                                                     ALU.is_equal)
                        ins.then_inc(s_ohf, 1)

                run_slots(pool, lambda g: None, slot, lambda rc, j: None, lambda c: None,
                          route_end)

            @block.scalar
            def _(act):
                def slot(s, g, jp, routed):
                    if has(s, 3):
                        act.wait_ge(s_nx, s - 2)
                        need(act, s_second, s - 5)
                        nc.scalar.activation(nT[:, jp, :, :, :], psM[:, :, :, :], ACT.Copy).then_inc(s_nT, 1)
                    if has(s, 1):
                        k = (jp - 1) % PG
                        act.wait_ge(s_hid, s)
                        need(act, s_norm, s - 3)
                        nc.scalar.activation(act1[:, k, :, :], hid[:, k, :, :], ACT.Silu).then_inc(s_act1, 1)
                    if has(s, 0):
                        act.wait_ge(s_turned, s + 1)
                        need(act, s_first, s - 2)
                        nc.scalar.activation(ohT[:, jp, :, :], psT[:, 0:2 * P].rearrange("p (n e) -> p n e", n=2),
                                             ACT.Copy).then_inc(s_ohT, 1)
                    if has(s, 3):
                        act.wait_ge(s_second, s - 2)
                        need(act, s_sum, s - 5)
                        nc.scalar.activation(msg[:, jp, :, :], ps2[:, :, :], ACT.Silu).then_inc(s_msg, 1)

                run_slots(act, lambda g: None, slot, lambda rc, j: None, lambda c: None, lambda c: None)

            @block.tensor
            def _(pe):
                regs = [pe.alloc_register(f"pe_block{n}") for n in range(GROUP)]

                iota_zero = iota_q[:, :].unsqueeze(1).broadcast_to([P, 2, TC])

                def route_begin(c):
                    if isinstance(c, int):
                        pe.wait_ge(s_clear, 1)
                    else:
                        pe.wait_ge(s_sorted, c)
                    for k in range(3):
                        pe.matmul(psR[:, k, 0:TC * 2], zerob[0:EP, :], iota_zero[0:EP, :, :], start=True, stop=False)

                def route_end(c):
                    for k in range(3):
                        mm = pe.matmul(psR[:, k, 0:TC * 2], zerob[0:EP, :], iota_zero[0:EP, :, :], start=False, stop=True)
                    mm.then_inc(s_rdone, 1)

                def route(rc, j):
                    pe.wait_ge(s_rready, rc + 1)
                    for k in range(3):
                        mm = pe.matmul(psR[:, k, 0:2 * TC], or_[0:EP, j % 3, :],
                                       oq[0:EP, j % 3, 2 * k:2 * k + 2, :], start=False, stop=False)
                    mm.then_inc(s_rused, 1)

                def prepare(g):
                    lo = g * GROUP - 2
                    n0 = 0
                    if isinstance(lo, int) and lo < 0:
                        n0, lo = -lo, 0
                    n1 = GROUP
                    if isinstance(g, int) and g * GROUP - 2 + n1 > TILES:
                        n1 = TILES - (g * GROUP - 2)
                    if n1 > n0:
                        pe.reg_load(regs[n0:n1], tile_block[0:1, bass.ds(lo, n1 - n0)])

                def slot(s, g, jp, routed):
                    if has(s, 1):
                        k = (jp - 1) % PG
                        pe.wait_ge(s_ohT, s)
                        need(pe, s_hid, s - 1)
                        for n in range(2):
                            b = pe.snap(regs[2 * jp + n], min_val=0, max_val=BLOCKS - 1)
                            for part in range(3):
                                mm = pe.matmul(psH[:, n, :], ohT[:, k, n, :],
                                               a_sb[:, bass.ds(b, 1), part, :].rearrange("p a n -> p (a n)"),
                                               start=(part == 0), stop=(part == 2))
                        mm.then_inc(s_first, 1)
                    if has(s, 0):
                        pe.wait_ge(s_oh, s + 1)
                        need(pe, s_ohT, s)
                        for n in range(2):
                            mm = pe.transpose(psT[:, n * P:(n + 1) * P], ohb[:, jp, n, :], identb[:, :])
                        mm.then_inc(s_turned, 1)
                    if routed is not None:
                        route(routed + 2 * jp, 2 * jp)
                    if has(s, 3):
                        pe.wait_ge(s_nT, s - 2)
                        need(pe, s_msg, s - 3)
                        for n in range(2):
                            pe.matmul(ps2[:, n, :], ones3[:, :], c_rows[:, :], start=True, stop=False)
                            for k in range(2):
                                mm = pe.matmul(ps2[:, n, :], nT[:, jp, n, k, :], w2g[:, k, :],
                                               start=False, stop=(k == 1))
                        mm.then_inc(s_second, 1)
                    if routed is not None:
                        route(routed + 2 * jp + 1, 2 * jp + 1)
                    if has(s, 4):
                        k = (jp - 1) % PG
                        pe.wait_ge(s_msg, s - 3)
                        pe.wait_ge(s_ohf, s - 3)
                        need(pe, s_agg, 2 * s - 8)
                        for n in range(2):
                            mm = pe.matmul(psG[0:NB, n, :], ohf[:, k, n, :], msg[:, k, n, :], start=True, stop=True)
                        mm.then_inc(s_sum, 1)
                    if has(s, 2):
                        k = (jp - 2) % PG
                        pe.wait_ge(s_norm, s - 1)
                        need(pe, s_nT, s - 2)
                        for n in range(2):
                            for q in range(2):
                                mm = pe.transpose(psM[:, n, q, :], normed[:, k, n, q * P:(q + 1) * P], identf[:, :])
                        mm.then_inc(s_nx, 1)

                run_slots(pe, prepare, slot, route, route_begin, route_end)

            @block.vector
            def _(dve):
                V = nc.vector
                regs = [dve.alloc_register(f"dve_block{n}") for n in range(GROUP)]
                dve.wait_ge(s_clear, 2)

                def route(rc, j):
                    need(dve, s_rused, rc - 2)
                    c_t = bass.ds(rc, 1)
                    qf = q_col[:, :, :].rearrange("p c t -> p (c t)")
                    rf = r_col[:, :, :].rearrange("p c t -> p (c t)")
                    V.tensor_scalar(or_[0:EP, j % 3, :], iota_n[0:EP, :], rf[0:EP, c_t], None, ALU.is_equal)
                    for n in range(NPART):
                        vf = vals[:, n, :, :].rearrange("p c t -> p (c t)")
                        ins = V.tensor_scalar(oq[0:EP, j % 3, n, :], iota_q[0:EP, :], qf[0:EP, c_t], vf[0:EP, c_t],
                                              ALU.is_equal, ALU.mult)
                    ins.then_inc(s_rready, 1)

                def route_end(c):
                    dve.wait_ge(s_rdone, c + 1)
                    cols = bass.ds(c * TC, TC)
                    if not isinstance(c, int):
                        dve.wait_ge(s_fin, c * 4)
                    V.tensor_scalar(loc[:, cols], psR[:, 0, 0:TC], -1.0, None, ALU.add).then_inc(s_fin, 1)
                    V.tensor_scalar(half[:, 0, :], psR[:, 0, TC:2 * TC], 32.0, None, ALU.mult).then_inc(s_fin, 1)
                    V.tensor_copy(ewp[:, cols, 0], psR[:, 1, TC:2 * TC]).then_inc(s_fin, 1)
                    V.tensor_copy(ewp[:, cols, 1:3], psR[:, 2, 0:2 * TC].rearrange("p (k t) -> p t k", k=2)).then_inc(s_fin, 1)
                    dve.wait_ge(s_fin, c * 4 + 4)
                    V.tensor_tensor(idx[:, cols], half[:, 0, :], psR[:, 1, 0:TC], ALU.add).then_inc(s_sorted, 1)
                    need_apart(dve, (s_sorted, c + 1))

                def prepare(g):
                    lo = g * GROUP - 8
                    n0 = 0
                    if isinstance(lo, int) and lo < 0:
                        n0, lo = min(-lo, GROUP), 0
                    if n0 < GROUP:
                        n1 = GROUP
                        if isinstance(g, int) and g * GROUP - 8 + n1 > TILES:
                            n1 = TILES - (g * GROUP - 8)
                        dve.reg_load(regs[n0:n1], tile_block[0:1, bass.ds(lo, n1 - n0)])

                def slot(s, g, jp, routed):
                    if has(s, 2):
                        k = (jp - 2) % PG
                        dve.wait_ge(s_rstd, s - 1)
                        need(dve, s_nx, s - 4)
                        for n in range(2):
                            ins = V.tensor_scalar(normed[:, k, n, :], act1[:, k, n, :], meanvar[:, k, n, 0:1],
                                                  rstd_e[:, k, n:n + 1], ALU.subtract, ALU.mult)
                        ins.then_inc(s_norm, 1)
                    if has(s, 1):
                        k = (jp - 1) % PG
                        rounds = g if jp == 0 else g + 1
                        dve.wait_ge(s_first, s)
                        for n in range(2):
                            dve.wait_ge(s_gather[k][n], 16 * rounds)
                        need(dve, s_act1, s - 3)
                        V.tensor_tensor(hid[:, k, :, :], psH[:, :, :], g_rows[:, k, :, :], ALU.add).then_inc(s_hid, 1)
                    if has(s, 0):
                        need(dve, s_turned, s - 2)
                        for n in range(2):
                            t = g * GROUP + 2 * jp + n
                            V.tensor_scalar(ohb[:, jp, n, 0:NB], iota_n[:, 0:NB], loc[:, bass.ds(t, 1)], None,
                                            ALU.is_equal)
                        V.tensor_copy(ohb[:, jp, :, NB:P], ewp[:, bass.ds(g * GROUP + 2 * jp, 2), :]).then_inc(s_oh, 1)
                    if routed is not None:
                        route(routed + 2 * jp, 2 * jp)
                    if has(s, 1):
                        dve.wait_ge(s_act1, s)
                        need(dve, s_bn, 2 * s - 6)
                        for n in range(2):
                            V.bn_stats(stat6[:, k, n, :], act1[:, k, n, :]).then_inc(s_bn, 1)
                        need_apart(dve, (s_bn, 2 * s), (s_rstd, s - 3), (s_norm, s - 3))
                        for n in range(2):
                            ins = V.bn_aggr(meanvar[:, k, n, :], stat6[:, k, n, :])
                        ins.then_inc(s_mv, 1)
                    if routed is not None:
                        route(routed + 2 * jp + 1, 2 * jp + 1)
                    if has(s, 4):
                        dve.wait_ge(s_sum, s - 3)
                        for n in range(2):
                            b = dve.snap(regs[2 * jp + n], min_val=0, max_val=BLOCKS - 1)
                            need(dve, s_agg, 2 * s - 8 + n)
                            room = agg[:, bass.ds(b, 1), :].rearrange("p a n -> p (a n)")
                            V.tensor_tensor(room, psG[0:NB, n, :], room, ALU.add).then_inc(s_agg, 1)

                run_slots(dve, prepare, slot, route, lambda c: None, route_end)

        edge_mem.close()

        x_sb = alloc(whole, "x_sb", [NB, BLOCKS, D], F32)
        wts = (alloc(whole, "uw1", [P, 4, D], F32), alloc(whole, "uw2", [P, 2, D], F32),
               alloc(whole, "ub1c", [P, 2], F32), alloc(whole, "ub2b", [P, D], F32), alloc(whole, "wrb", [P, D], F32),
               alloc(whole, "brb", [P, 1], F32), alloc(whole, "w1s", [P, 2, H], F32), alloc(whole, "b1c", [P, HC], F32),
               alloc(whole, "w2s", [P, HC, D], F32), alloc(whole, "b2r", [1, D], F32))
        with nc.Block() as block:
            @block.sync
            def _(sp):
                def bc(v):
                    return v.rearrange("(a n) -> a n", a=1)

                todo = [(x_sb[:, :, :], x_v), (wts[0][:, :, :], uW1.rearrange("(k p) n -> p k n", p=P)),
                        (wts[1][:, :, :], uW2.rearrange("(k p) n -> p k n", p=P)),
                        (wts[2][:, :], ub1.rearrange("(k p) -> p k", p=P)),
                        (wts[3][:, :], bc(ub2).broadcast_to([P, D])),
                        (wts[4][:, :], wr.rearrange("n a -> a n").broadcast_to([P, D])),
                        (wts[5][:, :], bc(br).broadcast_to([P, 1])),
                        (wts[6][:, :, :], w1.rearrange("(k p) n -> p k n", p=P)),
                        (wts[7][:, :], b1.rearrange("(k p) -> p k", p=P)),
                        (wts[8][:, :, :], w2.rearrange("(k p) n -> p k n", p=P)),
                        (wts[9][:, :], bc(b2))]
                for to, frm in todo:
                    sp.dma_start(to, frm, allow_slow_non_contiguous=True).then_inc(s_late, 16)
                sp.wait_ge(s_late, 16 * len(todo))

        node_phase(nc, io, out_v, x_sb, h_sb, agg, identf, exph, score_d, wts)


def node_phase(nc, io, out_v, x_sb, h_sb, agg, identf, exph, score_d, wts):
    with ExitStack() as ctx:
        def sb(name, shape, dt):
            return ctx.enter_context(nc.sbuf_tensor(name, shape, dt))

        def sem(name):
            return ctx.enter_context(nc.semaphore(name))

        def bank(name):
            return ctx.enter_context(nc.psum_tensor(name, [P, 512], F32))

        uw1, uw2, ub1c, ub2b, wrb, brb, w1s, b1c, w2s, b2r = wts
        GB = 5
        NG = BLOCKS // GB
        GN = GB * NB
        CUT = (0, 320, GN)

        stage = sb("stage", [NB, GB, 4, P], F32)
        fT = sb("fT", [P, 4, GN], F32)
        u1 = sb("u1", [P, 2, GN], F32)
        x2s = sb("x2s", [NB, GB, D], F32)
        prod = sb("prod", [NB, 2, D], F32)
        sc5 = sb("sc5", [NB, GB], F32)
        stat = sb("stat", [NB, GB, 6], F32)
        mv = sb("mv_n", [NB, GB, 2], F32)
        rs = sb("rs", [NB, GB], F32)
        score = sb("score", [NB, BLOCKS], F32)
        stage2 = sb("stage2", [NB, GB, 2, P], F32)
        x2T = sb("x2T", [P, 2, GN], F32)
        gT = sb("gT", [P, HC, GN], F32)
        epst = sb("epst", [NB, GB], F32)
        ones1 = sb("ones1", [1, P], F32)
        row = sb("row", [NB, NODES], F32)
        tri = sb("tri_n", [NB, NB], F32)
        junk = sb("junk", [NB, NODES], BF16)
        counts = sb("counts", [NB, 3, BLOCKS], F32)
        coef = sb("coef", [NB, BLOCKS], F32)
        psX = [bank("psX0"), bank("psX1")]
        psU = [bank("psU0"), bank("psU1")]
        psY = [bank("psY0"), bank("psY1")]

        s_con = sem("s_con")
        s_res = sem("s_res")
        s_stage = sem("s_stage")
        s_fx = sem("s_fx")
        s_fT = sem("s_fT")
        s_u = sem("s_u")
        s_u1 = sem("s_u1")
        s_y = sem("s_y")
        s_x1 = sem("s_x1")
        s_st = sem("s_st")
        s_mvn = sem("s_mvn")
        s_ep = sem("s_ep")
        s_rs = sem("s_rs")
        s_x2 = sem("s_x2")
        s_x2c = sem("s_x2c")
        s_pr = sem("s_pr")
        s_score = sem("s_score")
        s_scd = sem("s_scd")
        s_row = sem("s_row_n")
        s_stage2 = sem("s_stage2")
        s_gx = sem("s_gx")
        s_x2T = sem("s_x2T")
        s_f = sem("s_f")
        s_g = sem("s_g")
        s_z = sem("s_z")
        s_Y = sem("s_Y")
        s_sum = sem("s_sum_n")
        s_apart = sem("s_apart_n")
        s_rank = sem("s_rank")
        s_fin = sem("s_fin_n")
        s_out = sem("s_out")

        block = ctx.enter_context(nc.Block())

        def need(eng, sm_, value):
            if not isinstance(value, int) or value > 0:
                eng.wait_ge(sm_, value)

        def before(b, k):
            return b - (1, 3)[k] if k < 2 else b - 2

        def groups(eng, body, last=None):
            body(0)
            body(1)
            with eng.Fori(2, NG) as g:
                body(g)
            if last:
                last(NG)

        def at(ap, b, n=1):
            v = ap[:, bass.ds(b, n), :] if len(ap.shape) == 3 else ap[:, bass.ds(b, n)]
            return v.rearrange("p a n -> p (a n)") if len(ap.shape) == 3 else v

        @block.sync
        def _(sp):
            sp.wait_ge(s_score, NG)
            sp.dma_start(score_d.rearrange("b p -> p b"), score[:, :], allow_slow_non_contiguous=True).then_inc(s_scd, 16)
            sp.wait_ge(s_scd, 16)
            sp.dma_start(row[:, :], score_d.rearrange("(a b) p -> a (b p)", a=1).broadcast_to([NB, NODES])).then_inc(s_row, 16)
            for g in range(NG):
                sp.wait_ge(s_fin, g + 1)
                sp.dma_start(out_v[:, g * GB:(g + 1) * GB, :], x_sb[:, g * GB:(g + 1) * GB, :]).then_inc(s_out, 16)
            sp.wait_ge(s_out, 16 * NG)

        @block.gpsimd
        def _(pool):
            pool.memset(ones1[:, :], 1.0).then_inc(s_con, 1)
            pool.memset(epst[:, :], LN_EPS).then_inc(s_con, 1)
            pool.memset(tri[:, :], 1.0).then_inc(s_con, 1)
            pool.wait_ge(s_con, 3)
            pool.affine_select(out=tri[:, :], in_=tri[:, :], compare_op=ALU.is_gt, fill=0.0, base=0,
                               pattern=[[-1, NB]], channel_multiplier=1).then_inc(s_con, 1)

            pool.tensor_tensor(x_sb[:, :, :], x_sb[:, :, :], ub2b[0:NB, :].unsqueeze(1).broadcast_to([NB, BLOCKS, D]),
                               ALU.add).then_inc(s_con, 1)
            pool.wait_ge(s_con, 5)

            def residual(g):
                for k in range(GB):
                    b = g * GB + k
                    pool.tensor_tensor(at(x_sb, b), at(x_sb, b), at(h_sb, b), ALU.add).then_inc(s_res, 1)

            def norm(g):
                pool.wait_ge(s_mvn, g)
                need(pool, s_x2, g - 1)
                pool.tensor_tensor(rs[:, :], mv[:, :, 1], epst[:, :], ALU.add).then_inc(s_ep, 1)
                pool.wait_ge(s_ep, g)
                pool.tensor_tensor(rs[:, :], rs[:, :], exph[0:NB, 0:GB], ALU.pow).then_inc(s_rs, 1)
                pool.wait_ge(s_x2, g)
                pool.tensor_copy(at(h_sb, (g - 1) * GB, GB), x2s[:, :, :].rearrange("p k n -> p (k n)")).then_inc(s_x2c, 1)

            def body(g):
                residual(g)
                if not (isinstance(g, int) and g == 0):
                    norm(g)

            groups(pool, body, norm)

            def copy2(g):
                for k in range(GB):
                    b = g * GB + k
                    need(pool, s_gx, b - GB + 1)
                    pool.wait_ge(s_x2c, NG)
                    pool.tensor_copy(stage2[:, k, :, :].rearrange("p k n -> p (k n)"), at(h_sb, b)).then_inc(s_stage2, 1)

            def total(g):
                g = g - 1
                pool.tensor_tensor(at(x_sb, g * GB, GB), at(x_sb, g * GB, GB), at(h_sb, g * GB, GB), ALU.add).then_inc(s_sum, 1)

            groups(pool, lambda g: (copy2(g), None if isinstance(g, int) and g == 0 else total(g)), total)

        @block.scalar
        def _(act):
            def body(g):
                for k in range(GB):
                    b = g * GB + k
                    act.wait_ge(s_fx, b + 1)
                    if k == 0:
                        need(act, s_u, 4 * g)
                    nc.scalar.activation(fT[:, :, k * NB:(k + 1) * NB],
                                         psX[k % 2][:, :].rearrange("p (q n) -> p q n", q=4)[:, :, 0:NB],
                                         ACT.Copy).then_inc(s_fT, 1)
                for f in range(2):
                    for n in range(2):
                        o = 2 * f + n
                        act.wait_ge(s_u, g * 4 + o + 1)
                        if o == 0:
                            need(act, s_y, g * GB)
                        nc.scalar.activation(u1[:, f, CUT[n]:CUT[n + 1]], psU[o % 2][:, 0:CUT[n + 1] - CUT[n]],
                                             ACT.Silu, bias=ub1c[:, f:f + 1]).then_inc(s_u1, 1)

            groups(act, body)

            def out_rows(g):
                for k in range(GB):
                    b = g * GB + k - GB
                    act.wait_ge(s_z, b + 1)
                    nc.scalar.activation(at(agg, b), psY[k % 2][0:NB, 0:D], ACT.Copy).then_inc(s_Y, 1)

            def body2(g):
                for k in range(GB):
                    b = g * GB + k
                    act.wait_ge(s_gx, b + 1)
                    if k == 0:
                        need(act, s_f, 2 * HC * g)
                    nc.scalar.activation(x2T[:, :, k * NB:(k + 1) * NB],
                                         psX[k % 2][:, 0:2 * P].rearrange("p (q n) -> p q n", q=2)[:, :, 0:NB],
                                         ACT.Copy).then_inc(s_x2T, 1)
                if not (isinstance(g, int) and g == 0):
                    out_rows(g)
                for hc in range(HC):
                    for n in range(2):
                        o = 2 * hc + n
                        act.wait_ge(s_f, g * 2 * HC + o + 1)
                        if o == 0:
                            need(act, s_z, g * GB)
                        nc.scalar.activation(gT[:, hc, CUT[n]:CUT[n + 1]], psU[o % 2][:, 0:CUT[n + 1] - CUT[n]],
                                             ACT.Gelu_apprx_tanh, bias=b1c[:, hc:hc + 1]).then_inc(s_g, 1)

            groups(act, body2, out_rows)

        @block.tensor
        def _(pe):
            pe.wait_ge(s_con, 4)

            def turn(g):
                for k in range(GB):
                    b = g * GB + k
                    pe.wait_ge(s_stage, b + 1)
                    need(pe, s_fT, before(b, k) + 1)
                    for q in range(4):
                        mm = pe.transpose(psX[k % 2][:, q * P:q * P + NB], stage[:, k, q, :], identf[0:NB, 0:NB])
                    mm.then_inc(s_fx, 1)

            def first(g):
                pe.wait_ge(s_fT, g * GB + GB)
                for f in range(2):
                    for n in range(2):
                        o = 2 * f + n
                        need(pe, s_u1, g * 4 + o - 1)
                        for q in range(4):
                            mm = pe.matmul(psU[o % 2][:, 0:CUT[n + 1] - CUT[n]], uw1[:, q, f * P:(f + 1) * P],
                                           fT[:, q, CUT[n]:CUT[n + 1]], start=(q == 0), stop=(q == 3))
                        mm.then_inc(s_u, 1)

            def second(g):
                pe.wait_ge(s_u1, g * 4)
                for k in range(GB):
                    b = g * GB + k - GB
                    need(pe, s_x1, before(b, k) + 1)
                    for q in range(2):
                        mm = pe.matmul(psY[k % 2][0:NB, 0:D], u1[:, q, k * NB:(k + 1) * NB], uw2[:, q, :],
                                       start=(q == 0), stop=(q == 1))
                    mm.then_inc(s_y, 1)

            def body(g):
                turn(g)
                if not (isinstance(g, int) and g == 0):
                    second(g)
                first(g)

            groups(pe, body, second)
            pe.wait_ge(s_x1, BLOCKS)

            def turn2(g):
                for k in range(GB):
                    b = g * GB + k
                    pe.wait_ge(s_stage2, b + 1)
                    need(pe, s_x2T, before(b, k) + 1)
                    for q in range(2):
                        mm = pe.transpose(psX[k % 2][:, q * P:q * P + NB], stage2[:, k, q, :], identf[0:NB, 0:NB])
                    mm.then_inc(s_gx, 1)

            def first2(g):
                pe.wait_ge(s_x2T, g * GB + GB)
                for hc in range(HC):
                    for n in range(2):
                        o = 2 * hc + n
                        need(pe, s_g, g * 2 * HC + o - 1)
                        for q in range(2):
                            mm = pe.matmul(psU[o % 2][:, 0:CUT[n + 1] - CUT[n]], w1s[:, q, hc * P:(hc + 1) * P],
                                           x2T[:, q, CUT[n]:CUT[n + 1]], start=(q == 0), stop=(q == 1))
                        mm.then_inc(s_f, 1)

            def second2(g):
                pe.wait_ge(s_g, g * 2 * HC)
                for k in range(GB):
                    b = g * GB + k - GB
                    need(pe, s_Y, before(b, k) + 1)
                    pe.matmul(psY[k % 2][0:NB, 0:D], ones1[:, 0:NB], b2r[:, :], start=True, stop=False)
                    for hc in range(HC):
                        mm = pe.matmul(psY[k % 2][0:NB, 0:D], gT[:, hc, k * NB:(k + 1) * NB], w2s[:, hc, :],
                                       start=False, stop=(hc == HC - 1))
                    mm.then_inc(s_z, 1)

            def body2(g):
                turn2(g)
                if not (isinstance(g, int) and g == 0):
                    second2(g)
                first2(g)

            groups(pe, body2, second2)

        @block.vector
        def _(dve):
            V = nc.vector

            def copy(g):
                for k in range(GB):
                    b = g * GB + k
                    need(dve, s_fx, b - GB + 1)
                    V.tensor_copy(stage[:, k, 0:2, :].rearrange("p k n -> p (k n)"), at(h_sb, b))
                    V.tensor_copy(stage[:, k, 2:4, :].rearrange("p k n -> p (k n)"), at(agg, b)).then_inc(s_stage, 1)

            def finish(g):
                for k in range(GB):
                    b = g * GB + k - GB
                    dve.wait_ge(s_res, b + 1)
                    dve.wait_ge(s_y, b + 1)
                    V.tensor_tensor(at(x_sb, b), psY[k % 2][0:NB, 0:D], at(x_sb, b), ALU.add).then_inc(s_x1, 1)
                need(dve, s_rs, g - 1)
                dve.wait_ge(s_x1, g * GB)
                dve.sem_inc(s_apart, 1)
                for k in range(GB):
                    b = g * GB + k - GB
                    ins = V.bn_stats(stat[:, k, :], at(x_sb, b))
                ins.then_inc(s_st, 1)
                dve.wait_ge(s_st, g)
                dve.sem_inc(s_apart, 1)
                for k in range(GB):
                    ins = V.bn_aggr(mv[:, k, :], stat[:, k, :])
                ins.then_inc(s_mvn, 1)
                dve.wait_ge(s_rs, g)
                need(dve, s_x2c, g - 1)
                need(dve, s_score, g - 1)
                for k in range(GB):
                    b = g * GB + k - GB
                    ins = V.tensor_scalar(x2s[:, k, :], at(x_sb, b), mv[:, k, 0:1], rs[:, k:k + 1],
                                          ALU.subtract, ALU.mult)
                ins.then_inc(s_x2, 1)
                dve.wait_ge(s_x2, g)
                for k in range(GB):
                    need(dve, s_pr, (g - 1) * GB + k - 1)
                    V.tensor_tensor_reduce(prod[:, k % 2, :], x2s[:, k, :], wrb[0:NB, :], 1.0, 0.0, ALU.mult, ALU.add,
                                           sc5[:, k:k + 1]).then_inc(s_pr, 1)
                dve.wait_ge(s_pr, g * GB)
                V.tensor_scalar(at(score, (g - 1) * GB, GB), sc5[:, :], brb[0:NB, :], None, ALU.add).then_inc(s_score, 1)

            def body(g):
                copy(g)
                if not (isinstance(g, int) and g == 0):
                    finish(g)

            groups(dve, body, finish)

            links = [0]

            def link(ins):
                links[0] += 1
                ins.then_inc(s_rank, 1)
                dve.wait_ge(s_rank, links[0])

            dve.wait_ge(s_row, 16)
            dve.wait_ge(s_con, 4)
            dve.wait_ge(s_score, NG)
            link(V.memset(counts[:, :, :], 0.0))
            for b in range(BLOCKS):
                lo, hi = b * NB, (b + 1) * NB
                own = score[:, b:b + 1]
                if b:
                    link(V.tensor_scalar(junk[:, 0:lo], row[:, 0:lo], own, None, ALU.is_ge, ALU.add,
                                         accum_out=counts[:, 0, b:b + 1]))
                link(V.tensor_scalar(junk[:, lo:NODES], row[:, lo:NODES], own, None, ALU.is_gt, ALU.add,
                                     accum_out=counts[:, 1, b:b + 1]))
                link(V.scalar_tensor_tensor(out=junk[:, lo:hi], in0=row[:, lo:hi], scalar=own, in1=tri[:, :],
                                            op0=ALU.is_equal, op1=ALU.mult))
                link(V.tensor_reduce(counts[:, 2, b:b + 1], junk[:, lo:hi], AX_X, ALU.add))
            link(V.tensor_tensor(counts[:, 0, :], counts[:, 0, :], counts[:, 1, :], ALU.add))
            link(V.tensor_tensor(counts[:, 0, :], counts[:, 0, :], counts[:, 2, :], ALU.add))
            link(V.scalar_tensor_tensor(out=coef[:, :], in0=counts[:, 0, :], scalar=float(TOPK), in1=score[:, :],
                                        op0=ALU.is_lt, op1=ALU.mult))
            for g in range(NG):
                dve.wait_ge(s_sum, g + 1)
                for k in range(GB):
                    b = g * GB + k
                    dve.wait_ge(s_Y, b + 1)
                    ins = V.scalar_tensor_tensor(out=x_sb[:, b, :], in0=agg[:, b, :], scalar=coef[:, b:b + 1],
                                                 in1=x_sb[:, b, :], op0=ALU.mult, op1=ALU.add)
                ins.then_inc(s_fin, 1)


_INS = ["x", "src", "dst", "edge_weight1", "L0_gnn_mW1", "L0_gnn_mb1", "L0_gnn_ln_g", "L0_gnn_ln_b", "L0_gnn_mW2",
        "L0_gnn_mb2", "L0_gnn_uW1", "L0_gnn_ub1", "L0_gnn_uW2", "L0_gnn_ub2", "L0_ffn_wr", "L0_ffn_br", "L0_ffn_w1",
        "L0_ffn_b1", "L0_ffn_w2", "L0_ffn_b2"]


def kernel(**inputs):
    import numpy as np
    import concourse.bacc as bacc
    from concourse.bass_utils import run_bass_kernel_spmd as run

    nc = bacc.Bacc("TRN2", target_bir_lowering=False, num_devices=1)
    arrays, io = {}, {}
    for name in _INS:
        a = np.ascontiguousarray(inputs[name])
        arrays[f"in_{name}"] = a
        io[name] = nc.dram_tensor(f"in_{name}", a.shape, mybir.dt.from_np(a.dtype), kind="ExternalInput").ap()
    io["out"] = nc.dram_tensor("out_0", (NODES, D), F32, kind="ExternalOutput").ap()
    build(nc, io)
    r = run(nc, [arrays], core_ids=[0])
    return r.results[0]["out_0"]
```

```python
from contextlib import ExitStack

import concourse.bass as bass
from concourse import mybir

F32 = mybir.dt.float32
BF16 = mybir.dt.bfloat16
I32 = mybir.dt.int32
ALU = mybir.AluOpType
ACT = mybir.ActivationFunctionType
AX_X = mybir.AxisListType.X

P = 128
NODES, D = 3125, 256
EDGES = 103125
NB = 125
BLOCKS = NODES // NB
EP = 125
EC = EDGES // EP
CHUNKS = 5
CC = EC // CHUNKS
GROUP = 6
RI = -(-CC // GROUP)
CP = RI * GROUP
GI = 31
TC = GI * GROUP
TILES = CHUNKS * TC
PAIRS = TILES // 2
GROUPS = CHUNKS * GI
PG = GROUP // 2
NPART = 2
RB = GROUP
AHEAD = 2
DRAIN = 5
H = 1024
HC = H // P
TOPK = int(0.5 * NODES) - 1
LN_EPS = 1e-5
MAGIC = 12582912.0
assert NODES == NB * BLOCKS and EDGES == EP * EC and EC == CHUNKS * CC
assert TC >= (EP * CC + BLOCKS * (P - 1)) // P and TC % 2 == 0


def build(nc, io):
    x, src, dst, ew = io["x"], io["src"], io["dst"], io["edge_weight1"]
    mW1, mb1, ln_g, ln_b = io["L0_gnn_mW1"], io["L0_gnn_mb1"], io["L0_gnn_ln_g"], io["L0_gnn_ln_b"]
    mW2, mb2 = io["L0_gnn_mW2"], io["L0_gnn_mb2"]
    uW1, ub1, uW2, ub2 = io["L0_gnn_uW1"], io["L0_gnn_ub1"], io["L0_gnn_uW2"], io["L0_gnn_ub2"]
    wr, br, w1, b1 = io["L0_ffn_wr"], io["L0_ffn_br"], io["L0_ffn_w1"], io["L0_ffn_b1"]
    w2, b2, out = io["L0_ffn_w2"], io["L0_ffn_b2"], io["out"]

    b_table = nc.dram_tensor("b_table", (NODES, D), F32, kind="Internal").ap()
    tile_block_d = nc.dram_tensor("tile_block_d", (CHUNKS, TC), I32, kind="Internal").ap()
    w_row_d = nc.dram_tensor("w_row_d", (1, 3 * D), BF16, kind="Internal").ap()
    c_row_d = nc.dram_tensor("c_row_d", (1, 3 * D), BF16, kind="Internal").ap()
    score_d = nc.dram_tensor("score_d", (BLOCKS, NB), F32, kind="Internal").ap()

    x_v = x.rearrange("(b p) d -> p b d", p=NB)
    out_v = out.rearrange("(b p) d -> p b d", p=NB)

    with ExitStack() as whole:
        def alloc(stack, name, shape, dt):
            return stack.enter_context(nc.sbuf_tensor(name, shape, dt))

        def semaphore(stack, name):
            return stack.enter_context(nc.semaphore(name))

        h_sb = alloc(whole, "h_sb", [NB, BLOCKS, D], F32)
        identf = alloc(whole, "identf", [P, P], F32)
        exph = alloc(whole, "exph", [P, BLOCKS], F32)

        agg = alloc(whole, "agg", [NB, BLOCKS, D], F32)
        s_late = semaphore(whole, "s_late")

        edge_mem = ExitStack()
        a_sb = alloc(edge_mem, "a_sb", [P, BLOCKS, 3, D], BF16)
        w2g = alloc(edge_mem, "w2g", [P, 2, D], F32)
        c_rows = alloc(edge_mem, "c_rows", [3, D], BF16)
        ones3 = alloc(edge_mem, "ones3", [3, P], BF16)
        identb = alloc(edge_mem, "identb", [P, P], BF16)
        iota_n = alloc(edge_mem, "iota_n", [P, P], BF16)
        iota_q = alloc(edge_mem, "iota_q", [P, TC], BF16)
        iota_f = alloc(edge_mem, "iota_f", [P, P], F32)
        q_all = alloc(edge_mem, "q_all", [P, CHUNKS * CP + AHEAD], F32)
        r_all = alloc(edge_mem, "r_all", [P, CHUNKS * CP + AHEAD], F32)
        vals_all = alloc(edge_mem, "vals_all", [P, NPART, CHUNKS * CP + AHEAD], F32)
        q_col = q_all[:, 0:CHUNKS * CP].rearrange("p (c t) -> p c t", c=CHUNKS)
        r_col = r_all[:, 0:CHUNKS * CP].rearrange("p (c t) -> p c t", c=CHUNKS)
        vals = vals_all[:, :, 0:CHUNKS * CP].rearrange("p n (c t) -> p n c t", c=CHUNKS)
        tile_block = alloc(edge_mem, "tile_block", [1, TILES], I32)

        with ExitStack() as ctx:
            def sb(name, shape, dt):
                return alloc(ctx, name, shape, dt)

            def sem(name):
                return semaphore(ctx, name)

            src_i = sb("src_i", [EP, EC], I32)
            dst_i = sb("dst_i", [EP, EC], I32)
            ew_f = sb("ew_f", [EP, EC], F32)
            f1 = sb("f1", [EP, EC], F32)
            f2 = sb("f2", [EP, EC], F32)
            blk = sb("blk", [EP, EC], BF16)
            eq = sb("eq", [EP, BLOCKS, CC], BF16)
            cum = sb("cum", [EP, BLOCKS, CC], F32)
            pos = sb("pos", [EP, CC], F32)
            zero = sb("zero", [P, 1], F32)
            cnt = sb("cnt", [EP, BLOCKS], BF16)
            sm = sb("sm", [P, 12, BLOCKS], F32)
            tb_f = sb("tb_f", [P, 2], F32)
            tb_i = sb("tb_i", [P, 2 * CHUNKS], I32)
            tid = sb("tid", [P, 2], F32)
            tri = sb("tri", [P, P], BF16)
            onesb = sb("onesb", [P, P], BF16)
            stats = sb("stats", [NB, BLOCKS, 6], F32)
            mv = sb("mv", [NB, BLOCKS, 2], F32)
            rstd = sb("rstd", [NB, BLOCKS], F32)
            hT = sb("hT", [P, 2, 2, P], F32)
            wij = sb("wij", [P, 2, 2 * D], F32)
            mb1_b = sb("mb1_b", [P, D], F32)
            res = sb("res", [NB, 3, D], F32)
            b_out = sb("b_out", [NB, 2, D], F32)
            w2raw = sb("w2raw", [P, 2, D], F32)
            gcol = sb("gcol", [P, 2], F32)
            bcol = sb("bcol", [P, 2], F32)
            rowf = sb("rowf", [1, 4, D], F32)
            rowb = sb("rowb", [1, 2, 3, D], BF16)
            psX = ctx.enter_context(nc.psum_tensor("psX", [P, 2, 512], F32))
            psAB = ctx.enter_context(nc.psum_tensor("psAB", [P, 2, 512], F32))
            psC = ctx.enter_context(nc.psum_tensor("psC", [P, 512], F32))
            psK = ctx.enter_context(nc.psum_tensor("psK", [P, 512], F32))

            s_x = sem("s_x")
            s_edges = sem("s_edges")
            s_weights = sem("s_weights")
            s_pool = sem("s_pool")
            s_dve = sem("s_dve")
            s_mv1 = sem("s_mv1")
            s_rstd1 = sem("s_rstd1")
            s_h = sem("s_h")
            s_hx = sem("s_hx")
            s_hT = sem("s_hT")
            s_ab = sem("s_ab")
            s_abf = sem("s_abf")
            s_bst = [sem("s_bst0"), sem("s_bst1")]
            s_bo = sem("s_bo")
            s_w2g = sem("s_w2g")
            s_c = sem("s_c")
            s_row = sem("s_row")
            s_mv_rows = sem("s_mv_rows")
            s_rows_in = sem("s_rows_in")
            s_cnt = sem("s_cnt")
            s_cntm = sem("s_cntm")
            s_cntu = sem("s_cntu")
            s_tb = sem("s_tb")
            s_tbd = sem("s_tbd")
            s_tbl = sem("s_tbl")

            block = ctx.enter_context(nc.Block())

            @block.sync
            def _(sp):
                sp.dma_start(src_i[:, :], src.rearrange("(p t) -> p t", p=EP)).then_inc(s_edges, 16)
                sp.dma_start(h_sb[:, :, :], x_v).then_inc(s_x, 16)
                sp.dma_start(wij[:, :, 0:D], mW1[0:D, :].rearrange("(k p) n -> p k n", p=P)).then_inc(s_weights, 16)
                sp.dma_start(wij[:, :, D:2 * D], mW1[D:2 * D, :].rearrange("(k p) n -> p k n", p=P)).then_inc(s_weights, 16)
                sp.dma_start(mb1_b[:, :], mb1.rearrange("(a n) -> a n", a=1).broadcast_to([P, D])).then_inc(s_weights, 16)
                sp.dma_start(w2raw[:, :, :], mW2.rearrange("(k p) n -> p k n", p=P)).then_inc(s_weights, 16)
                sp.dma_start(gcol[:, :], ln_g.rearrange("(k p) -> p k", p=P), allow_slow_non_contiguous=True).then_inc(s_weights, 16)
                sp.dma_start(bcol[:, :], ln_b.rearrange("(k p) -> p k", p=P), allow_slow_non_contiguous=True).then_inc(s_weights, 16)
                sp.dma_start(rowf[0:1, 0, :], mW1[2 * D:2 * D + 1, :]).then_inc(s_weights, 16)
                sp.dma_start(rowf[0:1, 1, :], mb2.rearrange("(a n) -> a n", a=1)).then_inc(s_weights, 16)
                for b in range(BLOCKS):
                    sp.wait_ge(s_bo, b + 1)
                    sp.dma_start(b_table[b * NB:(b + 1) * NB, :], b_out[:, b % 2, :]).then_inc(s_bst[b % 2], 16)
                sp.wait_ge(s_bst[0], 16 * 13)
                sp.wait_ge(s_bst[1], 16 * 12)

            @block.scalar
            def _(act):
                act.dma_start(dst_i[:, :], dst.rearrange("(p t) -> p t", p=EP)).then_inc(s_edges, 16)
                act.dma_start(ew_f[:, :], ew.rearrange("(p t) a -> p (t a)", p=EP)).then_inc(s_edges, 16)
                for b in range(BLOCKS):
                    act.wait_ge(s_hx, b + 1)
                    if b >= 2:
                        act.wait_ge(s_ab, b - 1)
                    nc.scalar.activation(hT[:, b % 2, :, 0:NB], psX[:, b % 2, 0:2 * P].rearrange(
                        "p (k n) -> p k n", k=2)[:, :, 0:NB], ACT.Copy).then_inc(s_hT, 1)
                act.wait_ge(s_row, 2)
                act.dma_start(w_row_d, rowb[0:1, 0, :, :].rearrange("a k n -> a (k n)")).then_inc(s_mv_rows, 16)
                act.dma_start(c_row_d, rowb[0:1, 1, :, :].rearrange("a k n -> a (k n)")).then_inc(s_mv_rows, 16)
                act.wait_ge(s_mv_rows, 32)
                for k in range(3):
                    act.dma_start(a_sb[NB + k:NB + k + 1, :, :, :].rearrange("p b k n -> p b (k n)"),
                                  w_row_d.unsqueeze(1).broadcast_to([1, BLOCKS, 3 * D])).then_inc(s_rows_in, 16)
                act.dma_start(c_rows[:, :], c_row_d.rearrange("a (k n) -> (a k) n", k=3)).then_inc(s_rows_in, 16)
                act.wait_ge(s_tb, CHUNKS)
                for c in range(CHUNKS):
                    act.dma_start(tile_block_d[c, 0:P].rearrange("(p a) -> p a", a=1),
                                  tb_i[:, 2 * c:2 * c + 1]).then_inc(s_tbd, 16)
                    act.dma_start(tile_block_d[c, P:TC].rearrange("(p a) -> p a", a=1),
                                  tb_i[0:TC - P, 2 * c + 1:2 * c + 2]).then_inc(s_tbd, 16)
                act.wait_ge(s_tbd, 32 * CHUNKS)
                act.dma_start(tile_block[:, :], tile_block_d.rearrange("(a c) t -> a (c t)", a=1)).then_inc(s_tbl, 16)
                act.wait_ge(s_tbl, 16)
                act.wait_ge(s_rows_in, 64)

            @block.gpsimd
            def _(pool):
                pool.memset(exph[:, :], -0.5).then_inc(s_pool, 1)
                pool.memset(identf[:, :], 0.0).then_inc(s_pool, 1)
                pool.wait_ge(s_pool, 2)
                pool.affine_select(out=identf[:, :], in_=identf[:, :], compare_op=ALU.not_equal, fill=1.0, base=0,
                                   pattern=[[-1, P]], channel_multiplier=1).then_inc(s_pool, 1)
                pool.iota(iota_f[:, :], pattern=[[1, P]], base=0, channel_multiplier=0,
                          allow_small_or_imprecise_dtypes=True).then_inc(s_pool, 1)
                pool.iota(iota_n[:, :], pattern=[[1, P]], base=0, channel_multiplier=0,
                          allow_small_or_imprecise_dtypes=True).then_inc(s_pool, 1)
                pool.iota(iota_q[:, :], pattern=[[1, TC]], base=0, channel_multiplier=0,
                          allow_small_or_imprecise_dtypes=True).then_inc(s_pool, 1)
                pool.iota(tid[:, :], pattern=[[P, 2]], base=0, channel_multiplier=1,
                          allow_small_or_imprecise_dtypes=True).then_inc(s_pool, 1)
                pool.memset(onesb[:, :], 1.0).then_inc(s_pool, 1)
                pool.wait_ge(s_pool, 8)
                pool.affine_select(out=tri[:, :], in_=onesb[:, :], compare_op=ALU.is_gt, fill=0.0, base=0,
                                   pattern=[[1, P]], channel_multiplier=-1).then_inc(s_pool, 1)
                pool.tensor_copy(identb[:, :], identf[:, :]).then_inc(s_pool, 1)
                pool.memset(ones3[:, :], 1.0).then_inc(s_pool, 1)
                pool.memset(zero[:, :], 0.0).then_inc(s_pool, 1)
                pool.wait_ge(s_mv1, 1)
                pool.tensor_scalar(rstd[:, :], mv[:, :, 1], LN_EPS, None, ALU.add).then_inc(s_pool, 1)
                pool.wait_ge(s_pool, 13)
                pool.tensor_tensor(rstd[:, :], rstd[:, :], exph[0:NB, :], ALU.pow).then_inc(s_rstd1, 1)
                pool.memset(q_all[:, :], 0.0).then_inc(s_pool, 1)
                pool.memset(r_all[:, :], 0.0).then_inc(s_pool, 1)
                pool.memset(vals_all[:, :, :], 0.0).then_inc(s_pool, 1)

            @block.tensor
            def _(pe):
                pe.wait_ge(s_pool, 3)
                pe.wait_ge(s_weights, 16 * 8)
                for b in range(BLOCKS + 1):
                    if b < BLOCKS:
                        pe.wait_ge(s_h, b + 1)
                        if b >= 2:
                            pe.wait_ge(s_hT, b - 1)
                        for k in range(2):
                            mm = pe.transpose(psX[:, b % 2, k * P:k * P + NB], h_sb[:, b, k * P:(k + 1) * P],
                                              identf[0:NB, 0:NB])
                        mm.then_inc(s_hx, 1)
                    if b >= 1:
                        a = b - 1
                        pe.wait_ge(s_hT, a + 1)
                        if a >= 2:
                            pe.wait_ge(s_abf, a - 1)
                        for k in range(2):
                            mm = pe.matmul(psAB[0:NB, a % 2, :], hT[:, a % 2, k, 0:NB], wij[:, k, :],
                                           start=(k == 0), stop=(k == 1))
                        mm.then_inc(s_ab, 1)
                for k in range(2):
                    mm = pe.matmul(psC[0:1, 0:D], bcol[:, k:k + 1], w2raw[:, k, :], start=(k == 0), stop=(k == 1))
                mm.then_inc(s_c, 1)
                pe.wait_ge(s_pool, 9)
                for c in range(CHUNKS):
                    pe.wait_ge(s_cnt, c + 1)
                    if c:
                        pe.wait_ge(s_cntu, c)
                    pe.matmul(psK[0:EP, 0:BLOCKS], tri[0:EP, 0:EP], cnt[:, :], start=True, stop=True)
                    pe.matmul(psK[:, 64:64 + BLOCKS], onesb[0:EP, :], cnt[:, :], start=True, stop=True).then_inc(s_cntm, 1)

            @block.vector
            def _(dve):
                links = [0]

                def link(ins):
                    links[0] += 1
                    ins.then_inc(s_dve, 1)
                    dve.wait_ge(s_dve, links[0])

                V = nc.vector
                dve.wait_ge(s_x, 16)
                for b in range(BLOCKS):
                    ins = V.bn_stats(stats[:, b, :], h_sb[:, b, :])
                link(ins)
                for b in range(BLOCKS):
                    ins = V.bn_aggr(mv[:, b, :], stats[:, b, :])
                ins.then_inc(s_mv1, 1)

                def split_row(n, source):
                    link(V.tensor_copy(rowb[0:1, n, 0, :], source))
                    link(V.tensor_tensor(rowf[0:1, 2, :], source, rowb[0:1, n, 0, :], ALU.subtract))
                    link(V.tensor_copy(rowb[0:1, n, 1, :], rowf[0:1, 2, :]))
                    link(V.tensor_tensor(rowf[0:1, 3, :], rowf[0:1, 2, :], rowb[0:1, n, 1, :], ALU.subtract))
                    V.tensor_copy(rowb[0:1, n, 2, :], rowf[0:1, 3, :]).then_inc(s_row, 1)

                dve.wait_ge(s_weights, 16 * 8)
                split_row(0, rowf[0:1, 0, :])
                for k in range(2):
                    V.tensor_scalar(w2g[:, k, :], w2raw[:, k, :], gcol[:, k:k + 1], None, ALU.mult).then_inc(s_w2g, 1)
                dve.wait_ge(s_rstd1, 1)
                for b in range(BLOCKS):
                    V.tensor_scalar(h_sb[:, b, :], h_sb[:, b, :], mv[:, b, 0:1], rstd[:, b:b + 1],
                                    ALU.subtract, ALU.mult).then_inc(s_h, 1)

                def tables(b):
                    dve.wait_ge(s_ab, b + 1)
                    if b >= 2:
                        dve.wait_ge(s_bst[b % 2], 16 * (b // 2))
                    V.tensor_copy(b_out[:, b % 2, :], psAB[0:NB, b % 2, D:2 * D]).then_inc(s_bo, 1)
                    link(V.tensor_tensor(res[:, 0, :], psAB[0:NB, b % 2, 0:D], mb1_b[0:NB, :], ALU.add))
                    link(V.tensor_copy(a_sb[0:NB, b, 0, :], res[:, 0, :]))
                    link(V.tensor_tensor(res[:, 1, :], res[:, 0, :], a_sb[0:NB, b, 0, :], ALU.subtract))
                    link(V.tensor_copy(a_sb[0:NB, b, 1, :], res[:, 1, :]))
                    link(V.tensor_tensor(res[:, 2, :], res[:, 1, :], a_sb[0:NB, b, 1, :], ALU.subtract))
                    ins = V.tensor_copy(a_sb[0:NB, b, 2, :], res[:, 2, :])
                    ins.then_inc(s_abf, 1)
                    dve.wait_ge(s_abf, b + 1)

                for b in range(BLOCKS):
                    tables(b)

                dve.wait_ge(s_c, 1)
                link(V.tensor_tensor(rowf[0:1, 1, :], psC[0:1, 0:D], rowf[0:1, 1, :], ALU.add))
                dve.wait_ge(s_row, 1)
                split_row(1, rowf[0:1, 1, :])

                def chunked(ap):
                    return ap.rearrange("p (c t) -> p c t", c=CHUNKS)

                def put(n, source):
                    V.tensor_copy(vals[0:EP, n, :, 0:CC], chunked(source))

                dve.wait_ge(s_edges, 48)
                dve.wait_ge(s_pool, 16)
                link(V.tensor_copy(f1[:, :], src_i[:, :]))
                link(V.tensor_scalar(f2[:, :], f1[:, :], 1.0 / NB, -(NB // 2) / NB, ALU.mult, ALU.add))
                link(V.tensor_scalar(f2[:, :], f2[:, :], MAGIC, None, ALU.add))
                link(V.tensor_scalar(f2[:, :], f2[:, :], -MAGIC, None, ALU.add))
                link(V.tensor_copy(blk[:, :], f2[:, :]))
                link(V.scalar_tensor_tensor(out=f1[:, :], in0=f2[:, :], scalar=-float(NB), in1=f1[:, :],
                                            op0=ALU.mult, op1=ALU.add))
                link(V.tensor_copy(f2[:, :], dst_i[:, :]))
                link(V.tensor_scalar(f2[:, :], f2[:, :], float(P), 1.0, ALU.mult, ALU.add))
                link(V.tensor_tensor(vals[0:EP, 0, :, 0:CC], chunked(f2[:, :]), chunked(f1[:, :]), ALU.add))
                put(1, ew_f[:, :])

                for c in range(CHUNKS):
                    cols = slice(c * CC, (c + 1) * CC)
                    for b in range(BLOCKS):
                        ins = V.tensor_scalar(eq[:, b, :], blk[:, cols], float(b), None, ALU.is_equal)
                    link(ins)
                    flat = eq[:, :, :].rearrange("p b t -> p (b t)")
                    link(V.tensor_tensor_scan(cum[:, :, :].rearrange("p b t -> p (b t)"), flat, flat, 0.0,
                                              ALU.add, ALU.bypass))
                    link(V.memset(sm[0:EP, 0, 0:1], 0.0))
                    link(V.tensor_copy(sm[0:EP, 0, 1:BLOCKS], cum[:, 0:BLOCKS - 1, CC - 1]))
                    link(V.tensor_tensor(sm[0:EP, 1, :], cum[:, :, CC - 1], sm[0:EP, 0, :], ALU.subtract))
                    ins = V.tensor_copy(cnt[:, :], sm[0:EP, 1, :])
                    ins.then_inc(s_cnt, 1)
                    dve.wait_ge(s_cntm, c + 1)
                    link(V.tensor_scalar(sm[:, 2, :], psK[:, 64:64 + BLOCKS], 1.0 / P, (P - 1.0) / P - 0.498,
                                         ALU.mult, ALU.add))
                    link(V.tensor_scalar(sm[:, 2, :], sm[:, 2, :], MAGIC, None, ALU.add))
                    link(V.tensor_scalar(sm[:, 2, :], sm[:, 2, :], -MAGIC, None, ALU.add))
                    link(V.tensor_tensor_scan(sm[:, 3, :], sm[:, 2, :], sm[:, 2, :], 0.0, ALU.add, ALU.bypass))
                    link(V.tensor_tensor(sm[:, 4, :], sm[:, 3, :], sm[:, 2, :], ALU.subtract))
                    link(V.scalar_tensor_tensor(out=sm[0:EP, 5, :], in0=sm[0:EP, 4, :], scalar=float(P),
                                                in1=psK[0:EP, 0:BLOCKS], op0=ALU.mult, op1=ALU.add))
                    ins = V.scalar_tensor_tensor(out=sm[0:EP, 6, :], in0=sm[0:EP, 5, :], scalar=-1.0,
                                                 in1=sm[0:EP, 0, :], op0=ALU.add, op1=ALU.subtract)
                    ins.then_inc(s_cntu, 1)
                    dve.wait_ge(s_cntu, c + 1)
                    for b in range(BLOCKS):
                        ins = V.scalar_tensor_tensor(out=cum[:, b, :], in0=cum[:, b, :], scalar=sm[0:EP, 6, b:b + 1],
                                                     in1=eq[:, b, :], op0=ALU.add, op1=ALU.mult)
                    link(ins)
                    link(V.tensor_reduce(pos[:, :], cum[:, :, :].rearrange("p b t -> p t b"), AX_X, ALU.add))
                    q = q_col[0:EP, c, 0:CC]
                    link(V.tensor_scalar(q, pos[:, :], 1.0 / P, -0.498, ALU.mult, ALU.add))
                    link(V.tensor_scalar(q, q, MAGIC, None, ALU.add))
                    link(V.tensor_scalar(q, q, -MAGIC, None, ALU.add))
                    link(V.scalar_tensor_tensor(out=r_col[0:EP, c, 0:CC], in0=q, scalar=-float(P), in1=pos[:, :],
                                                op0=ALU.mult, op1=ALU.add))
                    for n in range(2):
                        link(V.tensor_scalar(sm[:, 7, :], sm[:, 3, :], tid[:, n:n + 1], None, ALU.is_le))
                        link(V.tensor_reduce(tb_f[:, n:n + 1], sm[:, 7, :], AX_X, ALU.add))
                    V.tensor_scalar(tb_i[:, 2 * c:2 * c + 2], tb_f[:, :], BLOCKS - 1.0, None, ALU.min).then_inc(s_tb, 1)
                    dve.wait_ge(s_tb, c + 1)

        with ExitStack() as ctx:
            def sb(name, shape, dt):
                return alloc(ctx, name, shape, dt)

            def sem(name):
                return semaphore(ctx, name)

            loc = sb("loc", [P, TILES], F32)
            idx = sb("idx", [P, TILES], I32)
            idx_pair = sb("idx_pair", [P, PG, 2], I32)
            ewp = sb("ewp", [P, TILES, 3], BF16)
            or_ = sb("or_", [P, RB, P], F32)
            oq = sb("oq", [P, RB, NPART, TC], F32)
            zerob = sb("zerob", [P, P], BF16)
            rec = sb("rec", [P, 2, TC], I32)
            ew_r = sb("ew_r", [P, 2, TC], F32)
            ohb = sb("ohb", [P, PG, 2, P], BF16)
            ohT = sb("ohT", [P, PG, 2, P], BF16)
            ohf = sb("ohf", [P, PG, 2, NB], F32)
            g_rows = sb("g_rows", [P, PG, 2, D], F32)
            hid = sb("hid", [P, PG, 2, D], F32)
            act1 = sb("act1", [P, PG, 2, D], F32)
            normed = sb("normed", [P, PG, 2, D], F32)
            nT = sb("nT", [P, PG, 2, 2, P], F32)
            msg = sb("msg", [P, PG, 2, D], F32)
            stat6 = sb("stat6", [P, PG, 2, 6], F32)
            meanvar = sb("meanvar", [P, PG, 2, 2], F32)
            vare = sb("vare", [P, PG, 2], F32)
            neg_mean = sb("neg_mean", [P, PG, 2], F32)
            rstd_e = sb("rstd_e", [P, PG, 2], F32)
            shift = sb("shift", [P, PG, 2], F32)
            psR = ctx.enter_context(nc.psum_tensor("psR", [P, 512], F32))
            psT = ctx.enter_context(nc.psum_tensor("psT", [P, 1024], BF16))
            psH = ctx.enter_context(nc.psum_tensor("psH", [P, 2, D], F32))
            psM = ctx.enter_context(nc.psum_tensor("psM", [P, 2, 2, P], F32))
            ps2 = ctx.enter_context(nc.psum_tensor("ps2", [P, 2, D], F32))
            psG = ctx.enter_context(nc.psum_tensor("psG", [P, 2, D], F32))

            s_clear = sem("s_clear")
            s_rready = sem("s_rready")
            s_rused = sem("s_rused")
            s_rdone = sem("s_rdone")
            s_fin = sem("s_fin")
            s_sorted = sem("s_sorted")
            s_oh = sem("s_oh")
            s_turned = sem("s_turned")
            s_ohT = sem("s_ohT")
            s_gather = [[sem(f"s_gather{j}{n}") for n in range(2)] for j in range(PG)]
            s_idx = sem("s_idx")
            s_first = sem("s_first")
            s_hid = sem("s_hid")
            s_act1 = sem("s_act1")
            s_bn = sem("s_bn")
            s_mv = sem("s_mv")
            s_eps = sem("s_eps")
            s_pow = sem("s_pow")
            s_rstd = sem("s_rstd")
            s_norm = sem("s_norm")
            s_nx = sem("s_nx")
            s_nT = sem("s_nT")
            s_second = sem("s_second")
            s_msg = sem("s_msg")
            s_ohf = sem("s_ohf")
            s_sum = sem("s_sum")
            s_agg = sem("s_agg")

            block = ctx.enter_context(nc.Block())

            s_apart = {nc.gpsimd.engine: sem("s_apart_pool"), nc.vector.engine: sem("s_apart_dve")}

            def need(eng, sm_, value):
                if not isinstance(value, int) or value > 0:
                    eng.wait_ge(sm_, value)

            def need_apart(eng, *waits):
                for sm_, v in waits:
                    need(eng, sm_, v)
                eng.sem_inc(s_apart[eng.engine], 1)

            def run_slots(eng, prepare, slot, route, route_begin, route_end):
                route_begin(0)
                for j in range(GROUP):
                    route(j, j)
                with eng.Fori(1, RI) as i:
                    for j in range(GROUP):
                        route(i * GROUP + j, j)
                route_end(0)

                def group(g, routed=None):
                    prepare(g)
                    for jp in range(PG):
                        slot(g * PG + jp, g, jp, None if routed is None else routed)

                group(0)
                group(1)
                with eng.Fori(0, CHUNKS - 1) as c:
                    route_begin(c + 1)
                    with eng.Fori(2, 2 + RI) as i:
                        group(c * GI + i, (c + 1) * CP + (i - 2) * GROUP)
                    route_end(c + 1)
                    with eng.Fori(2 + RI, 2 + GI) as i:
                        group(c * GI + i)
                with eng.Fori(2, GI) as i:
                    group((CHUNKS - 1) * GI + i)
                prepare(GROUPS)
                for jp in range(PG):
                    slot(PAIRS + jp, GROUPS, jp, None)
                prepare(GROUPS + 1)
                for jp in range(DRAIN - PG):
                    slot(PAIRS + PG + jp, GROUPS + 1, jp, None)

            def has(s, lag):
                return not isinstance(s, int) or 0 <= s - lag < PAIRS

            @block.gpsimd
            def _(pool):
                pool.memset(zerob[:, :], 0.0).then_inc(s_clear, 1)
                pool.memset(agg[:, :, :], 0.0).then_inc(s_clear, 1)

                def route_end(c):
                    need_apart(pool, (s_sorted, c + 1))

                def slot(s, g, jp, routed):
                    if has(s, 0):
                        need(pool, s_hid, s - 2)
                        pool.tensor_copy(idx_pair[:, jp, :], idx[:, bass.ds(g * GROUP + 2 * jp, 2)]).then_inc(s_idx, 1)
                        need_apart(pool, (s_idx, s + 1))
                        for n in range(2):
                            pool.indirect_dma_start(
                                g_rows[:, jp, n, :], None, b_table[:, :],
                                bass.IndirectOffsetOnAxis(ap=idx_pair[:, jp, n:n + 1], axis=0)).then_inc(s_gather[jp][n], 16)
                    if has(s, 2):
                        k = (jp - 2) % PG
                        need_apart(pool, (s_mv, s - 1), (s_norm, s - 4))
                        pool.tensor_scalar(vare[:, k, :], meanvar[:, k, :, 1], LN_EPS, None, ALU.add).then_inc(s_eps, 1)
                        pool.tensor_scalar(neg_mean[:, k, :], meanvar[:, k, :, 0], -1.0, None, ALU.mult).then_inc(s_eps, 1)
                        pool.wait_ge(s_eps, 2 * s - 2)
                        pool.tensor_tensor(rstd_e[:, k, :], vare[:, k, :], exph[:, 0:2], ALU.pow).then_inc(s_pow, 1)
                        pool.wait_ge(s_pow, s - 1)
                        pool.tensor_tensor(shift[:, k, :], neg_mean[:, k, :], rstd_e[:, k, :], ALU.mult).then_inc(s_rstd, 1)

                run_slots(pool, lambda g: None, slot, lambda rc, j: None, lambda c: None,
                          route_end)

            @block.scalar
            def _(act):
                def slot(s, g, jp, routed):
                    k2 = (jp - 2) % PG
                    if has(s, 2):
                        act.wait_ge(s_hid, s - 1)
                        need(act, s_norm, s - 4)
                        nc.scalar.activation(act1[:, k2, :, :], hid[:, k2, :, :], ACT.Silu).then_inc(s_act1, 1)
                    if has(s, 3):
                        act.wait_ge(s_rstd, s - 2)
                        need(act, s_nx, s - 5)
                        for n in range(2):
                            ins = nc.scalar.activation(normed[:, jp, n, :], act1[:, jp, n, :], ACT.Identity,
                                                       scale=rstd_e[:, jp, n:n + 1], bias=shift[:, jp, n:n + 1])
                        ins.then_inc(s_norm, 1)
                    if has(s, 1):
                        k = (jp - 1) % PG
                        act.wait_ge(s_turned, s)
                        need(act, s_first, s - 3)
                        nc.scalar.activation(ohT[:, k, :, :], psT[:, 0:2 * P].rearrange("p (n e) -> p n e", n=2),
                                             ACT.Copy).then_inc(s_ohT, 1)
                    if has(s, 2):
                        act.wait_ge(s_oh, s - 1)
                        need(act, s_sum, s - 4)
                        nc.scalar.activation(ohf[:, k2, :, :], ohb[:, k2, :, 0:NB], ACT.Copy).then_inc(s_ohf, 1)
                    if has(s, 4):
                        k = (jp - 1) % PG
                        act.wait_ge(s_second, s - 3)
                        need(act, s_sum, s - 5)
                        nc.scalar.activation(msg[:, k, :, :], ps2[:, :, :], ACT.Silu).then_inc(s_msg, 1)
                    if has(s, 3):
                        act.wait_ge(s_nx, s - 2)
                        need(act, s_second, s - 5)
                        nc.scalar.activation(nT[:, jp, :, :, :], psM[:, :, :, :], ACT.Copy).then_inc(s_nT, 1)

                run_slots(act, lambda g: None, slot, lambda rc, j: None, lambda c: None, lambda c: None)

            @block.tensor
            def _(pe):
                regs = [pe.alloc_register(f"pe_block{n}") for n in range(GROUP)]

                iota_zero = iota_q[:, :].unsqueeze(1).broadcast_to([P, NPART, TC])

                def route_begin(c):
                    if isinstance(c, int):
                        pe.wait_ge(s_clear, 1)
                    else:
                        pe.wait_ge(s_sorted, c)
                    pe.matmul(psR[:, 0:NPART * TC], zerob[0:EP, :], iota_zero[0:EP, :, :], start=True, stop=False)

                def route_end(c):
                    pe.matmul(psR[:, 0:NPART * TC], zerob[0:EP, :], iota_zero[0:EP, :, :], start=False,
                              stop=True).then_inc(s_rdone, 1)

                def route(rc, j):
                    pe.wait_ge(s_rready, rc + 1)
                    pe.matmul(psR[:, 0:NPART * TC], or_[0:EP, j % RB, :], oq[0:EP, j % RB, :, :],
                              start=False, stop=False).then_inc(s_rused, 1)

                def prepare(g):
                    lo = g * GROUP - 4
                    n0 = 0
                    if isinstance(lo, int) and lo < 0:
                        n0, lo = -lo, 0
                    n1 = GROUP
                    if isinstance(g, int) and g * GROUP - 4 + n1 > TILES:
                        n1 = TILES - (g * GROUP - 4)
                    if n1 > n0:
                        pe.reg_load(regs[n0:n1], tile_block[0:1, bass.ds(lo, n1 - n0)])

                def slot(s, g, jp, routed):
                    if has(s, 2):
                        k = (jp - 2) % PG
                        pe.wait_ge(s_ohT, s - 1)
                        need(pe, s_hid, s - 2)
                        for n in range(2):
                            b = pe.snap(regs[2 * jp + n], min_val=0, max_val=BLOCKS - 1)
                            for part in range(3):
                                mm = pe.matmul(psH[:, n, :], ohT[:, k, n, :],
                                               a_sb[:, bass.ds(b, 1), part, :].rearrange("p a n -> p (a n)"),
                                               start=(part == 0), stop=(part == 2))
                        mm.then_inc(s_first, 1)
                    if has(s, 1):
                        k = (jp - 1) % PG
                        pe.wait_ge(s_oh, s)
                        need(pe, s_ohT, s - 1)
                        for n in range(2):
                            mm = pe.transpose(psT[:, n * P:(n + 1) * P], ohb[:, k, n, :], identb[:, :])
                        mm.then_inc(s_turned, 1)
                    if has(s, 5):
                        k = (jp - 2) % PG
                        pe.wait_ge(s_msg, s - 4)
                        pe.wait_ge(s_ohf, s - 4)
                        need(pe, s_agg, 2 * s - 10)
                        for n in range(2):
                            mm = pe.matmul(psG[0:NB, n, :], ohf[:, k, n, :], msg[:, k, n, :], start=True, stop=True)
                        mm.then_inc(s_sum, 1)
                    if has(s, 4):
                        k = (jp - 1) % PG
                        pe.wait_ge(s_nT, s - 3)
                        need(pe, s_msg, s - 4)
                        for n in range(2):
                            pe.matmul(ps2[:, n, :], ones3[:, :], c_rows[:, :], start=True, stop=False)
                            for q in range(2):
                                mm = pe.matmul(ps2[:, n, :], nT[:, k, n, q, :], w2g[:, q, :],
                                               start=False, stop=(q == 1))
                        mm.then_inc(s_second, 1)
                    if has(s, 3):
                        pe.wait_ge(s_norm, s - 2)
                        need(pe, s_nT, s - 3)
                        for n in range(2):
                            for q in range(2):
                                mm = pe.transpose(psM[:, n, q, :], normed[:, jp, n, q * P:(q + 1) * P], identf[:, :])
                        mm.then_inc(s_nx, 1)
                    if routed is not None:
                        route(routed + 2 * jp, 2 * jp)
                        route(routed + 2 * jp + 1, 2 * jp + 1)

                run_slots(pe, prepare, slot, route, route_begin, route_end)

            @block.vector
            def _(dve):
                V = nc.vector
                regs = [dve.alloc_register(f"dve_block{n}") for n in range(GROUP)]
                dve.wait_ge(s_clear, 2)

                def one_hot_r(rc, j):
                    need(dve, s_rused, rc - RB + 1)
                    V.tensor_scalar(or_[0:EP, j % RB, :], iota_n[0:EP, :], r_all[0:EP, bass.ds(rc, 1)], None,
                                    ALU.is_equal)

                def one_hot_q(rc, j):
                    c_t = bass.ds(rc, 1)
                    for n in range(NPART):
                        ins = V.tensor_scalar(oq[0:EP, j % RB, n, :], iota_q[0:EP, :], q_all[0:EP, c_t],
                                              vals_all[0:EP, n, c_t], ALU.is_equal, ALU.mult)
                    ins.then_inc(s_rready, 1)

                def route(rc, j):
                    one_hot_r(rc + AHEAD, j + AHEAD)
                    one_hot_q(rc + AHEAD, j + AHEAD)

                def route_begin(c):
                    if isinstance(c, int):
                        for j in range(AHEAD):
                            one_hot_r(j, j)
                            one_hot_q(j, j)

                def route_end(c):
                    dve.wait_ge(s_rdone, c + 1)
                    cols = bass.ds(c * TC, TC)
                    if not isinstance(c, int):
                        dve.wait_ge(s_fin, c * 8)

                    def link(n, ins):
                        ins.then_inc(s_fin, 1)
                        dve.wait_ge(s_fin, c * 8 + n)

                    link(1, V.tensor_copy(rec[:, 0, :], psR[:, 0:TC]))
                    link(2, V.tensor_single_scalar(rec[:, 1, :], rec[:, 0, :], P - 1, ALU.bitwise_and))
                    link(3, V.tensor_scalar(loc[:, cols], rec[:, 1, :], -1.0, None, ALU.add))
                    link(4, V.tensor_copy(ewp[:, cols, 0], psR[:, TC:2 * TC]))
                    link(5, V.tensor_tensor(ew_r[:, 0, :], psR[:, TC:2 * TC], ewp[:, cols, 0], ALU.subtract))
                    link(6, V.tensor_copy(ewp[:, cols, 1], ew_r[:, 0, :]))
                    link(7, V.tensor_tensor(ew_r[:, 1, :], ew_r[:, 0, :], ewp[:, cols, 1], ALU.subtract))
                    link(8, V.tensor_copy(ewp[:, cols, 2], ew_r[:, 1, :]))
                    V.tensor_single_scalar(idx[:, cols], rec[:, 0, :], 7, ALU.logical_shift_right).then_inc(s_sorted, 1)
                    need_apart(dve, (s_sorted, c + 1))

                def prepare(g):
                    lo = g * GROUP - 10
                    n0 = 0
                    if isinstance(lo, int) and lo < 0:
                        n0, lo = min(-lo, GROUP), 0
                    if n0 < GROUP:
                        n1 = GROUP
                        if isinstance(g, int) and g * GROUP - 10 + n1 > TILES:
                            n1 = TILES - (g * GROUP - 10)
                        dve.reg_load(regs[n0:n1], tile_block[0:1, bass.ds(lo, n1 - n0)])

                def slot(s, g, jp, routed):
                    if has(s, 2):
                        k = (jp - 2) % PG
                        rounds = g + 1 if jp >= 2 else g
                        dve.wait_ge(s_first, s - 1)
                        for n in range(2):
                            dve.wait_ge(s_gather[k][n], 16 * rounds)
                        need(dve, s_act1, s - 4)
                        V.tensor_tensor(hid[:, k, :, :], psH[:, :, :], g_rows[:, k, :, :], ALU.add).then_inc(s_hid, 1)
                    if routed is not None:
                        route(routed + 2 * jp, 2 * jp)
                    if has(s, 2):
                        dve.wait_ge(s_act1, s - 1)
                        need(dve, s_bn, 2 * s - 8)
                        for n in range(2):
                            V.bn_stats(stat6[:, k, n, :], act1[:, k, n, :]).then_inc(s_bn, 1)
                    if routed is not None:
                        one_hot_r(routed + 2 * jp + 1 + AHEAD, 2 * jp + 1 + AHEAD)
                    if has(s, 2):
                        need_apart(dve, (s_bn, 2 * s - 2), (s_rstd, s - 4))
                        for n in range(2):
                            ins = V.bn_aggr(meanvar[:, k, n, :], stat6[:, k, n, :])
                        ins.then_inc(s_mv, 1)

                    def add(n):
                        b = dve.snap(regs[2 * jp + n], min_val=0, max_val=BLOCKS - 1)
                        if n == 0:
                            dve.wait_ge(s_sum, s - 4)
                        need(dve, s_agg, 2 * s - 10 + n)
                        room = agg[:, bass.ds(b, 1), :].rearrange("p a n -> p (a n)")
                        V.tensor_tensor(room, psG[0:NB, n, :], room, ALU.add).then_inc(s_agg, 1)

                    if has(s, 5):
                        add(0)
                    if routed is not None:
                        one_hot_q(routed + 2 * jp + 1 + AHEAD, 2 * jp + 1 + AHEAD)
                    if has(s, 0):
                        need_apart(dve, (s_turned, s - 2), (s_ohf, s - 2))
                        for n in range(2):
                            t = g * GROUP + 2 * jp + n
                            V.tensor_scalar(ohb[:, jp, n, 0:NB], iota_n[:, 0:NB], loc[:, bass.ds(t, 1)], None,
                                            ALU.is_equal)
                        V.tensor_copy(ohb[:, jp, :, NB:P], ewp[:, bass.ds(g * GROUP + 2 * jp, 2), :]).then_inc(s_oh, 1)
                    if has(s, 5):
                        add(1)

                run_slots(dve, prepare, slot, route, route_begin, route_end)

        edge_mem.close()

        x_sb = alloc(whole, "x_sb", [NB, BLOCKS, D], F32)
        wts = (alloc(whole, "uw1", [P, 4, D], F32), alloc(whole, "uw2", [P, 2, D], F32),
               alloc(whole, "ub1c", [P, 2], F32), alloc(whole, "ub2b", [P, D], F32), alloc(whole, "wrb", [P, D], F32),
               alloc(whole, "brb", [P, 1], F32), alloc(whole, "w1s", [P, 2, H], F32), alloc(whole, "b1c", [P, HC], F32),
               alloc(whole, "w2s", [P, HC, D], F32), alloc(whole, "b2r", [1, D], F32))
        with nc.Block() as block:
            @block.sync
            def _(sp):
                def bc(v):
                    return v.rearrange("(a n) -> a n", a=1)

                todo = [(x_sb[:, :, :], x_v), (wts[0][:, :, :], uW1.rearrange("(k p) n -> p k n", p=P)),
                        (wts[1][:, :, :], uW2.rearrange("(k p) n -> p k n", p=P)),
                        (wts[2][:, :], ub1.rearrange("(k p) -> p k", p=P)),
                        (wts[3][:, :], bc(ub2).broadcast_to([P, D])),
                        (wts[4][:, :], wr.rearrange("n a -> a n").broadcast_to([P, D])),
                        (wts[5][:, :], bc(br).broadcast_to([P, 1])),
                        (wts[6][:, :, :], w1.rearrange("(k p) n -> p k n", p=P)),
                        (wts[7][:, :], b1.rearrange("(k p) -> p k", p=P)),
                        (wts[8][:, :, :], w2.rearrange("(k p) n -> p k n", p=P)),
                        (wts[9][:, :], bc(b2))]
                for to, frm in todo:
                    sp.dma_start(to, frm, allow_slow_non_contiguous=True).then_inc(s_late, 16)
                sp.wait_ge(s_late, 16 * len(todo))

        node_phase(nc, io, out_v, x_sb, h_sb, agg, identf, exph, score_d, wts)


def node_phase(nc, io, out_v, x_sb, h_sb, agg, identf, exph, score_d, wts):
    with ExitStack() as ctx:
        def sb(name, shape, dt):
            return ctx.enter_context(nc.sbuf_tensor(name, shape, dt))

        def sem(name):
            return ctx.enter_context(nc.semaphore(name))

        def bank(name):
            return ctx.enter_context(nc.psum_tensor(name, [P, 512], F32))

        uw1, uw2, ub1c, ub2b, wrb, brb, w1s, b1c, w2s, b2r = wts
        GB = 5
        NG = BLOCKS // GB
        GN = GB * NB
        CUT = (0, 320, GN)

        stage = sb("stage", [NB, GB, 4, P], F32)
        fT = sb("fT", [P, 4, GN], F32)
        u1 = sb("u1", [P, 2, GN], F32)
        x2s = sb("x2s", [NB, GB, D], F32)
        prod = sb("prod", [NB, 2, D], F32)
        sc5 = sb("sc5", [NB, GB], F32)
        stat = sb("stat", [NB, GB, 6], F32)
        mv = sb("mv_n", [NB, GB, 2], F32)
        rs = sb("rs", [NB, GB], F32)
        score = sb("score", [NB, BLOCKS], F32)
        stage2 = sb("stage2", [NB, GB, 2, P], F32)
        x2T = sb("x2T", [P, 2, GN], F32)
        gT = sb("gT", [P, HC, GN], F32)
        epst = sb("epst", [NB, GB], F32)
        ones1 = sb("ones1", [1, P], F32)
        row = sb("row", [NB, NODES], F32)
        tri = sb("tri_n", [NB, NB], F32)
        junk = sb("junk", [NB, NODES], BF16)
        counts = sb("counts", [NB, 3, BLOCKS], F32)
        coef = sb("coef", [NB, BLOCKS], F32)
        psX = [bank("psX0"), bank("psX1")]
        psU = [bank("psU0"), bank("psU1")]
        psY = [bank("psY0"), bank("psY1")]

        s_con = sem("s_con")
        s_res = sem("s_res")
        s_stage = sem("s_stage")
        s_fx = sem("s_fx")
        s_fT = sem("s_fT")
        s_u = sem("s_u")
        s_u1 = sem("s_u1")
        s_y = sem("s_y")
        s_x1 = sem("s_x1")
        s_st = sem("s_st")
        s_mvn = sem("s_mvn")
        s_ep = sem("s_ep")
        s_rs = sem("s_rs")
        s_x2 = sem("s_x2")
        s_x2c = sem("s_x2c")
        s_pr = sem("s_pr")
        s_score = sem("s_score")
        s_scd = sem("s_scd")
        s_row = sem("s_row_n")
        s_stage2 = sem("s_stage2")
        s_gx = sem("s_gx")
        s_x2T = sem("s_x2T")
        s_f = sem("s_f")
        s_g = sem("s_g")
        s_z = sem("s_z")
        s_Y = sem("s_Y")
        s_sum = sem("s_sum_n")
        s_apart = sem("s_apart_n")
        s_rank = sem("s_rank")
        s_fin = sem("s_fin_n")
        s_out = sem("s_out")

        block = ctx.enter_context(nc.Block())

        def need(eng, sm_, value):
            if not isinstance(value, int) or value > 0:
                eng.wait_ge(sm_, value)

        def before(b, k):
            return b - (1, 3)[k] if k < 2 else b - 2

        def groups(eng, body, last=None):
            body(0)
            body(1)
            with eng.Fori(2, NG) as g:
                body(g)
            if last:
                last(NG)

        def at(ap, b, n=1):
            v = ap[:, bass.ds(b, n), :] if len(ap.shape) == 3 else ap[:, bass.ds(b, n)]
            return v.rearrange("p a n -> p (a n)") if len(ap.shape) == 3 else v

        @block.sync
        def _(sp):
            sp.wait_ge(s_score, NG)
            sp.dma_start(score_d.rearrange("b p -> p b"), score[:, :], allow_slow_non_contiguous=True).then_inc(s_scd, 16)
            sp.wait_ge(s_scd, 16)
            sp.dma_start(row[:, :], score_d.rearrange("(a b) p -> a (b p)", a=1).broadcast_to([NB, NODES])).then_inc(s_row, 16)
            for g in range(NG):
                sp.wait_ge(s_fin, g + 1)
                sp.dma_start(out_v[:, g * GB:(g + 1) * GB, :], x_sb[:, g * GB:(g + 1) * GB, :]).then_inc(s_out, 16)
            sp.wait_ge(s_out, 16 * NG)

        @block.gpsimd
        def _(pool):
            pool.memset(ones1[:, :], 1.0).then_inc(s_con, 1)
            pool.memset(epst[:, :], LN_EPS).then_inc(s_con, 1)
            pool.memset(tri[:, :], 1.0).then_inc(s_con, 1)
            pool.wait_ge(s_con, 3)
            pool.affine_select(out=tri[:, :], in_=tri[:, :], compare_op=ALU.is_gt, fill=0.0, base=0,
                               pattern=[[-1, NB]], channel_multiplier=1).then_inc(s_con, 1)

            pool.tensor_tensor(x_sb[:, :, :], x_sb[:, :, :], ub2b[0:NB, :].unsqueeze(1).broadcast_to([NB, BLOCKS, D]),
                               ALU.add).then_inc(s_con, 1)
            pool.wait_ge(s_con, 5)

            def residual(g):
                for k in range(GB):
                    b = g * GB + k
                    pool.tensor_tensor(at(x_sb, b), at(x_sb, b), at(h_sb, b), ALU.add).then_inc(s_res, 1)

            def norm(g):
                pool.wait_ge(s_mvn, g)
                need(pool, s_x2, g - 1)
                pool.tensor_tensor(rs[:, :], mv[:, :, 1], epst[:, :], ALU.add).then_inc(s_ep, 1)
                pool.wait_ge(s_ep, g)
                pool.tensor_tensor(rs[:, :], rs[:, :], exph[0:NB, 0:GB], ALU.pow).then_inc(s_rs, 1)
                pool.wait_ge(s_x2, g)
                pool.tensor_copy(at(h_sb, (g - 1) * GB, GB), x2s[:, :, :].rearrange("p k n -> p (k n)")).then_inc(s_x2c, 1)

            def body(g):
                residual(g)
                if not (isinstance(g, int) and g == 0):
                    norm(g)

            groups(pool, body, norm)

            def copy2(g):
                for k in range(GB):
                    b = g * GB + k
                    need(pool, s_gx, b - GB + 1)
                    pool.wait_ge(s_x2c, NG)
                    pool.tensor_copy(stage2[:, k, :, :].rearrange("p k n -> p (k n)"), at(h_sb, b)).then_inc(s_stage2, 1)

            def total(g):
                g = g - 1
                pool.tensor_tensor(at(x_sb, g * GB, GB), at(x_sb, g * GB, GB), at(h_sb, g * GB, GB), ALU.add).then_inc(s_sum, 1)

            groups(pool, lambda g: (copy2(g), None if isinstance(g, int) and g == 0 else total(g)), total)

        @block.scalar
        def _(act):
            def body(g):
                for k in range(GB):
                    b = g * GB + k
                    act.wait_ge(s_fx, b + 1)
                    if k == 0:
                        need(act, s_u, 4 * g)
                    nc.scalar.activation(fT[:, :, k * NB:(k + 1) * NB],
                                         psX[k % 2][:, :].rearrange("p (q n) -> p q n", q=4)[:, :, 0:NB],
                                         ACT.Copy).then_inc(s_fT, 1)
                for f in range(2):
                    for n in range(2):
                        o = 2 * f + n
                        act.wait_ge(s_u, g * 4 + o + 1)
                        if o == 0:
                            need(act, s_y, g * GB)
                        nc.scalar.activation(u1[:, f, CUT[n]:CUT[n + 1]], psU[o % 2][:, 0:CUT[n + 1] - CUT[n]],
                                             ACT.Silu, bias=ub1c[:, f:f + 1]).then_inc(s_u1, 1)

            groups(act, body)

            def out_rows(g):
                for k in range(GB):
                    b = g * GB + k - GB
                    act.wait_ge(s_z, b + 1)
                    nc.scalar.activation(at(agg, b), psY[k % 2][0:NB, 0:D], ACT.Copy).then_inc(s_Y, 1)

            def body2(g):
                for k in range(GB):
                    b = g * GB + k
                    act.wait_ge(s_gx, b + 1)
                    if k == 0:
                        need(act, s_f, 2 * HC * g)
                    nc.scalar.activation(x2T[:, :, k * NB:(k + 1) * NB],
                                         psX[k % 2][:, 0:2 * P].rearrange("p (q n) -> p q n", q=2)[:, :, 0:NB],
                                         ACT.Copy).then_inc(s_x2T, 1)
                if not (isinstance(g, int) and g == 0):
                    out_rows(g)
                for hc in range(HC):
                    for n in range(2):
                        o = 2 * hc + n
                        act.wait_ge(s_f, g * 2 * HC + o + 1)
                        if o == 0:
                            need(act, s_z, g * GB)
                        nc.scalar.activation(gT[:, hc, CUT[n]:CUT[n + 1]], psU[o % 2][:, 0:CUT[n + 1] - CUT[n]],
                                             ACT.Gelu_apprx_tanh, bias=b1c[:, hc:hc + 1]).then_inc(s_g, 1)

            groups(act, body2, out_rows)

        @block.tensor
        def _(pe):
            pe.wait_ge(s_con, 4)

            def turn(g):
                for k in range(GB):
                    b = g * GB + k
                    pe.wait_ge(s_stage, b + 1)
                    need(pe, s_fT, before(b, k) + 1)
                    for q in range(4):
                        mm = pe.transpose(psX[k % 2][:, q * P:q * P + NB], stage[:, k, q, :], identf[0:NB, 0:NB])
                    mm.then_inc(s_fx, 1)

            def first(g):
                pe.wait_ge(s_fT, g * GB + GB)
                for f in range(2):
                    for n in range(2):
                        o = 2 * f + n
                        need(pe, s_u1, g * 4 + o - 1)
                        for q in range(4):
                            mm = pe.matmul(psU[o % 2][:, 0:CUT[n + 1] - CUT[n]], uw1[:, q, f * P:(f + 1) * P],
                                           fT[:, q, CUT[n]:CUT[n + 1]], start=(q == 0), stop=(q == 3))
                        mm.then_inc(s_u, 1)

            def second(g):
                pe.wait_ge(s_u1, g * 4)
                for k in range(GB):
                    b = g * GB + k - GB
                    need(pe, s_x1, before(b, k) + 1)
                    for q in range(2):
                        mm = pe.matmul(psY[k % 2][0:NB, 0:D], u1[:, q, k * NB:(k + 1) * NB], uw2[:, q, :],
                                       start=(q == 0), stop=(q == 1))
                    mm.then_inc(s_y, 1)

            def body(g):
                turn(g)
                if not (isinstance(g, int) and g == 0):
                    second(g)
                first(g)

            groups(pe, body, second)
            pe.wait_ge(s_x1, BLOCKS)

            def turn2(g):
                for k in range(GB):
                    b = g * GB + k
                    pe.wait_ge(s_stage2, b + 1)
                    need(pe, s_x2T, before(b, k) + 1)
                    for q in range(2):
                        mm = pe.transpose(psX[k % 2][:, q * P:q * P + NB], stage2[:, k, q, :], identf[0:NB, 0:NB])
                    mm.then_inc(s_gx, 1)

            def first2(g):
                pe.wait_ge(s_x2T, g * GB + GB)
                for hc in range(HC):
                    for n in range(2):
                        o = 2 * hc + n
                        need(pe, s_g, g * 2 * HC + o - 1)
                        for q in range(2):
                            mm = pe.matmul(psU[o % 2][:, 0:CUT[n + 1] - CUT[n]], w1s[:, q, hc * P:(hc + 1) * P],
                                           x2T[:, q, CUT[n]:CUT[n + 1]], start=(q == 0), stop=(q == 1))
                        mm.then_inc(s_f, 1)

            def second2(g):
                pe.wait_ge(s_g, g * 2 * HC)
                for k in range(GB):
                    b = g * GB + k - GB
                    need(pe, s_Y, before(b, k) + 1)
                    pe.matmul(psY[k % 2][0:NB, 0:D], ones1[:, 0:NB], b2r[:, :], start=True, stop=False)
                    for hc in range(HC):
                        mm = pe.matmul(psY[k % 2][0:NB, 0:D], gT[:, hc, k * NB:(k + 1) * NB], w2s[:, hc, :],
                                       start=False, stop=(hc == HC - 1))
                    mm.then_inc(s_z, 1)

            def body2(g):
                turn2(g)
                if not (isinstance(g, int) and g == 0):
                    second2(g)
                first2(g)

            groups(pe, body2, second2)

        @block.vector
        def _(dve):
            V = nc.vector

            def copy(g):
                for k in range(GB):
                    b = g * GB + k
                    need(dve, s_fx, b - GB + 1)
                    V.tensor_copy(stage[:, k, 0:2, :].rearrange("p k n -> p (k n)"), at(h_sb, b))
                    V.tensor_copy(stage[:, k, 2:4, :].rearrange("p k n -> p (k n)"), at(agg, b)).then_inc(s_stage, 1)

            def finish(g):
                for k in range(GB):
                    b = g * GB + k - GB
                    dve.wait_ge(s_res, b + 1)
                    dve.wait_ge(s_y, b + 1)
                    V.tensor_tensor(at(x_sb, b), psY[k % 2][0:NB, 0:D], at(x_sb, b), ALU.add).then_inc(s_x1, 1)
                need(dve, s_rs, g - 1)
                dve.wait_ge(s_x1, g * GB)
                dve.sem_inc(s_apart, 1)
                for k in range(GB):
                    b = g * GB + k - GB
                    ins = V.bn_stats(stat[:, k, :], at(x_sb, b))
                ins.then_inc(s_st, 1)
                dve.wait_ge(s_st, g)
                dve.sem_inc(s_apart, 1)
                for k in range(GB):
                    ins = V.bn_aggr(mv[:, k, :], stat[:, k, :])
                ins.then_inc(s_mvn, 1)
                dve.wait_ge(s_rs, g)
                need(dve, s_x2c, g - 1)
                need(dve, s_score, g - 1)
                for k in range(GB):
                    b = g * GB + k - GB
                    ins = V.tensor_scalar(x2s[:, k, :], at(x_sb, b), mv[:, k, 0:1], rs[:, k:k + 1],
                                          ALU.subtract, ALU.mult)
                ins.then_inc(s_x2, 1)
                dve.wait_ge(s_x2, g)
                for k in range(GB):
                    need(dve, s_pr, (g - 1) * GB + k - 1)
                    V.tensor_tensor_reduce(prod[:, k % 2, :], x2s[:, k, :], wrb[0:NB, :], 1.0, 0.0, ALU.mult, ALU.add,
                                           sc5[:, k:k + 1]).then_inc(s_pr, 1)
                dve.wait_ge(s_pr, g * GB)
                V.tensor_scalar(at(score, (g - 1) * GB, GB), sc5[:, :], brb[0:NB, :], None, ALU.add).then_inc(s_score, 1)

            def body(g):
                copy(g)
                if not (isinstance(g, int) and g == 0):
                    finish(g)

            groups(dve, body, finish)

            links = [0]

            def link(ins):
                links[0] += 1
                ins.then_inc(s_rank, 1)
                dve.wait_ge(s_rank, links[0])

            dve.wait_ge(s_row, 16)
            dve.wait_ge(s_con, 4)
            dve.wait_ge(s_score, NG)
            link(V.memset(counts[:, :, :], 0.0))
            for b in range(BLOCKS):
                lo, hi = b * NB, (b + 1) * NB
                own = score[:, b:b + 1]
                if b:
                    link(V.tensor_scalar(junk[:, 0:lo], row[:, 0:lo], own, None, ALU.is_ge, ALU.add,
                                         accum_out=counts[:, 0, b:b + 1]))
                link(V.tensor_scalar(junk[:, lo:NODES], row[:, lo:NODES], own, None, ALU.is_gt, ALU.add,
                                     accum_out=counts[:, 1, b:b + 1]))
                link(V.scalar_tensor_tensor(out=junk[:, lo:hi], in0=row[:, lo:hi], scalar=own, in1=tri[:, :],
                                            op0=ALU.is_equal, op1=ALU.mult))
                link(V.tensor_reduce(counts[:, 2, b:b + 1], junk[:, lo:hi], AX_X, ALU.add))
            link(V.tensor_tensor(counts[:, 0, :], counts[:, 0, :], counts[:, 1, :], ALU.add))
            link(V.tensor_tensor(counts[:, 0, :], counts[:, 0, :], counts[:, 2, :], ALU.add))
            link(V.scalar_tensor_tensor(out=coef[:, :], in0=counts[:, 0, :], scalar=float(TOPK), in1=score[:, :],
                                        op0=ALU.is_lt, op1=ALU.mult))
            for g in range(NG):
                dve.wait_ge(s_sum, g + 1)
                for k in range(GB):
                    b = g * GB + k
                    dve.wait_ge(s_Y, b + 1)
                    ins = V.scalar_tensor_tensor(out=x_sb[:, b, :], in0=agg[:, b, :], scalar=coef[:, b:b + 1],
                                                 in1=x_sb[:, b, :], op0=ALU.mult, op1=ALU.add)
                ins.then_inc(s_fin, 1)


_INS = ["x", "src", "dst", "edge_weight1", "L0_gnn_mW1", "L0_gnn_mb1", "L0_gnn_ln_g", "L0_gnn_ln_b", "L0_gnn_mW2",
        "L0_gnn_mb2", "L0_gnn_uW1", "L0_gnn_ub1", "L0_gnn_uW2", "L0_gnn_ub2", "L0_ffn_wr", "L0_ffn_br", "L0_ffn_w1",
        "L0_ffn_b1", "L0_ffn_w2", "L0_ffn_b2"]


def kernel(**inputs):
    import numpy as np
    import concourse.bacc as bacc
    from concourse.bass_utils import run_bass_kernel_spmd as run

    nc = bacc.Bacc("TRN2", target_bir_lowering=False, num_devices=1)
    arrays, io = {}, {}
    for name in _INS:
        a = np.ascontiguousarray(inputs[name])
        arrays[f"in_{name}"] = a
        io[name] = nc.dram_tensor(f"in_{name}", a.shape, mybir.dt.from_np(a.dtype), kind="ExternalInput").ap()
    io["out"] = nc.dram_tensor("out_0", (NODES, D), F32, kind="ExternalOutput").ap()
    build(nc, io)
    r = run(nc, [arrays], core_ids=[0])
    return r.results[0]["out_0"]
```

```python
from contextlib import ExitStack

import concourse.bass as bass
from concourse import mybir

F32 = mybir.dt.float32
BF16 = mybir.dt.bfloat16
I32 = mybir.dt.int32
F32R = mybir.dt.float32r
ALU = mybir.AluOpType
ACT = mybir.ActivationFunctionType
AX_X = mybir.AxisListType.X

P = 128
NODES, D = 3125, 256
EDGES = 103125
NB = 125
BLOCKS = NODES // NB
EP = 125
EC = EDGES // EP
CHUNKS = 5
CC = EC // CHUNKS
GROUP = 6
RI = -(-CC // GROUP)
CP = RI * GROUP
POOL_CHUNKS = (0, 2, 3)
GI = 31
TC = GI * GROUP
TILES = CHUNKS * TC
PAIRS = TILES // 2
GROUPS = CHUNKS * GI
PG = GROUP // 2
NPART = 2
RB = GROUP
AHEAD = 2
DRAIN = 5
H = 1024
HC = H // P
TOPK = int(0.5 * NODES) - 1
LN_EPS = 1e-5
MAGIC = 12582912.0
assert NODES == NB * BLOCKS and EDGES == EP * EC and EC == CHUNKS * CC
assert TC >= (EP * CC + BLOCKS * (P - 1)) // P and TC % 2 == 0


def build(nc, io):
    x, src, dst, ew = io["x"], io["src"], io["dst"], io["edge_weight1"]
    mW1, mb1, ln_g, ln_b = io["L0_gnn_mW1"], io["L0_gnn_mb1"], io["L0_gnn_ln_g"], io["L0_gnn_ln_b"]
    mW2, mb2 = io["L0_gnn_mW2"], io["L0_gnn_mb2"]
    uW1, ub1, uW2, ub2 = io["L0_gnn_uW1"], io["L0_gnn_ub1"], io["L0_gnn_uW2"], io["L0_gnn_ub2"]
    wr, br, w1, b1 = io["L0_ffn_wr"], io["L0_ffn_br"], io["L0_ffn_w1"], io["L0_ffn_b1"]
    w2, b2, out = io["L0_ffn_w2"], io["L0_ffn_b2"], io["out"]

    b_table = nc.dram_tensor("b_table", (NODES, D), F32, kind="Internal").ap()
    tile_block_d = nc.dram_tensor("tile_block_d", (CHUNKS, TC), I32, kind="Internal").ap()
    c_row_d = nc.dram_tensor("c_row_d", (1, 3 * D), BF16, kind="Internal").ap()
    score_d = nc.dram_tensor("score_d", (BLOCKS, NB), F32, kind="Internal").ap()

    x_v = x.rearrange("(b p) d -> p b d", p=NB)
    out_v = out.rearrange("(b p) d -> p b d", p=NB)

    with ExitStack() as whole:
        def alloc(stack, name, shape, dt):
            return stack.enter_context(nc.sbuf_tensor(name, shape, dt))

        def semaphore(stack, name):
            return stack.enter_context(nc.semaphore(name))

        h_sb = alloc(whole, "h_sb", [NB, BLOCKS, D], F32)
        identf = alloc(whole, "identf", [P, P], F32)
        exph = alloc(whole, "exph", [P, BLOCKS], F32)

        agg = alloc(whole, "agg", [NB, BLOCKS, D], F32)
        s_late = semaphore(whole, "s_late")

        wts = (alloc(whole, "uw1", [P, 4, D], F32), alloc(whole, "uw2", [P, 2, D], F32),
               alloc(whole, "ub1c", [P, 2], F32), alloc(whole, "ub2b", [P, D], F32), alloc(whole, "wrb", [P, D], F32),
               alloc(whole, "brb", [P, 1], F32))

        edge_mem = ExitStack()
        a_sb = alloc(edge_mem, "a_sb", [P, BLOCKS, 2, D], F32R)
        w2g = alloc(edge_mem, "w2g", [P, 2, D], F32)
        c_rows = alloc(edge_mem, "c_rows", [3, D], BF16)
        ones3 = alloc(edge_mem, "ones3", [3, P], BF16)
        identb = alloc(edge_mem, "identb", [P, P], BF16)
        iota_n = alloc(edge_mem, "iota_n", [P, P], BF16)
        iota_q = alloc(edge_mem, "iota_q", [P, TC], BF16)
        iota_f = alloc(edge_mem, "iota_f", [P, P], F32)
        q_all = alloc(edge_mem, "q_all", [P, CHUNKS * CP + AHEAD], F32)
        r_all = alloc(edge_mem, "r_all", [P, CHUNKS * CP + AHEAD], F32)
        vals_all = alloc(edge_mem, "vals_all", [P, NPART, CHUNKS * CP + AHEAD], F32)
        q_col = q_all[:, 0:CHUNKS * CP].rearrange("p (c t) -> p c t", c=CHUNKS)
        r_col = r_all[:, 0:CHUNKS * CP].rearrange("p (c t) -> p c t", c=CHUNKS)
        vals = vals_all[:, :, 0:CHUNKS * CP].rearrange("p n (c t) -> p n c t", c=CHUNKS)
        tile_block = alloc(edge_mem, "tile_block", [1, TILES], I32)

        with ExitStack() as ctx:
            def sb(name, shape, dt):
                return alloc(ctx, name, shape, dt)

            def sem(name):
                return semaphore(ctx, name)

            src_i = sb("src_i", [EP, EC], I32)
            dst_i = sb("dst_i", [EP, EC], I32)
            ew_f = sb("ew_f", [EP, EC], F32)
            f1 = sb("f1", [EP, EC], F32)
            f2 = sb("f2", [EP, EC], F32)
            blk = sb("blk", [EP, EC], BF16)
            eqs = [sb("eq0", [EP, BLOCKS, CC], BF16), sb("eq1", [EP, BLOCKS, CC], BF16)]
            cums = [sb("cum", [EP, BLOCKS, CC], F32)[:, :, :],
                    agg[:, :, :].rearrange("p b d -> p (b d)")[0:EP, 0:BLOCKS * CC].rearrange("p (b t) -> p b t", t=CC)]
            base = sb("base", [EP, 2, BLOCKS], F32)
            pos = sb("pos", [EP, CC], F32)
            cnt = sb("cnt", [EP, BLOCKS], BF16)
            sm = sb("sm", [P, 12, BLOCKS], F32)
            tb_f = sb("tb_f", [P, 2], F32)
            tb_i = sb("tb_i", [P, 2 * CHUNKS], I32)
            tid = sb("tid", [P, 2], F32)
            tri = sb("tri", [P, P], BF16)
            onesb = sb("onesb", [P, P], BF16)
            stats = sb("stats", [NB, BLOCKS, 6], F32)
            mv = sb("mv", [NB, BLOCKS, 2], F32)
            rstd = sb("rstd", [NB, BLOCKS], F32)
            hT = sb("hT", [P, 2, 2, P], F32)
            wij = sb("wij", [P, 2, 2 * D], F32)
            mb1_b = sb("mb1_b", [P, D], F32)
            res = sb("res", [NB, D], F32)
            b_out = sb("b_out", [NB, 2, D], F32)
            w2raw = sb("w2raw", [P, 2, D], F32)
            gcol = sb("gcol", [P, 2], F32)
            bcol = sb("bcol", [P, 2], F32)
            rowf = sb("rowf", [1, 3, D], F32)
            rowb = sb("rowb", [1, 3, D], BF16)
            WP = 96
            w_last = sb("w_last", [P, D], F32)
            w_parts = sb("w_parts", [P, 2, D], F32R)
            psX = ctx.enter_context(nc.psum_tensor("psX", [P, 2, 512], F32))
            psA = ctx.enter_context(nc.psum_tensor("psA", [P, 2, 512], F32))
            psB = ctx.enter_context(nc.psum_tensor("psB", [P, 2, 512], F32))
            psC = ctx.enter_context(nc.psum_tensor("psC", [P, 512], F32))
            psK = ctx.enter_context(nc.psum_tensor("psK", [P, 512], F32))

            s_x = sem("s_x")
            s_edges = sem("s_edges")
            s_last = sem("s_last")
            s_wrows = sem("s_wrows")
            s_weights = sem("s_weights")
            s_pool = sem("s_pool")
            s_dve = sem("s_dve")
            s_mv1 = sem("s_mv1")
            s_rstd1 = sem("s_rstd1")
            s_h = sem("s_h")
            s_hx = sem("s_hx")
            s_hT = sem("s_hT")
            s_ab = sem("s_ab")
            s_abf = sem("s_abf")
            s_bst = [sem("s_bst0"), sem("s_bst1")]
            s_bo = sem("s_bo")
            s_w2g = sem("s_w2g")
            s_c = sem("s_c")
            s_row = sem("s_row")
            s_mv_rows = sem("s_mv_rows")
            s_rows_in = sem("s_rows_in")
            s_cnt = sem("s_cnt")
            s_cntm = sem("s_cntm")
            s_base = sem("s_base")
            s_add = sem("s_add")
            s_place = sem("s_place")
            s_tb = sem("s_tb")
            s_tbd = sem("s_tbd")
            s_tbl = sem("s_tbl")

            block = ctx.enter_context(nc.Block())

            @block.sync
            def _(sp):
                sp.dma_start(src_i[:, :], src.rearrange("(p t) -> p t", p=EP)).then_inc(s_edges, 16)
                sp.dma_start(h_sb[:, :, :], x_v).then_inc(s_x, 16)
                sp.dma_start(wij[:, :, 0:D], mW1[0:D, :].rearrange("(k p) n -> p k n", p=P)).then_inc(s_weights, 16)
                sp.dma_start(wij[:, :, D:2 * D], mW1[D:2 * D, :].rearrange("(k p) n -> p k n", p=P)).then_inc(s_weights, 16)
                sp.dma_start(mb1_b[:, :], mb1.rearrange("(a n) -> a n", a=1).broadcast_to([P, D])).then_inc(s_weights, 16)
                sp.dma_start(w2raw[:, :, :], mW2.rearrange("(k p) n -> p k n", p=P)).then_inc(s_weights, 16)
                sp.dma_start(gcol[:, :], ln_g.rearrange("(k p) -> p k", p=P), allow_slow_non_contiguous=True).then_inc(s_weights, 16)
                sp.dma_start(bcol[:, :], ln_b.rearrange("(k p) -> p k", p=P), allow_slow_non_contiguous=True).then_inc(s_weights, 16)
                sp.dma_start(w_last[WP:P, :], mW1[2 * D:2 * D + 1, :].broadcast_to([P - WP, D])).then_inc(s_last, 16)
                sp.dma_start(rowf[0:1, 0, :], mb2.rearrange("(a n) -> a n", a=1)).then_inc(s_weights, 16)
                for b in range(BLOCKS):
                    sp.wait_ge(s_bo, b + 1)
                    sp.dma_start(b_table[b * NB:(b + 1) * NB, :], b_out[:, b % 2, :]).then_inc(s_bst[b % 2], 16)
                sp.wait_ge(s_bst[0], 16 * 13)
                sp.wait_ge(s_bst[1], 16 * 12)

            @block.scalar
            def _(act):
                act.dma_start(dst_i[:, :], dst.rearrange("(p t) -> p t", p=EP)).then_inc(s_edges, 16)
                act.dma_start(ew_f[:, :], ew.rearrange("(p t) a -> p (t a)", p=EP)).then_inc(s_edges, 16)
                act.wait_ge(s_pool, 13)
                for b in range(BLOCKS):
                    nc.scalar.activation(a_sb[WP:P, b, :, :], w_parts[WP:P, :, :], ACT.Copy).then_inc(s_wrows, 1)


                def b_rows(b):
                    act.wait_ge(s_ab, b + 1)
                    if b >= 2:
                        act.wait_ge(s_bst[b % 2], 16 * (b // 2))
                    nc.scalar.activation(b_out[:, b % 2, :], psB[0:NB, b % 2, 0:D], ACT.Copy).then_inc(s_bo, 1)

                for b in range(BLOCKS):
                    act.wait_ge(s_hx, b + 1)
                    if b >= 2:
                        act.wait_ge(s_ab, b - 1)
                    nc.scalar.activation(hT[:, b % 2, :, 0:NB], psX[:, b % 2, 0:2 * P].rearrange(
                        "p (k n) -> p k n", k=2)[:, :, 0:NB], ACT.Copy).then_inc(s_hT, 1)
                    if b >= 1:
                        b_rows(b - 1)
                b_rows(BLOCKS - 1)
                act.wait_ge(s_row, 1)
                act.dma_start(c_row_d, rowb[0:1, :, :].rearrange("a k n -> a (k n)")).then_inc(s_mv_rows, 16)
                act.wait_ge(s_mv_rows, 16)
                act.dma_start(c_rows[:, :], c_row_d.rearrange("a (k n) -> (a k) n", k=3)).then_inc(s_rows_in, 16)
                act.wait_ge(s_tb, CHUNKS)
                for c in range(CHUNKS):
                    act.dma_start(tile_block_d[c, 0:P].rearrange("(p a) -> p a", a=1),
                                  tb_i[:, 2 * c:2 * c + 1]).then_inc(s_tbd, 16)
                    act.dma_start(tile_block_d[c, P:TC].rearrange("(p a) -> p a", a=1),
                                  tb_i[0:TC - P, 2 * c + 1:2 * c + 2]).then_inc(s_tbd, 16)
                act.wait_ge(s_tbd, 32 * CHUNKS)
                act.dma_start(tile_block[:, :], tile_block_d.rearrange("(a c) t -> a (c t)", a=1)).then_inc(s_tbl, 16)
                act.wait_ge(s_tbl, 16)
                act.wait_ge(s_rows_in, 16)

            @block.gpsimd
            def _(pool):
                pool.memset(exph[:, :], -0.5).then_inc(s_pool, 1)
                pool.memset(identf[:, :], 0.0).then_inc(s_pool, 1)
                pool.wait_ge(s_pool, 2)
                pool.affine_select(out=identf[:, :], in_=identf[:, :], compare_op=ALU.not_equal, fill=1.0, base=0,
                                   pattern=[[-1, P]], channel_multiplier=1).then_inc(s_pool, 1)
                pool.iota(iota_f[:, :], pattern=[[1, P]], base=0, channel_multiplier=0,
                          allow_small_or_imprecise_dtypes=True).then_inc(s_pool, 1)
                pool.iota(iota_n[:, :], pattern=[[1, P]], base=0, channel_multiplier=0,
                          allow_small_or_imprecise_dtypes=True).then_inc(s_pool, 1)
                pool.iota(iota_q[:, :], pattern=[[1, TC]], base=0, channel_multiplier=0,
                          allow_small_or_imprecise_dtypes=True).then_inc(s_pool, 1)
                pool.iota(tid[:, :], pattern=[[P, 2]], base=0, channel_multiplier=1,
                          allow_small_or_imprecise_dtypes=True).then_inc(s_pool, 1)
                pool.memset(onesb[:, :], 1.0).then_inc(s_pool, 1)
                pool.wait_ge(s_pool, 8)
                pool.affine_select(out=tri[:, :], in_=onesb[:, :], compare_op=ALU.is_gt, fill=0.0, base=0,
                                   pattern=[[1, P]], channel_multiplier=-1).then_inc(s_pool, 1)
                pool.tensor_copy(identb[:, :], identf[:, :]).then_inc(s_pool, 1)
                pool.memset(ones3[:, :], 1.0).then_inc(s_pool, 1)
                pool.wait_ge(s_last, 16)
                pool.wait_ge(s_pool, 11)
                pool.tensor_copy(w_parts[WP:P, 0, :], w_last[WP:P, :]).then_inc(s_pool, 1)
                pool.wait_ge(s_pool, 12)
                pool.tensor_tensor(w_parts[WP:P, 1, :], w_last[WP:P, :], w_parts[WP:P, 0, :],
                                   ALU.subtract).then_inc(s_pool, 1)
                pool.wait_ge(s_pool, 13)
                pool.wait_ge(s_mv1, 1)
                pool.tensor_scalar(rstd[:, :], mv[:, :, 1], LN_EPS, None, ALU.add).then_inc(s_pool, 1)
                pool.wait_ge(s_pool, 14)
                pool.tensor_tensor(rstd[:, :], rstd[:, :], exph[0:NB, :], ALU.pow).then_inc(s_rstd1, 1)
                pool.memset(q_all[:, :], 0.0).then_inc(s_pool, 1)
                pool.memset(r_all[:, :], 0.0).then_inc(s_pool, 1)
                pool.memset(vals_all[:, :, :], 0.0).then_inc(s_pool, 1)
                for k, c in enumerate(POOL_CHUNKS):
                    pool.wait_ge(s_base, c + 1)
                    for b in range(BLOCKS):
                        ins = pool.tensor_scalar(cums[c % 2][:, b, :], cums[c % 2][:, b, :], base[:, c % 2, b:b + 1],
                                                 None, ALU.add)
                    ins.then_inc(s_add, 1)
                    pool.wait_ge(s_add, k + 1)
                    pool.tensor_tensor(cums[c % 2], cums[c % 2], eqs[c % 2][:, :, :], ALU.mult).then_inc(s_place, 1)

            @block.tensor
            def _(pe):
                pe.wait_ge(s_pool, 3)
                pe.wait_ge(s_pool, 9)
                pe.wait_ge(s_weights, 16 * 7)

                def sums(c):
                    pe.wait_ge(s_cnt, c + 1)
                    if c:
                        pe.wait_ge(s_base, c)
                    pe.matmul(psK[0:EP, 0:BLOCKS], tri[0:EP, 0:EP], cnt[:, :], start=True, stop=True)
                    pe.matmul(psK[:, 64:64 + BLOCKS], onesb[0:EP, :], cnt[:, :], start=True, stop=True).then_inc(s_cntm, 1)

                for b in range(BLOCKS + 1):
                    if b < BLOCKS:
                        pe.wait_ge(s_h, b + 1)
                        if b >= 2:
                            pe.wait_ge(s_hT, b - 1)
                        for k in range(2):
                            mm = pe.transpose(psX[:, b % 2, k * P:k * P + NB], h_sb[:, b, k * P:(k + 1) * P],
                                              identf[0:NB, 0:NB])
                        mm.then_inc(s_hx, 1)
                    if b >= 1:
                        a = b - 1
                        pe.wait_ge(s_hT, a + 1)
                        if a >= 2:
                            pe.wait_ge(s_abf, a - 1)
                            pe.wait_ge(s_bo, a - 1)
                        for n, to in enumerate((psA, psB)):
                            for k in range(2):
                                mm = pe.matmul(to[0:NB, a % 2, 0:D], hT[:, a % 2, k, 0:NB],
                                               wij[:, k, n * D:(n + 1) * D], start=(k == 0), stop=(k == 1))
                        mm.then_inc(s_ab, 1)
                        if a % 5 == 3:
                            sums(a // 5)
                for k in range(2):
                    mm = pe.matmul(psC[0:1, 0:D], bcol[:, k:k + 1], w2raw[:, k, :], start=(k == 0), stop=(k == 1))
                mm.then_inc(s_c, 1)

            @block.vector
            def _(dve):
                links = [0]

                def link(ins):
                    links[0] += 1
                    ins.then_inc(s_dve, 1)
                    dve.wait_ge(s_dve, links[0])

                V = nc.vector
                dve.wait_ge(s_x, 16)
                for b in range(BLOCKS):
                    ins = V.bn_stats(stats[:, b, :], h_sb[:, b, :])
                link(ins)
                for b in range(BLOCKS):
                    ins = V.bn_aggr(mv[:, b, :], stats[:, b, :])
                ins.then_inc(s_mv1, 1)

                dve.wait_ge(s_weights, 16 * 7)
                for k in range(2):
                    V.tensor_scalar(w2g[:, k, :], w2raw[:, k, :], gcol[:, k:k + 1], None, ALU.mult).then_inc(s_w2g, 1)
                dve.wait_ge(s_rstd1, 1)
                for b in range(BLOCKS):
                    V.tensor_scalar(h_sb[:, b, :], h_sb[:, b, :], mv[:, b, 0:1], rstd[:, b:b + 1],
                                    ALU.subtract, ALU.mult).then_inc(s_h, 1)

                def tables(b):
                    dve.wait_ge(s_ab, b + 1)
                    link(V.tensor_tensor(res[:, :], psA[0:NB, b % 2, 0:D], mb1_b[0:NB, :], ALU.add))
                    dve.wait_ge(s_wrows, b + 1)
                    link(V.tensor_copy(a_sb[0:NB, b, 0, :], res[:, :]))
                    ins = V.tensor_tensor(a_sb[0:NB, b, 1, :], res[:, :], a_sb[0:NB, b, 0, :], ALU.subtract)
                    ins.then_inc(s_abf, 1)
                    dve.wait_ge(s_abf, b + 1)

                assert BLOCKS == 5 * CHUNKS

                def chunked(ap):
                    return ap.rearrange("p (c t) -> p c t", c=CHUNKS)

                def put(n, source):
                    V.tensor_copy(vals[0:EP, n, :, 0:CC], chunked(source))

                dve.wait_ge(s_edges, 48)
                dve.wait_ge(s_pool, 17)
                link(V.tensor_copy(f1[:, :], src_i[:, :]))
                link(V.tensor_scalar(f2[:, :], f1[:, :], 1.0 / NB, -(NB // 2) / NB, ALU.mult, ALU.add))
                link(V.tensor_scalar(f2[:, :], f2[:, :], MAGIC, None, ALU.add))
                link(V.tensor_scalar(f2[:, :], f2[:, :], -MAGIC, None, ALU.add))
                link(V.tensor_copy(blk[:, :], f2[:, :]))
                link(V.scalar_tensor_tensor(out=f1[:, :], in0=f2[:, :], scalar=-float(NB), in1=f1[:, :],
                                            op0=ALU.mult, op1=ALU.add))
                link(V.tensor_copy(f2[:, :], dst_i[:, :]))
                link(V.tensor_scalar(f2[:, :], f2[:, :], float(P), 1.0, ALU.mult, ALU.add))
                link(V.tensor_tensor(vals[0:EP, 0, :, 0:CC], chunked(f2[:, :]), chunked(f1[:, :]), ALU.add))
                put(1, ew_f[:, :])

                def count(c):
                    eq, cum = eqs[c % 2], cums[c % 2]
                    cols = slice(c * CC, (c + 1) * CC)
                    for b in range(BLOCKS):
                        ins = V.tensor_scalar(eq[:, b, :], blk[:, cols], float(b), None, ALU.is_equal)
                    link(ins)
                    flat = eq[:, :, :].rearrange("p b t -> p (b t)")
                    link(V.tensor_tensor_scan(cum[:, :, :].rearrange("p b t -> p (b t)"), flat, flat, 0.0,
                                              ALU.add, ALU.bypass))
                    link(V.memset(sm[0:EP, 0, 0:1], 0.0))
                    link(V.tensor_copy(sm[0:EP, 0, 1:BLOCKS], cum[:, 0:BLOCKS - 1, CC - 1]))
                    link(V.tensor_tensor(sm[0:EP, 1, :], cum[:, :, CC - 1], sm[0:EP, 0, :], ALU.subtract))
                    V.tensor_copy(cnt[:, :], sm[0:EP, 1, :]).then_inc(s_cnt, 1)

                def starts(c):
                    dve.wait_ge(s_cntm, c + 1)
                    link(V.tensor_scalar(sm[:, 2, :], psK[:, 64:64 + BLOCKS], 1.0 / P, (P - 1.0) / P - 0.498,
                                         ALU.mult, ALU.add))
                    link(V.tensor_scalar(sm[:, 2, :], sm[:, 2, :], MAGIC, None, ALU.add))
                    link(V.tensor_scalar(sm[:, 2, :], sm[:, 2, :], -MAGIC, None, ALU.add))
                    link(V.tensor_tensor_scan(sm[:, 3, :], sm[:, 2, :], sm[:, 2, :], 0.0, ALU.add, ALU.bypass))
                    link(V.tensor_tensor(sm[:, 4, :], sm[:, 3, :], sm[:, 2, :], ALU.subtract))
                    link(V.scalar_tensor_tensor(out=sm[0:EP, 5, :], in0=sm[0:EP, 4, :], scalar=float(P),
                                                in1=psK[0:EP, 0:BLOCKS], op0=ALU.mult, op1=ALU.add))
                    ins = V.scalar_tensor_tensor(out=base[:, c % 2, :], in0=sm[0:EP, 5, :], scalar=-1.0,
                                                 in1=sm[0:EP, 0, :], op0=ALU.add, op1=ALU.subtract)
                    ins.then_inc(s_base, 1)
                    for n in range(2):
                        link(V.tensor_scalar(sm[:, 7, :], sm[:, 3, :], tid[:, n:n + 1], None, ALU.is_le))
                        link(V.tensor_reduce(tb_f[:, n:n + 1], sm[:, 7, :], AX_X, ALU.add))
                    V.tensor_scalar(tb_i[:, 2 * c:2 * c + 2], tb_f[:, :], BLOCKS - 1.0, None, ALU.min).then_inc(s_tb, 1)
                    dve.wait_ge(s_tb, c + 1)

                def places(c):
                    eq, cum = eqs[c % 2], cums[c % 2]
                    if c in POOL_CHUNKS:
                        dve.wait_ge(s_place, POOL_CHUNKS.index(c) + 1)
                    else:
                        dve.wait_ge(s_base, c + 1)
                        for b in range(BLOCKS):
                            ins = V.scalar_tensor_tensor(out=cum[:, b, :], in0=cum[:, b, :],
                                                         scalar=base[:, c % 2, b:b + 1], in1=eq[:, b, :],
                                                         op0=ALU.add, op1=ALU.mult)
                        link(ins)
                    link(V.tensor_reduce(pos[:, :], cums[c % 2].rearrange("p b t -> p t b"), AX_X, ALU.add))
                    q = q_col[0:EP, c, 0:CC]
                    link(V.tensor_scalar(q, pos[:, :], 1.0 / P, -0.498, ALU.mult, ALU.add))
                    link(V.tensor_scalar(q, q, MAGIC, None, ALU.add))
                    link(V.tensor_scalar(q, q, -MAGIC, None, ALU.add))
                    link(V.scalar_tensor_tensor(out=r_col[0:EP, c, 0:CC], in0=q, scalar=-float(P), in1=pos[:, :],
                                                op0=ALU.mult, op1=ALU.add))

                for c in range(CHUNKS):
                    tables(5 * c)
                    tables(5 * c + 1)
                    count(c)
                    tables(5 * c + 2)
                    tables(5 * c + 3)
                    starts(c)
                    tables(5 * c + 4)
                    if 0 < c < CHUNKS - 1:
                        places(c - 1)
                dve.wait_ge(s_c, 1)
                link(V.tensor_tensor(rowf[0:1, 0, :], psC[0:1, 0:D], rowf[0:1, 0, :], ALU.add))
                link(V.tensor_copy(rowb[0:1, 0, :], rowf[0:1, 0, :]))
                link(V.tensor_tensor(rowf[0:1, 1, :], rowf[0:1, 0, :], rowb[0:1, 0, :], ALU.subtract))
                link(V.tensor_copy(rowb[0:1, 1, :], rowf[0:1, 1, :]))
                link(V.tensor_tensor(rowf[0:1, 2, :], rowf[0:1, 1, :], rowb[0:1, 1, :], ALU.subtract))
                V.tensor_copy(rowb[0:1, 2, :], rowf[0:1, 2, :]).then_inc(s_row, 1)

                places(CHUNKS - 1)
                places(CHUNKS - 2)

        with ExitStack() as ctx:
            def sb(name, shape, dt):
                return alloc(ctx, name, shape, dt)

            def sem(name):
                return semaphore(ctx, name)

            loc = sb("loc", [P, TILES], F32)
            idx = sb("idx", [P, TILES], I32)
            idx_pair = sb("idx_pair", [P, PG, 2], I32)
            ewp = sb("ewp", [P, TILES, 3], BF16)
            or_ = sb("or_", [P, RB, P], F32)
            oq = sb("oq", [P, RB, NPART, TC], F32)
            zerob = sb("zerob", [P, P], BF16)
            r_six = sb("r_six", [P, GROUP], F32)
            rec = sb("rec", [P, 2, TC], I32)
            ew_r = sb("ew_r", [P, 2, TC], F32)
            ohb = sb("ohb", [P, PG, 2, P], BF16)
            ohT = sb("ohT", [P, PG, 2, P], F32R)
            ohf = sb("ohf", [P, PG, 2, NB], F32)
            g_rows = sb("g_rows", [P, PG, 2, D], F32)
            act1 = sb("act1", [P, PG, 2, D], F32)
            normed = sb("normed", [P, PG, 2, D], F32)
            nT = sb("nT", [P, PG, 2, 2, P], F32)
            msg = sb("msg", [P, PG, 2, D], F32)
            stat6 = sb("stat6", [P, PG, 2, 6], F32)
            meanvar = sb("meanvar", [P, PG, 2, 2], F32)
            vare = sb("vare", [P, PG, 2], F32)
            neg_mean = sb("neg_mean", [P, PG, 2], F32)
            rstd_e = sb("rstd_e", [P, PG, 2], F32)
            shift = sb("shift", [P, PG, 2], F32)
            psR = ctx.enter_context(nc.psum_tensor("psR", [P, 512], F32))
            psT = ctx.enter_context(nc.psum_tensor("psT", [P, 1024], BF16))
            psH = ctx.enter_context(nc.psum_tensor("psH", [P, 2, D], F32))
            psM = ctx.enter_context(nc.psum_tensor("psM", [P, 2, 2, P], F32))
            ps2 = ctx.enter_context(nc.psum_tensor("ps2", [P, 2, D], F32))
            psG = ctx.enter_context(nc.psum_tensor("psG", [P, PG, 2, D], F32))

            s_clear = sem("s_clear")
            s_rready = sem("s_rready")
            s_rplace = sem("s_rplace")
            s_six = sem("s_six")
            s_rused = sem("s_rused")
            s_rdone = sem("s_rdone")
            s_fin = sem("s_fin")
            s_sorted = sem("s_sorted")
            s_oh = sem("s_oh")
            s_turned = sem("s_turned")
            s_ohT = sem("s_ohT")
            s_gather = [[sem(f"s_gather{j}{n}") for n in range(2)] for j in range(PG)]
            s_idx = sem("s_idx")
            s_first = sem("s_first")
            s_hid = sem("s_hid")
            s_act1 = sem("s_act1")
            s_bn = sem("s_bn")
            s_mv = sem("s_mv")
            s_eps = sem("s_eps")
            s_pow = sem("s_pow")
            s_rstd = sem("s_rstd")
            s_norm = sem("s_norm")
            s_nx = sem("s_nx")
            s_nT = sem("s_nT")
            s_second = sem("s_second")
            s_msg = sem("s_msg")
            s_ohf = sem("s_ohf")
            s_sum = sem("s_sum")
            s_agg = sem("s_agg")

            block = ctx.enter_context(nc.Block())

            s_apart = {nc.gpsimd.engine: sem("s_apart_pool"), nc.vector.engine: sem("s_apart_dve")}

            def need(eng, sm_, value):
                if not isinstance(value, int) or value > 0:
                    eng.wait_ge(sm_, value)

            def need_apart(eng, *waits):
                for sm_, v in waits:
                    need(eng, sm_, v)
                eng.sem_inc(s_apart[eng.engine], 1)

            def run_slots(eng, prepare, slot, route, route_begin, route_end):
                route_begin(0)
                for j in range(GROUP):
                    route(j, j, True)
                with eng.Fori(1, RI) as i:
                    for j in range(GROUP):
                        route(i * GROUP + j, j, True)
                route_end(0)

                def group(g, routed=None):
                    prepare(g)
                    for jp in range(PG):
                        slot(g * PG + jp, g, jp, None if routed is None else routed)

                group(0)
                group(1)
                with eng.Fori(0, CHUNKS - 1) as c:
                    route_begin(c + 1)
                    with eng.Fori(2, 2 + RI) as i:
                        group(c * GI + i, (c + 1) * CP + (i - 2) * GROUP)
                    route_end(c + 1)
                    with eng.Fori(2 + RI, 2 + GI) as i:
                        group(c * GI + i)
                with eng.Fori(2, GI) as i:
                    group((CHUNKS - 1) * GI + i)
                prepare(GROUPS)
                for jp in range(PG):
                    slot(PAIRS + jp, GROUPS, jp, None)
                prepare(GROUPS + 1)
                for jp in range(DRAIN - PG):
                    slot(PAIRS + PG + jp, GROUPS + 1, jp, None)

            def has(s, lag):
                return not isinstance(s, int) or 0 <= s - lag < PAIRS

            @block.sync
            def _(sp):
                def bc(v):
                    return v.rearrange("(a n) -> a n", a=1)

                todo = [(wts[0][:, :, :], uW1.rearrange("(k p) n -> p k n", p=P)),
                        (wts[1][:, :, :], uW2.rearrange("(k p) n -> p k n", p=P)),
                        (wts[2][:, :], ub1.rearrange("(k p) -> p k", p=P)),
                        (wts[3][:, :], bc(ub2).broadcast_to([P, D])),
                        (wts[4][:, :], wr.rearrange("n a -> a n").broadcast_to([P, D])),
                        (wts[5][:, :], bc(br).broadcast_to([P, 1]))]
                for to, frm in todo:
                    sp.dma_start(to, frm, allow_slow_non_contiguous=True).then_inc(s_late, 16)
                sp.wait_ge(s_late, 16 * len(todo))

            @block.gpsimd
            def _(pool):
                pool.memset(zerob[:, :], 0.0).then_inc(s_clear, 1)
                pool.memset(agg[:, :, :], 0.0).then_inc(s_clear, 1)

                def route_end(c):
                    need_apart(pool, (s_sorted, c + 1))

                def slot(s, g, jp, routed):
                    if has(s, 0):
                        need(pool, s_act1, s - 2)
                        pool.tensor_copy(idx_pair[:, jp, :], idx[:, bass.ds(g * GROUP + 2 * jp, 2)]).then_inc(s_idx, 1)
                        need_apart(pool, (s_idx, s + 1))
                        for n in range(2):
                            pool.indirect_dma_start(
                                g_rows[:, jp, n, :], None, b_table[:, :],
                                bass.IndirectOffsetOnAxis(ap=idx_pair[:, jp, n:n + 1], axis=0)).then_inc(s_gather[jp][n], 16)
                    if has(s, 2):
                        k = (jp - 2) % PG
                        need_apart(pool, (s_mv, s - 1), (s_norm, s - 4))
                        pool.tensor_scalar(vare[:, k, :], meanvar[:, k, :, 1], LN_EPS, None, ALU.add).then_inc(s_eps, 1)
                        pool.tensor_scalar(neg_mean[:, k, :], meanvar[:, k, :, 0], -1.0, None, ALU.mult).then_inc(s_eps, 1)
                        pool.wait_ge(s_eps, 2 * s - 2)
                        pool.tensor_tensor(rstd_e[:, k, :], vare[:, k, :], exph[:, 0:2], ALU.pow).then_inc(s_pow, 1)
                        pool.wait_ge(s_pow, s - 1)
                        pool.tensor_tensor(shift[:, k, :], neg_mean[:, k, :], rstd_e[:, k, :], ALU.mult).then_inc(s_rstd, 1)

                def one_hot_r(j, column):
                    ins = pool.tensor_scalar(or_[0:EP, j % RB, :], iota_n[0:EP, :], column, None, ALU.is_equal)
                    ins.then_inc(s_rplace, 1)

                def route_begin(c):
                    if isinstance(c, int):
                        for j in range(AHEAD):
                            one_hot_r(j, r_all[0:EP, j:j + 1])

                def route(rc, j, alone=False):
                    if j == 0:
                        need(pool, s_rplace, rc + AHEAD)
                        pool.tensor_copy(r_six[0:EP, :], r_all[0:EP, bass.ds(rc + AHEAD, GROUP)]).then_inc(s_six, GROUP)
                        need_apart(pool, (s_six, rc + GROUP))
                    need_apart(pool, (s_rused, rc + AHEAD - RB + 1))
                    one_hot_r(j + AHEAD, r_six[0:EP, j:j + 1])

                run_slots(pool, lambda g: None, slot, route, route_begin, route_end)

            @block.scalar
            def _(act):
                def slot(s, g, jp, routed):
                    k2 = (jp - 2) % PG
                    if has(s, 2):
                        act.wait_ge(s_hid, s - 1)
                        need(act, s_norm, s - 4)
                        nc.scalar.activation(act1[:, k2, :, :], g_rows[:, k2, :, :], ACT.Silu).then_inc(s_act1, 1)
                    if has(s, 3):
                        act.wait_ge(s_rstd, s - 2)
                        need(act, s_nx, s - 5)
                        for n in range(2):
                            ins = nc.scalar.activation(normed[:, jp, n, :], act1[:, jp, n, :], ACT.Identity,
                                                       scale=rstd_e[:, jp, n:n + 1], bias=shift[:, jp, n:n + 1])
                        ins.then_inc(s_norm, 1)
                    if has(s, 1):
                        k = (jp - 1) % PG
                        act.wait_ge(s_turned, s)
                        need(act, s_first, s - 3)
                        nc.scalar.activation(ohT[:, k, :, :], psT[:, 0:2 * P].rearrange("p (n e) -> p n e", n=2),
                                             ACT.Copy).then_inc(s_ohT, 1)
                    if has(s, 2):
                        act.wait_ge(s_oh, s - 1)
                        need(act, s_sum, s - 4)
                        nc.scalar.activation(ohf[:, k2, :, :], ohb[:, k2, :, 0:NB], ACT.Copy).then_inc(s_ohf, 1)
                    if has(s, 4):
                        k = (jp - 1) % PG
                        act.wait_ge(s_second, s - 3)
                        need(act, s_sum, s - 5)
                        nc.scalar.activation(msg[:, k, :, :], ps2[:, :, :], ACT.Silu).then_inc(s_msg, 1)
                    if has(s, 3):
                        act.wait_ge(s_nx, s - 2)
                        need(act, s_second, s - 5)
                        nc.scalar.activation(nT[:, jp, :, :, :], psM[:, :, :, :], ACT.Copy).then_inc(s_nT, 1)

                run_slots(act, lambda g: None, slot, lambda rc, j, alone=False: None, lambda c: None, lambda c: None)

            @block.tensor
            def _(pe):
                regs = [pe.alloc_register(f"pe_block{n}") for n in range(GROUP)]

                iota_zero = iota_q[:, :].unsqueeze(1).broadcast_to([P, NPART, TC])

                def route_begin(c):
                    if isinstance(c, int):
                        pe.wait_ge(s_clear, 1)
                    else:
                        pe.wait_ge(s_sorted, c)
                    pe.matmul(psR[:, 0:NPART * TC], zerob[0:EP, :], iota_zero[0:EP, :, :], start=True, stop=False)

                def route_end(c):
                    if isinstance(c, int):
                        pe.wait_ge(s_rplace, CP + AHEAD)
                    pe.matmul(psR[:, 0:NPART * TC], zerob[0:EP, :], iota_zero[0:EP, :, :], start=False,
                              stop=True).then_inc(s_rdone, 1)

                def route(rc, j, alone=False):
                    if alone:
                        pe.wait_ge(s_rplace, rc + 1)
                    pe.wait_ge(s_rready, rc + 1)
                    pe.matmul(psR[:, 0:NPART * TC], or_[0:EP, j % RB, :], oq[0:EP, j % RB, :, :],
                              start=False, stop=False).then_inc(s_rused, 1)

                def prepare(g):
                    lo = g * GROUP - 4
                    n0 = 0
                    if isinstance(lo, int) and lo < 0:
                        n0, lo = -lo, 0
                    n1 = GROUP
                    if isinstance(g, int) and g * GROUP - 4 + n1 > TILES:
                        n1 = TILES - (g * GROUP - 4)
                    if n1 > n0:
                        pe.reg_load(regs[n0:n1], tile_block[0:1, bass.ds(lo, n1 - n0)])

                def slot(s, g, jp, routed):
                    if has(s, 2):
                        k = (jp - 2) % PG
                        pe.wait_ge(s_ohT, s - 1)
                        need(pe, s_hid, s - 2)
                        for n in range(2):
                            b = pe.snap(regs[2 * jp + n], min_val=0, max_val=BLOCKS - 1)
                            for part in range(2):
                                rows = a_sb[:, bass.ds(b, 1), part, :].rearrange("p a n -> p (a n)")
                                mm = pe.matmul(psH[:, n, :], ohT[:, k, n, :], rows,
                                               start=(part == 0), stop=(part == 1))
                        mm.then_inc(s_first, 1)
                    if has(s, 1):
                        k = (jp - 1) % PG
                        pe.wait_ge(s_oh, s)
                        need(pe, s_ohT, s - 1)
                        for n in range(2):
                            mm = pe.transpose(psT[:, n * P:(n + 1) * P], ohb[:, k, n, :], identb[:, :])
                        mm.then_inc(s_turned, 1)
                    if has(s, 5):
                        k = (jp - 2) % PG
                        pe.wait_ge(s_msg, s - 4)
                        pe.wait_ge(s_ohf, s - 4)
                        need(pe, s_agg, 2 * s - 10)
                        for n in range(2):
                            mm = pe.matmul(psG[0:NB, k, n, :], ohf[:, k, n, :], msg[:, k, n, :], start=True, stop=True)
                        mm.then_inc(s_sum, 1)
                    if has(s, 4):
                        k = (jp - 1) % PG
                        pe.wait_ge(s_nT, s - 3)
                        need(pe, s_msg, s - 4)
                        for n in range(2):
                            pe.matmul(ps2[:, n, :], ones3[:, :], c_rows[:, :], start=True, stop=False)
                            for q in range(2):
                                mm = pe.matmul(ps2[:, n, :], nT[:, k, n, q, :], w2g[:, q, :],
                                               start=False, stop=(q == 1))
                        mm.then_inc(s_second, 1)
                    if has(s, 3):
                        pe.wait_ge(s_norm, s - 2)
                        need(pe, s_nT, s - 3)
                        for n in range(2):
                            for q in range(2):
                                mm = pe.transpose(psM[:, n, q, :], normed[:, jp, n, q * P:(q + 1) * P], identf[:, :])
                        mm.then_inc(s_nx, 1)
                    if routed is not None:
                        route(routed + 2 * jp, 2 * jp)
                        route(routed + 2 * jp + 1, 2 * jp + 1)

                run_slots(pe, prepare, slot, route, route_begin, route_end)

            @block.vector
            def _(dve):
                V = nc.vector
                regs = [dve.alloc_register(f"dve_block{n}") for n in range(GROUP)]
                dve.wait_ge(s_clear, 2)
                dve.sem_inc(s_agg, 4)

                def one_hot_r(rc, j):
                    need(dve, s_rused, rc - RB + 1)
                    V.tensor_scalar(or_[0:EP, j % RB, :], iota_n[0:EP, :], r_all[0:EP, bass.ds(rc, 1)], None,
                                    ALU.is_equal)

                def one_hot_q(rc, j, alone=False):
                    if alone:
                        need(dve, s_rused, rc - RB + 1)
                    c_t = bass.ds(rc, 1)
                    for n in range(NPART):
                        ins = V.tensor_scalar(oq[0:EP, j % RB, n, :], iota_q[0:EP, :], q_all[0:EP, c_t],
                                              vals_all[0:EP, n, c_t], ALU.is_equal, ALU.mult)
                    ins.then_inc(s_rready, 1)

                def route(rc, j, alone=False):
                    if not alone:
                        one_hot_r(rc + AHEAD, j + AHEAD)
                    one_hot_q(rc + AHEAD, j + AHEAD, alone)

                def route_begin(c):
                    if isinstance(c, int):
                        for j in range(AHEAD):
                            one_hot_q(j, j, True)

                def route_end(c):
                    dve.wait_ge(s_rdone, c + 1)
                    cols = bass.ds(c * TC, TC)
                    if not isinstance(c, int):
                        dve.wait_ge(s_fin, c * 8)

                    def link(n, ins):
                        ins.then_inc(s_fin, 1)
                        dve.wait_ge(s_fin, c * 8 + n)

                    link(1, V.tensor_copy(rec[:, 0, :], psR[:, 0:TC]))
                    link(2, V.tensor_single_scalar(rec[:, 1, :], rec[:, 0, :], P - 1, ALU.bitwise_and))
                    link(3, V.tensor_scalar(loc[:, cols], rec[:, 1, :], -1.0, None, ALU.add))
                    link(4, V.tensor_copy(ewp[:, cols, 0], psR[:, TC:2 * TC]))
                    link(5, V.tensor_tensor(ew_r[:, 0, :], psR[:, TC:2 * TC], ewp[:, cols, 0], ALU.subtract))
                    link(6, V.tensor_copy(ewp[:, cols, 1], ew_r[:, 0, :]))
                    link(7, V.tensor_tensor(ew_r[:, 1, :], ew_r[:, 0, :], ewp[:, cols, 1], ALU.subtract))
                    link(8, V.tensor_copy(ewp[:, cols, 2], ew_r[:, 1, :]))
                    V.tensor_single_scalar(idx[:, cols], rec[:, 0, :], 7, ALU.logical_shift_right).then_inc(s_sorted, 1)
                    need_apart(dve, (s_sorted, c + 1))

                def prepare(g):
                    lo = g * GROUP - 10
                    n0 = 0
                    if isinstance(lo, int) and lo < 0:
                        n0, lo = min(-lo, GROUP), 0
                    if n0 < GROUP:
                        n1 = GROUP
                        if isinstance(g, int) and g * GROUP - 10 + n1 > TILES:
                            n1 = TILES - (g * GROUP - 10)
                        dve.reg_load(regs[n0:n1], tile_block[0:1, bass.ds(lo, n1 - n0)])

                def slot(s, g, jp, routed):
                    if has(s, 2):
                        k = (jp - 2) % PG
                        rounds = g + 1 if jp >= 2 else g
                        dve.wait_ge(s_first, s - 1)
                        for n in range(2):
                            dve.wait_ge(s_gather[k][n], 16 * rounds)
                        V.tensor_tensor(g_rows[:, k, :, :], psH[:, :, :], g_rows[:, k, :, :], ALU.add).then_inc(s_hid, 1)
                    if jp == 0:
                        prepare(g)
                    if routed is not None:
                        route(routed + 2 * jp, 2 * jp)
                    if has(s, 2):
                        dve.wait_ge(s_act1, s - 1)
                        need(dve, s_bn, 2 * s - 8)
                        for n in range(2):
                            V.bn_stats(stat6[:, k, n, :], act1[:, k, n, :]).then_inc(s_bn, 1)
                    if routed is not None:
                        one_hot_r(routed + 2 * jp + 1 + AHEAD, 2 * jp + 1 + AHEAD)
                    if has(s, 2):
                        need_apart(dve, (s_bn, 2 * s - 2), (s_rstd, s - 4))
                        for n in range(2):
                            ins = V.bn_aggr(meanvar[:, k, n, :], stat6[:, k, n, :])
                        ins.then_inc(s_mv, 1)

                    def add(n):
                        b = dve.snap(regs[2 * jp + n], min_val=0, max_val=BLOCKS - 1)
                        if n == 0:
                            dve.wait_ge(s_sum, s - 4)
                        need(dve, s_agg, 2 * s - 6 + n)
                        room = agg[:, bass.ds(b, 1), :].rearrange("p a n -> p (a n)")
                        V.tensor_tensor(room, psG[0:NB, (jp - 2) % PG, n, :], room, ALU.add).then_inc(s_agg, 1)

                    if has(s, 5):
                        add(0)
                    if routed is not None:
                        one_hot_q(routed + 2 * jp + 1 + AHEAD, 2 * jp + 1 + AHEAD)
                    if has(s, 0):
                        need_apart(dve, (s_turned, s - 2), (s_ohf, s - 2))
                        for n in range(2):
                            t = g * GROUP + 2 * jp + n
                            V.tensor_scalar(ohb[:, jp, n, 0:NB], iota_n[:, 0:NB], loc[:, bass.ds(t, 1)], None,
                                            ALU.is_equal)
                        V.tensor_copy(ohb[:, jp, :, NB:P], ewp[:, bass.ds(g * GROUP + 2 * jp, 2), :]).then_inc(s_oh, 1)
                    if has(s, 5):
                        add(1)

                run_slots(dve, lambda g: None, slot, route, route_begin, route_end)

        edge_mem.close()

        x_sb = alloc(whole, "x_sb", [NB, BLOCKS, D], F32)
        wts += (alloc(whole, "w1s", [P, 2, H], F32), alloc(whole, "b1c", [P, HC], F32),
                alloc(whole, "w2s", [P, HC, D], F32), alloc(whole, "b2r", [1, D], F32))
        node_phase(nc, io, x_v, out_v, x_sb, h_sb, agg, identf, exph, score_d, wts)


def node_phase(nc, io, x_v, out_v, x_sb, h_sb, agg, identf, exph, score_d, wts):
    w1, b1, w2, b2 = io["L0_ffn_w1"], io["L0_ffn_b1"], io["L0_ffn_w2"], io["L0_ffn_b2"]
    with ExitStack() as ctx:
        def sb(name, shape, dt):
            return ctx.enter_context(nc.sbuf_tensor(name, shape, dt))

        def sem(name):
            return ctx.enter_context(nc.semaphore(name))

        def bank(name):
            return ctx.enter_context(nc.psum_tensor(name, [P, 512], F32))

        uw1, uw2, ub1c, ub2b, wrb, brb, w1s, b1c, w2s, b2r = wts
        GB = 5
        NG = BLOCKS // GB
        GN = GB * NB
        CUT = (0, 320, GN)

        stage = sb("stage", [NB, GB, 4, P], F32)
        fT = sb("fT", [P, 4, GN], F32)
        u1 = sb("u1", [P, 2, GN], F32)
        x2s = sb("x2s", [NB, GB, D], F32)
        prod = sb("prod", [NB, 2, D], F32)
        sc5 = sb("sc5", [NB, GB], F32)
        stat = sb("stat", [NB, GB, 6], F32)
        mv = sb("mv_n", [NB, GB, 2], F32)
        rs = sb("rs", [NB, GB], F32)
        score = sb("score", [NB, BLOCKS], F32)
        stage2 = sb("stage2", [NB, GB, 2, P], F32)
        x2T = sb("x2T", [P, 2, GN], F32)
        gT = sb("gT", [P, HC, GN], F32)
        epst = sb("epst", [NB, GB], F32)
        ones1 = sb("ones1", [1, P], F32)
        row = sb("row", [NB, NODES], F32)
        tri = sb("tri_n", [NB, NB], F32)
        junk = sb("junk", [NB, NODES], BF16)
        counts = sb("counts", [NB, 3, BLOCKS], F32)
        coef = sb("coef", [NB, BLOCKS], F32)
        psX = [bank("psX0"), bank("psX1")]
        psU = [bank("psU0"), bank("psU1")]
        psY = [bank("psY0"), bank("psY1")]

        s_x = sem("s_x_n")
        s_ffn = sem("s_ffn")
        s_ub = sem("s_ub")
        s_con = sem("s_con")
        s_res = sem("s_res")
        s_stage = sem("s_stage")
        s_fx = sem("s_fx")
        s_fT = sem("s_fT")
        s_u = sem("s_u")
        s_u1 = sem("s_u1")
        s_y = sem("s_y")
        s_x1 = sem("s_x1")
        s_st = sem("s_st")
        s_mvn = sem("s_mvn")
        s_ep = sem("s_ep")
        s_rs = sem("s_rs")
        s_x2 = sem("s_x2")
        s_x2c = sem("s_x2c")
        s_pr = sem("s_pr")
        s_score = sem("s_score")
        s_scd = sem("s_scd")
        s_row = sem("s_row_n")
        s_stage2 = sem("s_stage2")
        s_gx = sem("s_gx")
        s_x2T = sem("s_x2T")
        s_f = sem("s_f")
        s_g = sem("s_g")
        s_z = sem("s_z")
        s_Y = sem("s_Y")
        s_sum = sem("s_sum_n")
        s_apart_pool = sem("s_apart_np")
        s_apart = sem("s_apart_n")
        s_rank = sem("s_rank")
        s_fin = sem("s_fin_n")
        s_out = sem("s_out")

        block = ctx.enter_context(nc.Block())

        def need(eng, sm_, value):
            if not isinstance(value, int) or value > 0:
                eng.wait_ge(sm_, value)

        def before(b, k):
            return b - (1, 3)[k] if k < 2 else b - 2

        def groups(eng, body, last=None):
            body(0)
            body(1)
            with eng.Fori(2, NG) as g:
                body(g)
            if last:
                last(NG)

        def at(ap, b, n=1):
            v = ap[:, bass.ds(b, n), :] if len(ap.shape) == 3 else ap[:, bass.ds(b, n)]
            return v.rearrange("p a n -> p (a n)") if len(ap.shape) == 3 else v

        @block.sync
        def _(sp):
            sp.dma_start(x_sb[:, :, :], x_v).then_inc(s_x, 16)
            sp.dma_start(w1s[:, :, :], w1.rearrange("(k p) n -> p k n", p=P)).then_inc(s_ffn, 16)
            sp.dma_start(b1c[:, :], b1.rearrange("(k p) -> p k", p=P), allow_slow_non_contiguous=True).then_inc(s_ffn, 16)
            sp.dma_start(w2s[:, :, :], w2.rearrange("(k p) n -> p k n", p=P)).then_inc(s_ffn, 16)
            sp.dma_start(b2r[:, :], b2.rearrange("(a n) -> a n", a=1)).then_inc(s_ffn, 16)
            sp.wait_ge(s_score, NG)
            sp.dma_start(score_d.rearrange("b p -> p b"), score[:, :], allow_slow_non_contiguous=True).then_inc(s_scd, 16)
            sp.wait_ge(s_scd, 16)
            sp.dma_start(row[:, :], score_d.rearrange("(a b) p -> a (b p)", a=1).broadcast_to([NB, NODES])).then_inc(s_row, 16)
            for g in range(NG):
                sp.wait_ge(s_fin, g + 1)
                sp.dma_start(out_v[:, g * GB:(g + 1) * GB, :], x_sb[:, g * GB:(g + 1) * GB, :]).then_inc(s_out, 16)
            sp.wait_ge(s_out, 16 * NG)

        @block.gpsimd
        def _(pool):
            pool.memset(ones1[:, :], 1.0).then_inc(s_con, 1)
            pool.memset(epst[:, :], LN_EPS).then_inc(s_con, 1)
            pool.memset(tri[:, :], 1.0).then_inc(s_con, 1)
            pool.wait_ge(s_con, 3)
            pool.affine_select(out=tri[:, :], in_=tri[:, :], compare_op=ALU.is_gt, fill=0.0, base=0,
                               pattern=[[-1, NB]], channel_multiplier=1).then_inc(s_con, 1)

            pool.wait_ge(s_x, 16)

            def residual(g):
                pool.tensor_tensor(at(x_sb, g * GB, GB).rearrange("p (a n) -> p a n", a=GB),
                                   at(x_sb, g * GB, GB).rearrange("p (a n) -> p a n", a=GB),
                                   ub2b[0:NB, :].unsqueeze(1).broadcast_to([NB, GB, D]), ALU.add).then_inc(s_ub, 1)
                pool.wait_ge(s_ub, g + 1)
                pool.sem_inc(s_apart_pool, 1)
                for k in range(GB):
                    b = g * GB + k
                    pool.tensor_tensor(at(x_sb, b), at(x_sb, b), at(h_sb, b), ALU.add).then_inc(s_res, 1)

            def norm(g):
                pool.wait_ge(s_mvn, g)
                need(pool, s_x2, g - 1)
                pool.tensor_tensor(rs[:, :], mv[:, :, 1], epst[:, :], ALU.add).then_inc(s_ep, 1)
                pool.wait_ge(s_ep, g)
                pool.tensor_tensor(rs[:, :], rs[:, :], exph[0:NB, 0:GB], ALU.pow).then_inc(s_rs, 1)
                pool.wait_ge(s_x2, g)
                pool.tensor_copy(at(h_sb, (g - 1) * GB, GB), x2s[:, :, :].rearrange("p k n -> p (k n)")).then_inc(s_x2c, 1)

            def body(g):
                residual(g)
                if not (isinstance(g, int) and g == 0):
                    norm(g)

            groups(pool, body, norm)

            def copy2(g):
                for k in range(GB):
                    b = g * GB + k
                    need(pool, s_gx, b - GB + 1)
                    pool.wait_ge(s_x2c, NG)
                    pool.tensor_copy(stage2[:, k, :, :].rearrange("p k n -> p (k n)"), at(h_sb, b)).then_inc(s_stage2, 1)

            def total(g):
                g = g - 1
                pool.tensor_tensor(at(x_sb, g * GB, GB), at(x_sb, g * GB, GB), at(h_sb, g * GB, GB), ALU.add).then_inc(s_sum, 1)

            groups(pool, lambda g: (copy2(g), None if isinstance(g, int) and g == 0 else total(g)), total)

        @block.scalar
        def _(act):
            def body(g):
                for k in range(GB):
                    b = g * GB + k
                    act.wait_ge(s_fx, b + 1)
                    if k == 0:
                        need(act, s_u, 4 * g)
                    nc.scalar.activation(fT[:, :, k * NB:(k + 1) * NB],
                                         psX[k % 2][:, :].rearrange("p (q n) -> p q n", q=4)[:, :, 0:NB],
                                         ACT.Copy).then_inc(s_fT, 1)
                for f in range(2):
                    for n in range(2):
                        o = 2 * f + n
                        act.wait_ge(s_u, g * 4 + o + 1)
                        if o == 0:
                            need(act, s_y, g * GB)
                        nc.scalar.activation(u1[:, f, CUT[n]:CUT[n + 1]], psU[o % 2][:, 0:CUT[n + 1] - CUT[n]],
                                             ACT.Silu, bias=ub1c[:, f:f + 1]).then_inc(s_u1, 1)

            groups(act, body)
            act.wait_ge(s_ffn, 64)

            def out_rows(g):
                for k in range(GB):
                    b = g * GB + k - GB
                    act.wait_ge(s_z, b + 1)
                    nc.scalar.activation(at(agg, b), psY[k % 2][0:NB, 0:D], ACT.Copy).then_inc(s_Y, 1)

            def body2(g):
                for k in range(GB):
                    b = g * GB + k
                    act.wait_ge(s_gx, b + 1)
                    if k == 0:
                        need(act, s_f, 2 * HC * g)
                    nc.scalar.activation(x2T[:, :, k * NB:(k + 1) * NB],
                                         psX[k % 2][:, 0:2 * P].rearrange("p (q n) -> p q n", q=2)[:, :, 0:NB],
                                         ACT.Copy).then_inc(s_x2T, 1)
                if not (isinstance(g, int) and g == 0):
                    out_rows(g)
                for hc in range(HC):
                    for n in range(2):
                        o = 2 * hc + n
                        act.wait_ge(s_f, g * 2 * HC + o + 1)
                        if o == 0:
                            need(act, s_z, g * GB)
                        nc.scalar.activation(gT[:, hc, CUT[n]:CUT[n + 1]], psU[o % 2][:, 0:CUT[n + 1] - CUT[n]],
                                             ACT.Gelu_apprx_tanh, bias=b1c[:, hc:hc + 1]).then_inc(s_g, 1)

            groups(act, body2, out_rows)

        @block.tensor
        def _(pe):
            pe.wait_ge(s_con, 4)

            def turn(g):
                for k in range(GB):
                    b = g * GB + k
                    pe.wait_ge(s_stage, b + 1)
                    need(pe, s_fT, before(b, k) + 1)
                    for q in range(4):
                        mm = pe.transpose(psX[k % 2][:, q * P:q * P + NB], stage[:, k, q, :], identf[0:NB, 0:NB])
                    mm.then_inc(s_fx, 1)

            def first(g):
                pe.wait_ge(s_fT, g * GB + GB)
                for f in range(2):
                    for n in range(2):
                        o = 2 * f + n
                        need(pe, s_u1, g * 4 + o - 1)
                        for q in range(4):
                            mm = pe.matmul(psU[o % 2][:, 0:CUT[n + 1] - CUT[n]], uw1[:, q, f * P:(f + 1) * P],
                                           fT[:, q, CUT[n]:CUT[n + 1]], start=(q == 0), stop=(q == 3))
                        mm.then_inc(s_u, 1)

            def second(g):
                pe.wait_ge(s_u1, g * 4)
                for k in range(GB):
                    b = g * GB + k - GB
                    need(pe, s_x1, before(b, k) + 1)
                    for q in range(2):
                        mm = pe.matmul(psY[k % 2][0:NB, 0:D], u1[:, q, k * NB:(k + 1) * NB], uw2[:, q, :],
                                       start=(q == 0), stop=(q == 1))
                    mm.then_inc(s_y, 1)

            def body(g):
                turn(g)
                if not (isinstance(g, int) and g == 0):
                    second(g)
                first(g)

            groups(pe, body, second)
            pe.wait_ge(s_x1, BLOCKS)
            pe.wait_ge(s_ffn, 64)

            def turn2(g):
                for k in range(GB):
                    b = g * GB + k
                    pe.wait_ge(s_stage2, b + 1)
                    need(pe, s_x2T, before(b, k) + 1)
                    for q in range(2):
                        mm = pe.transpose(psX[k % 2][:, q * P:q * P + NB], stage2[:, k, q, :], identf[0:NB, 0:NB])
                    mm.then_inc(s_gx, 1)

            def first2(g):
                pe.wait_ge(s_x2T, g * GB + GB)
                for hc in range(HC):
                    for n in range(2):
                        o = 2 * hc + n
                        need(pe, s_g, g * 2 * HC + o - 1)
                        for q in range(2):
                            mm = pe.matmul(psU[o % 2][:, 0:CUT[n + 1] - CUT[n]], w1s[:, q, hc * P:(hc + 1) * P],
                                           x2T[:, q, CUT[n]:CUT[n + 1]], start=(q == 0), stop=(q == 1))
                        mm.then_inc(s_f, 1)

            def second2(g):
                pe.wait_ge(s_g, g * 2 * HC)
                for k in range(GB):
                    b = g * GB + k - GB
                    need(pe, s_Y, before(b, k) + 1)
                    pe.matmul(psY[k % 2][0:NB, 0:D], ones1[:, 0:NB], b2r[:, :], start=True, stop=False)
                    for hc in range(HC):
                        mm = pe.matmul(psY[k % 2][0:NB, 0:D], gT[:, hc, k * NB:(k + 1) * NB], w2s[:, hc, :],
                                       start=False, stop=(hc == HC - 1))
                    mm.then_inc(s_z, 1)

            def body2(g):
                turn2(g)
                if not (isinstance(g, int) and g == 0):
                    second2(g)
                first2(g)

            groups(pe, body2, second2)

        @block.vector
        def _(dve):
            V = nc.vector

            def copy(g):
                for k in range(GB):
                    b = g * GB + k
                    need(dve, s_fx, b - GB + 1)
                    V.tensor_copy(stage[:, k, 0:2, :].rearrange("p k n -> p (k n)"), at(h_sb, b))
                    V.tensor_copy(stage[:, k, 2:4, :].rearrange("p k n -> p (k n)"), at(agg, b)).then_inc(s_stage, 1)

            def finish(g):
                for k in range(GB):
                    b = g * GB + k - GB
                    dve.wait_ge(s_res, b + 1)
                    dve.wait_ge(s_y, b + 1)
                    V.tensor_tensor(at(x_sb, b), psY[k % 2][0:NB, 0:D], at(x_sb, b), ALU.add).then_inc(s_x1, 1)
                need(dve, s_rs, g - 1)
                dve.wait_ge(s_x1, g * GB)
                dve.sem_inc(s_apart, 1)
                for k in range(GB):
                    b = g * GB + k - GB
                    ins = V.bn_stats(stat[:, k, :], at(x_sb, b))
                ins.then_inc(s_st, 1)
                dve.wait_ge(s_st, g)
                dve.sem_inc(s_apart, 1)
                for k in range(GB):
                    ins = V.bn_aggr(mv[:, k, :], stat[:, k, :])
                ins.then_inc(s_mvn, 1)
                dve.wait_ge(s_rs, g)
                need(dve, s_x2c, g - 1)
                need(dve, s_score, g - 1)
                for k in range(GB):
                    b = g * GB + k - GB
                    ins = V.tensor_scalar(x2s[:, k, :], at(x_sb, b), mv[:, k, 0:1], rs[:, k:k + 1],
                                          ALU.subtract, ALU.mult)
                ins.then_inc(s_x2, 1)
                dve.wait_ge(s_x2, g)
                for k in range(GB):
                    need(dve, s_pr, (g - 1) * GB + k - 1)
                    V.tensor_tensor_reduce(prod[:, k % 2, :], x2s[:, k, :], wrb[0:NB, :], 1.0, 0.0, ALU.mult, ALU.add,
                                           sc5[:, k:k + 1]).then_inc(s_pr, 1)
                dve.wait_ge(s_pr, g * GB)
                V.tensor_scalar(at(score, (g - 1) * GB, GB), sc5[:, :], brb[0:NB, :], None, ALU.add).then_inc(s_score, 1)

            def body(g):
                copy(g)
                if not (isinstance(g, int) and g == 0):
                    finish(g)

            groups(dve, body, finish)

            links = [0]

            def link(ins):
                links[0] += 1
                ins.then_inc(s_rank, 1)
                dve.wait_ge(s_rank, links[0])

            dve.wait_ge(s_row, 16)
            dve.wait_ge(s_con, 4)
            dve.wait_ge(s_score, NG)
            link(V.memset(counts[:, :, :], 0.0))
            for b in range(BLOCKS):
                lo, hi = b * NB, (b + 1) * NB
                own = score[:, b:b + 1]
                if b:
                    link(V.tensor_scalar(junk[:, 0:lo], row[:, 0:lo], own, None, ALU.is_ge, ALU.add,
                                         accum_out=counts[:, 0, b:b + 1]))
                link(V.tensor_scalar(junk[:, lo:NODES], row[:, lo:NODES], own, None, ALU.is_gt, ALU.add,
                                     accum_out=counts[:, 1, b:b + 1]))
                link(V.scalar_tensor_tensor(out=junk[:, lo:hi], in0=row[:, lo:hi], scalar=own, in1=tri[:, :],
                                            op0=ALU.is_equal, op1=ALU.mult))
                link(V.tensor_reduce(counts[:, 2, b:b + 1], junk[:, lo:hi], AX_X, ALU.add))
            link(V.tensor_tensor(counts[:, 0, :], counts[:, 0, :], counts[:, 1, :], ALU.add))
            link(V.tensor_tensor(counts[:, 0, :], counts[:, 0, :], counts[:, 2, :], ALU.add))
            link(V.scalar_tensor_tensor(out=coef[:, :], in0=counts[:, 0, :], scalar=float(TOPK), in1=score[:, :],
                                        op0=ALU.is_lt, op1=ALU.mult))
            for g in range(NG):
                dve.wait_ge(s_sum, g + 1)
                for k in range(GB):
                    b = g * GB + k
                    dve.wait_ge(s_Y, b + 1)
                    ins = V.scalar_tensor_tensor(out=x_sb[:, b, :], in0=agg[:, b, :], scalar=coef[:, b:b + 1],
                                                 in1=x_sb[:, b, :], op0=ALU.mult, op1=ALU.add)
                ins.then_inc(s_fin, 1)


_INS = ["x", "src", "dst", "edge_weight1", "L0_gnn_mW1", "L0_gnn_mb1", "L0_gnn_ln_g", "L0_gnn_ln_b", "L0_gnn_mW2",
        "L0_gnn_mb2", "L0_gnn_uW1", "L0_gnn_ub1", "L0_gnn_uW2", "L0_gnn_ub2", "L0_ffn_wr", "L0_ffn_br", "L0_ffn_w1",
        "L0_ffn_b1", "L0_ffn_w2", "L0_ffn_b2"]


def kernel(**inputs):
    import numpy as np
    import concourse.bacc as bacc
    from concourse.bass_utils import run_bass_kernel_spmd as run

    nc = bacc.Bacc("TRN2", target_bir_lowering=False, num_devices=1)
    arrays, io = {}, {}
    for name in _INS:
        a = np.ascontiguousarray(inputs[name])
        arrays[f"in_{name}"] = a
        io[name] = nc.dram_tensor(f"in_{name}", a.shape, mybir.dt.from_np(a.dtype), kind="ExternalInput").ap()
    io["out"] = nc.dram_tensor("out_0", (NODES, D), F32, kind="ExternalOutput").ap()
    build(nc, io)
    r = run(nc, [arrays], core_ids=[0])
    return r.results[0]["out_0"]
```
